# Optimizing a Trainium2 kernel written in Bass

```python
import numpy as np
import jax
import jax.numpy as jnp

def _softmax(x, axis=-1):
    return jax.nn.softmax(x, axis=axis)

def _gelu(x):
    return jax.nn.gelu(x, approximate=True)

def _silu(x):
    return jax.nn.silu(x)

def _sigmoid(x):
    return jax.nn.sigmoid(x)

def _layernorm(x, axis=-1, eps=1e-05):
    m = jnp.mean(x, axis=axis, keepdims=True)
    v = jnp.var(x, axis=axis, keepdims=True)
    return (x - m) / jnp.sqrt(v + eps)

def _scatter_add(tgt, idx, src, axis=0):
    return tgt.at[idx].add(src)

def _segment_sum(src, seg, n):
    return jax.ops.segment_sum(src, seg, n)
kernel_name = 'mk_hybrid_d1_jaxref_r8_64ae17'

def setup_inputs(seed: int=0):
    np.random.seed(seed)
    _w = jnp.asarray

    def _L0_attn_a_setup():
        import jax, jax.numpy as jnp
        import numpy as np
        import math
        B, T, C = (4, 256, 128)
        N_HEAD = 16
        HEAD_DIM = C // N_HEAD
        key = jax.random.key(seed)
        k1, k2, k3, k4, k5 = jax.random.split(key, 5)
        s = 1.0 / math.sqrt(C)
        return {'x': jax.random.normal(k1, (B, T, C), dtype=jnp.float32), 'W_attn': jax.random.normal(k2, (3 * C, C), dtype=jnp.float32) * s, 'b_attn': jax.random.normal(k3, (3 * C,), dtype=jnp.float32) * 0.02, 'W_proj': jax.random.normal(k4, (C, C), dtype=jnp.float32) * s, 'b_proj': jax.random.normal(k5, (C,), dtype=jnp.float32) * 0.02}
    _L0_attn_a_in = _L0_attn_a_setup()

    def _L0_attn_b_setup():
        import jax, jax.numpy as jnp
        import numpy as np
        import math
        N_HEAD = 16
        V_HEAD = 32
        NOPE = 32
        ROPE_D = 64
        KEEP = 32
        EPS = 1e-06

        def _freqs(T, dim=ROPE_D, theta=10000.0):
            f = 1.0 / theta ** (jnp.arange(0, dim, 2, dtype=jnp.float32) / dim)
            t = jnp.arange(T, dtype=jnp.float32)
            a = jnp.outer(t, f)
            return (jnp.cos(a), jnp.sin(a))

        def _rope(x, cos, sin):
            S = x.shape[-2]
            c = cos[:S][None, None]
            s = sin[:S][None, None]
            x1, x2 = jnp.split(x, 2, axis=-1)
            return jnp.concatenate([x1 * c - x2 * s, x1 * s + x2 * c], axis=-1)

        def _rms(x, g, eps=EPS):
            return x * jax.lax.rsqrt(jnp.mean(x * x, axis=-1, keepdims=True) + eps) * g

        def _attn(q, k, v, causal):
            scale = 1.0 / math.sqrt(q.shape[-1])
            s = jnp.einsum('bhqd,bhkd->bhqk', q, k) * scale
            if causal:
                Tq, Tk = (s.shape[-2], s.shape[-1])
                mask = jnp.tril(jnp.ones((Tq, Tk), dtype=bool))
                s = jnp.where(mask, s, jnp.finfo(s.dtype).min)
            return jnp.einsum('bhqk,bhkd->bhqd', jax.nn.softmax(s, axis=-1), v)

        def _forward(x, w_cq, g_qnorm, w_dq_nope, w_dq_rope, w_ckv, g_kvnorm, w_dk_nope, w_dv, w_krope, w_imp, w_selk, w_selv, w_wink, w_winv, w_gate, w_proj):
            B, T, C = x.shape
            cos, sin = _freqs(T)
            nq = _rms(x @ w_cq, g_qnorm)
            q_nope = (nq @ w_dq_nope).reshape(B, T, N_HEAD, NOPE).transpose(0, 2, 1, 3)
            q_rope = (nq @ w_dq_rope).reshape(B, T, N_HEAD, ROPE_D).transpose(0, 2, 1, 3)
            q_rope = _rope(q_rope, cos, sin)
            q = jnp.concatenate([q_nope, q_rope], axis=-1)
            gate = jax.nn.softmax((x @ w_gate).mean(axis=1), axis=-1)
            ckv = _rms(x @ w_ckv, g_kvnorm)
            k_nope = (ckv @ w_dk_nope).reshape(B, T, N_HEAD, NOPE).transpose(0, 2, 1, 3)
            v1 = (ckv @ w_dv).reshape(B, T, N_HEAD, V_HEAD).transpose(0, 2, 1, 3)
            k_rope = (x @ w_krope).reshape(B, T, 1, ROPE_D).transpose(0, 2, 1, 3) / N_HEAD
            k_rope = _rope(k_rope, cos, sin)
            k1 = jnp.concatenate([k_nope, jnp.broadcast_to(k_rope, (B, N_HEAD, T, ROPE_D))], axis=-1)
            scores = (x @ w_imp)[..., 0]
            _, idx = jax.lax.top_k(scores, KEEP)
            idx = jnp.sort(idx, axis=1)
            sel = jnp.take_along_axis(x, idx[:, :, None], axis=1)
            ks = (sel @ w_selk).reshape(B, KEEP, N_HEAD, NOPE + ROPE_D).transpose(0, 2, 1, 3)
            vs = (sel @ w_selv).reshape(B, KEEP, N_HEAD, V_HEAD).transpose(0, 2, 1, 3)
            ks = jnp.concatenate([ks[..., :NOPE], _rope(ks[..., NOPE:], cos, sin)], axis=-1)
            kw = (x @ w_wink).reshape(B, T, N_HEAD, NOPE + ROPE_D).transpose(0, 2, 1, 3)
            vw = (x @ w_winv).reshape(B, T, N_HEAD, V_HEAD).transpose(0, 2, 1, 3)
            kw = jnp.concatenate([kw[..., :NOPE], _rope(kw[..., NOPE:], cos, sin)], axis=-1)
            a1 = _attn(q, k1, v1, causal=True)
            a2 = _attn(q, ks, vs, causal=False)
            a3 = _attn(q, kw, vw, causal=True)
            g = gate[:, :, None, None, None]
            out = g[:, 0] * a1 + g[:, 1] * a2 + g[:, 2] * a3
            out = out.transpose(0, 2, 1, 3).reshape(B, T, N_HEAD * V_HEAD)
            return out @ w_proj
        key = jax.random.key(seed)
        ks = jax.random.split(key, 20)
        B, T, C = (2, 128, 128)
        q_lora, kv_lora = (96, 32)
        std = 0.02

        def w(k, shape):
            return jax.random.normal(k, shape, dtype=jnp.float32) * std
        return {'x': jax.random.normal(ks[0], (B, T, C), dtype=jnp.float32), 'w_cq': w(ks[1], (C, q_lora)), 'g_qnorm': jnp.ones((q_lora,), jnp.float32), 'w_dq_nope': w(ks[2], (q_lora, N_HEAD * NOPE)), 'w_dq_rope': w(ks[3], (q_lora, N_HEAD * ROPE_D)), 'w_ckv': w(ks[4], (C, kv_lora)), 'g_kvnorm': jnp.ones((kv_lora,), jnp.float32), 'w_dk_nope': w(ks[5], (kv_lora, N_HEAD * NOPE)), 'w_dv': w(ks[6], (kv_lora, N_HEAD * V_HEAD)), 'w_krope': w(ks[7], (C, ROPE_D)), 'w_imp': w(ks[8], (C, 1)), 'w_selk': w(ks[9], (C, N_HEAD * (NOPE + ROPE_D))), 'w_selv': w(ks[10], (C, N_HEAD * V_HEAD)), 'w_wink': w(ks[11], (C, N_HEAD * (NOPE + ROPE_D))), 'w_winv': w(ks[12], (C, N_HEAD * V_HEAD)), 'w_gate': w(ks[13], (C, 3)), 'w_proj': w(ks[14], (N_HEAD * V_HEAD, C))}
    _L0_attn_b_in = _L0_attn_b_setup()

    def _L0_ffn_setup():
        import jax, jax.numpy as jnp
        import numpy as np
        DIM = 128
        HIDDEN = 384
        SCALE = 1.0 / 127.0

        def _dequant(w_int, dtype):
            return w_int.astype(dtype) * jnp.asarray(SCALE, dtype)
        key = jax.random.key(seed)
        k_x, k_g, k_u, k_d = jax.random.split(key, 4)
        x = jax.random.normal(k_x, (4, 256, DIM), dtype=jnp.float32)
        w_gate = jax.random.randint(k_g, (HIDDEN, DIM), -127, 128, dtype=jnp.int32)
        w_up = jax.random.randint(k_u, (HIDDEN, DIM), -127, 128, dtype=jnp.int32)
        w_down = jax.random.randint(k_d, (DIM, HIDDEN), -127, 128, dtype=jnp.int32)
        return {'x': x, 'w_gate': w_gate, 'w_up': w_up, 'w_down': w_down}
    _L0_ffn_in = _L0_ffn_setup()
    _d = {'L0_attn_a_x': _L0_attn_a_in['x'], 'L0_attn_a_W_attn': _L0_attn_a_in['W_attn'], 'L0_attn_a_b_attn': _L0_attn_a_in['b_attn'], 'L0_attn_a_W_proj': _L0_attn_a_in['W_proj'], 'L0_attn_a_b_proj': _L0_attn_a_in['b_proj'], 'L0_attn_b_w_cq': _L0_attn_b_in['w_cq'], 'L0_attn_b_g_qnorm': _L0_attn_b_in['g_qnorm'], 'L0_attn_b_w_dq_nope': _L0_attn_b_in['w_dq_nope'], 'L0_attn_b_w_dq_rope': _L0_attn_b_in['w_dq_rope'], 'L0_attn_b_w_ckv': _L0_attn_b_in['w_ckv'], 'L0_attn_b_g_kvnorm': _L0_attn_b_in['g_kvnorm'], 'L0_attn_b_w_dk_nope': _L0_attn_b_in['w_dk_nope'], 'L0_attn_b_w_dv': _L0_attn_b_in['w_dv'], 'L0_attn_b_w_krope': _L0_attn_b_in['w_krope'], 'L0_attn_b_w_imp': _L0_attn_b_in['w_imp'], 'L0_attn_b_w_selk': _L0_attn_b_in['w_selk'], 'L0_attn_b_w_selv': _L0_attn_b_in['w_selv'], 'L0_attn_b_w_wink': _L0_attn_b_in['w_wink'], 'L0_attn_b_w_winv': _L0_attn_b_in['w_winv'], 'L0_attn_b_w_gate': _L0_attn_b_in['w_gate'], 'L0_attn_b_w_proj': _L0_attn_b_in['w_proj'], 'L0_ffn_w_gate': _L0_ffn_in['w_gate'], 'L0_ffn_w_up': _L0_ffn_in['w_up'], 'L0_ffn_w_down': _L0_ffn_in['w_down']}
    _x0 = _d['L0_attn_a_x']
    _d['L0_attn_a_x'] = jax.random.normal(jax.random.fold_in(jax.random.key(seed), 1), (32, 256, 128), dtype=_x0.dtype)
    del _x0
    return _d

def reference(L0_attn_a_x, L0_attn_a_W_attn, L0_attn_a_b_attn, L0_attn_a_W_proj, L0_attn_a_b_proj, L0_attn_b_w_cq, L0_attn_b_g_qnorm, L0_attn_b_w_dq_nope, L0_attn_b_w_dq_rope, L0_attn_b_w_ckv, L0_attn_b_g_kvnorm, L0_attn_b_w_dk_nope, L0_attn_b_w_dv, L0_attn_b_w_krope, L0_attn_b_w_imp, L0_attn_b_w_selk, L0_attn_b_w_selv, L0_attn_b_w_wink, L0_attn_b_w_winv, L0_attn_b_w_gate, L0_attn_b_w_proj, L0_ffn_w_gate, L0_ffn_w_up, L0_ffn_w_down):

    def _L0_attn_a_ref(x, W_attn, b_attn, W_proj, b_proj):
        import jax, jax.numpy as jnp
        import numpy as np
        import math
        B, T, C = (4, 256, 128)
        N_HEAD = 16
        HEAD_DIM = C // N_HEAD
        Bx, Tx, Cx = x.shape
        qkv = jnp.einsum('btc,dc->btd', x, W_attn) + b_attn
        q, k, v = jnp.split(qkv, 3, axis=-1)

        def to_heads(t):
            return t.reshape(Bx, Tx, N_HEAD, HEAD_DIM).transpose(0, 2, 1, 3)
        q, k, v = (to_heads(q), to_heads(k), to_heads(v))
        scale = 1.0 / math.sqrt(HEAD_DIM)
        att = jnp.einsum('bhqd,bhkd->bhqk', q, k) * scale
        causal = jnp.tril(jnp.ones((Tx, Tx), dtype=bool))
        att = jnp.where(causal, att, -jnp.inf)
        att = jax.nn.softmax(att, axis=-1)
        y = jnp.einsum('bhqk,bhkd->bhqd', att, v)
        y = y.transpose(0, 2, 1, 3).reshape(Bx, Tx, Cx)
        y = jnp.einsum('btc,dc->btd', y, W_proj) + b_proj
        return y

    def _L0_attn_b_ref(x, w_cq, g_qnorm, w_dq_nope, w_dq_rope, w_ckv, g_kvnorm, w_dk_nope, w_dv, w_krope, w_imp, w_selk, w_selv, w_wink, w_winv, w_gate, w_proj):
        import jax, jax.numpy as jnp
        import numpy as np
        import math
        N_HEAD = 16
        V_HEAD = 32
        NOPE = 32
        ROPE_D = 64
        KEEP = 32
        EPS = 1e-06

        def _freqs(T, dim=ROPE_D, theta=10000.0):
            f = 1.0 / theta ** (jnp.arange(0, dim, 2, dtype=jnp.float32) / dim)
            t = jnp.arange(T, dtype=jnp.float32)
            a = jnp.outer(t, f)
            return (jnp.cos(a), jnp.sin(a))

        def _rope(x, cos, sin):
            S = x.shape[-2]
            c = cos[:S][None, None]
            s = sin[:S][None, None]
            x1, x2 = jnp.split(x, 2, axis=-1)
            return jnp.concatenate([x1 * c - x2 * s, x1 * s + x2 * c], axis=-1)

        def _rms(x, g, eps=EPS):
            return x * jax.lax.rsqrt(jnp.mean(x * x, axis=-1, keepdims=True) + eps) * g

        def _attn(q, k, v, causal):
            scale = 1.0 / math.sqrt(q.shape[-1])
            s = jnp.einsum('bhqd,bhkd->bhqk', q, k) * scale
            if causal:
                Tq, Tk = (s.shape[-2], s.shape[-1])
                mask = jnp.tril(jnp.ones((Tq, Tk), dtype=bool))
                s = jnp.where(mask, s, jnp.finfo(s.dtype).min)
            return jnp.einsum('bhqk,bhkd->bhqd', jax.nn.softmax(s, axis=-1), v)

        def _forward(x, w_cq, g_qnorm, w_dq_nope, w_dq_rope, w_ckv, g_kvnorm, w_dk_nope, w_dv, w_krope, w_imp, w_selk, w_selv, w_wink, w_winv, w_gate, w_proj):
            B, T, C = x.shape
            cos, sin = _freqs(T)
            nq = _rms(x @ w_cq, g_qnorm)
            q_nope = (nq @ w_dq_nope).reshape(B, T, N_HEAD, NOPE).transpose(0, 2, 1, 3)
            q_rope = (nq @ w_dq_rope).reshape(B, T, N_HEAD, ROPE_D).transpose(0, 2, 1, 3)
            q_rope = _rope(q_rope, cos, sin)
            q = jnp.concatenate([q_nope, q_rope], axis=-1)
            gate = jax.nn.softmax((x @ w_gate).mean(axis=1), axis=-1)
            ckv = _rms(x @ w_ckv, g_kvnorm)
            k_nope = (ckv @ w_dk_nope).reshape(B, T, N_HEAD, NOPE).transpose(0, 2, 1, 3)
            v1 = (ckv @ w_dv).reshape(B, T, N_HEAD, V_HEAD).transpose(0, 2, 1, 3)
            k_rope = (x @ w_krope).reshape(B, T, 1, ROPE_D).transpose(0, 2, 1, 3) / N_HEAD
            k_rope = _rope(k_rope, cos, sin)
            k1 = jnp.concatenate([k_nope, jnp.broadcast_to(k_rope, (B, N_HEAD, T, ROPE_D))], axis=-1)
            scores = (x @ w_imp)[..., 0]
            _, idx = jax.lax.top_k(scores, KEEP)
            idx = jnp.sort(idx, axis=1)
            sel = jnp.take_along_axis(x, idx[:, :, None], axis=1)
            ks = (sel @ w_selk).reshape(B, KEEP, N_HEAD, NOPE + ROPE_D).transpose(0, 2, 1, 3)
            vs = (sel @ w_selv).reshape(B, KEEP, N_HEAD, V_HEAD).transpose(0, 2, 1, 3)
            ks = jnp.concatenate([ks[..., :NOPE], _rope(ks[..., NOPE:], cos, sin)], axis=-1)
            kw = (x @ w_wink).reshape(B, T, N_HEAD, NOPE + ROPE_D).transpose(0, 2, 1, 3)
            vw = (x @ w_winv).reshape(B, T, N_HEAD, V_HEAD).transpose(0, 2, 1, 3)
            kw = jnp.concatenate([kw[..., :NOPE], _rope(kw[..., NOPE:], cos, sin)], axis=-1)
            a1 = _attn(q, k1, v1, causal=True)
            a2 = _attn(q, ks, vs, causal=False)
            a3 = _attn(q, kw, vw, causal=True)
            g = gate[:, :, None, None, None]
            out = g[:, 0] * a1 + g[:, 1] * a2 + g[:, 2] * a3
            out = out.transpose(0, 2, 1, 3).reshape(B, T, N_HEAD * V_HEAD)
            return out @ w_proj
        return _forward(x, w_cq, g_qnorm, w_dq_nope, w_dq_rope, w_ckv, g_kvnorm, w_dk_nope, w_dv, w_krope, w_imp, w_selk, w_selv, w_wink, w_winv, w_gate, w_proj)

    def _L0_ffn_ref(x, w_gate, w_up, w_down):
        import jax, jax.numpy as jnp
        import numpy as np
        DIM = 128
        HIDDEN = 384
        SCALE = 1.0 / 127.0

        def _dequant(w_int, dtype):
            return w_int.astype(dtype) * jnp.asarray(SCALE, dtype)
        wg = _dequant(w_gate, x.dtype)
        wu = _dequant(w_up, x.dtype)
        wd = _dequant(w_down, x.dtype)
        gate = jnp.einsum('bsd,hd->bsh', x, wg)
        up = jnp.einsum('bsd,hd->bsh', x, wu)
        h = jax.nn.silu(gate) * up
        return jnp.einsum('bsh,dh->bsd', h, wd)
    x = L0_attn_a_x
    x = x + _L0_attn_a_ref(_layernorm(x, axis=-1), L0_attn_a_W_attn, L0_attn_a_b_attn, L0_attn_a_W_proj, L0_attn_a_b_proj)
    x = x + _L0_ffn_ref(_layernorm(x, axis=-1), L0_ffn_w_gate, L0_ffn_w_up, L0_ffn_w_down)
    x = x + _L0_attn_b_ref(_layernorm(x, axis=-1), L0_attn_b_w_cq, L0_attn_b_g_qnorm, L0_attn_b_w_dq_nope, L0_attn_b_w_dq_rope, L0_attn_b_w_ckv, L0_attn_b_g_kvnorm, L0_attn_b_w_dk_nope, L0_attn_b_w_dv, L0_attn_b_w_krope, L0_attn_b_w_imp, L0_attn_b_w_selk, L0_attn_b_w_selv, L0_attn_b_w_wink, L0_attn_b_w_winv, L0_attn_b_w_gate, L0_attn_b_w_proj)
    x = x + _L0_ffn_ref(_layernorm(x, axis=-1), L0_ffn_w_gate, L0_ffn_w_up, L0_ffn_w_down)
    return x

_drawn_inputs = setup_inputs


def setup_inputs(seed=0):
    import zlib

    import numpy as np

    out = dict(_drawn_inputs(seed))
    spreads = {'L0_attn_b_g_qnorm': (1.0, 0.6), 'L0_attn_b_g_kvnorm': (1.0, 0.6)}
    factors = {'L0_attn_b_w_cq': 55.456,
     'L0_attn_b_w_dq_nope': 64.0,
     'L0_attn_b_w_dq_rope': 62.247,
     'L0_attn_b_w_ckv': 64.0,
     'L0_attn_b_w_dk_nope': 64.0,
     'L0_attn_b_w_dv': 64.0,
     'L0_attn_b_w_krope': 64.0,
     'L0_attn_b_w_imp': 64.0,
     'L0_attn_b_w_selk': 64.0,
     'L0_attn_b_w_selv': 64.0,
     'L0_attn_b_w_wink': 64.0,
     'L0_attn_b_w_winv': 64.0,
     'L0_attn_b_w_gate': 64.0,
     'L0_attn_b_w_proj': 52.071}
    for name, (base, spread) in spreads.items():
        noise = np.random.default_rng([zlib.crc32(name.encode()), seed]).standard_normal(out[name].shape)
        drawn = base * np.exp(spread * noise) if base else spread * noise
        out[name] = jnp.asarray(drawn.astype(out[name].dtype))
    for name, factor in factors.items():
        out[name] = (out[name] * factor).astype(out[name].dtype)
    return out
```

```python
from contextlib import ExitStack

import numpy as np

import concourse.bass as bass
from concourse import mybir

F32 = mybir.dt.float32
BF16 = mybir.dt.bfloat16
I32 = mybir.dt.int32
ALU = mybir.AluOpType
ACT = mybir.ActivationFunctionType
AX_X = mybir.AxisListType.X

NSEQ, T, C = 32, 256, 128
P = 128
TB = T // P
H = 16
DA = C // H
HID = 384
HC = HID // P
QL, KVL = 96, 32
NOPE, ROPE, VD = 32, 64, 32
DB = NOPE + ROPE
KEEP = 32
G = 4
NG = H // G
PARTS = 6
KA = PARTS * DA
SMALL = QL + KVL + ROPE + 3
KR, GT = QL + KVL, QL + KVL + ROPE
BIG = -1e30
FFN_SCALE = 1.0 / 127.0
LN_EPS, RMS_EPS = 1e-5, 1e-6

MISC = [(f"{name}{k}", engine) for name, n, engine in (
    ("A_xT", 1, "act"), ("A_qkv", TB, "dve"), ("A_qkT", 8, "act"), ("A_m", 1, "dve"),
    ("A_yT", 1, "act"), ("A_out", 1, "dve"),
    ("F0_xT", 1, "act"), ("F0_h", HC, "dve"), ("F0_out", 1, "dve"),
    ("B_xT", 1, "act"), ("B_small", 1, "act"), ("B_imp", 1, "act"), ("B_gate", 1, "dve"),
    ("B_nT", 1, "act"), ("B_q", TB * NG, "dve"), ("B_kv", 2 * TB, "act"),
    ("B_qT", TB * NG, "act"), ("B_k1T", TB * NG, "act"),
    ("B_w", TB * NG, "dve"), ("B_vw", TB, "act"), ("B_wT", TB * NG, "act"), ("B_m1", 1, "dve"),
    ("B_pos", 1, "dve"), ("B_sel", 1, "act"), ("B_ks", NG, "dve"), ("B_vs", 1, "dve"), ("B_ksT", 1, "act"),
    ("B_m3", 1, "dve"), ("B_m2", 1, "dve"), ("B_oT", TB, "act"), ("B_out", 1, "dve"),
    ("F1_xT", 1, "act"), ("F1_h", HC, "dve"), ("F1_out", 1, "dve"),
) for k in range(n)]
MISC_AT = {name: n for n, (name, _) in enumerate(MISC)}


def misc_emptied(engine, before):
    return sum(e == engine for _, e in MISC[:before])


PER_TURN = dict(
    x_loaded=16, stored=16, x_used=1,
    misc_full=len(MISC), misc_act=misc_emptied("act", len(MISC)), misc_dve=misc_emptied("dve", len(MISC)),
    max_scores=9 * NG + TB, max_found=9 * NG + TB,
    t_scores=9 * NG + 2, probs=9 * NG + 2,
    pv=4 * NG, o_used=4 * NG,
    var=5, rstd=5, xn=4, nrm=1,
    a_q=TB, a_k=TB, a_y=1, tanh=2 * HC,
    roped=2 * TB * NG + NG, krope=1, k1_full=TB,
    z_exp=1, picked=1, onehot=1, b_sum=1,
    dve_step=0, pool_step=0,
)
PER_TURN["dve_step"] = 69
PER_TURN["pool_step"] = 7
FIRST_STORED = 16


def build(nc, a, out):
    ctx = ExitStack()
    with ctx:
        def sb(name, shape, dt=F32):
            return ctx.enter_context(nc.sbuf_tensor(name, shape, dt))

        def bank(name):
            return ctx.enter_context(nc.psum_tensor(name, [P, 512], F32))

        ident = sb("ident", [P, P])
        ident_h = sb("ident_h", [P, P], BF16)
        mask_q = sb("mask_q", [P, P], BF16)
        mask_k = sb("mask_k", [P, P], BF16)
        row_of = sb("row_of", [48, H, P], BF16)
        row_of_sel = sb("row_of_sel", [48, NG, P], BF16)
        before = sb("before", [P, TB, T])
        before_k = sb("before_k", [P, P])
        ones = sb("ones", [P, P])
        mean_of = sb("mean_of", [P, P])
        slots = sb("slots", [P, KEEP])
        cosx = sb("cosx", [P, TB, DB])
        sinx = sb("sinx", [P, TB, ROPE])
        minus_half = sb("minus_half", [P, 4])
        w_raw = sb("w_raw", [P, HC, P])
        w_int = sb("w_int", [P, HC, P], I32)
        wqkv = sb("wqkv", [P, 3 * C])
        bqkv = sb("bqkv", [P, 3 * C])
        wout = sb("wout", [P, C])
        bout = sb("bout", [P, C])
        wgate = sb("wgate", [P, HID])
        wup = sb("wup", [P, HID])
        wdown = sb("wdown", [P, HC * C])
        wsmall = sb("wsmall", [P, SMALL])
        wimp = sb("wimp", [P, 1])
        wimp_all = sb("wimp_all", [P, P])
        gcol = sb("gcol", [P, 1])
        wq = sb("wq", [QL, H, DB])
        wkv = sb("wkv", [P, 2, H, NOPE])
        wselk = sb("wselk", [P, H, DB])
        wselv = sb("wselv", [P, H, VD])
        wwink = sb("wwink", [P, H, DB])
        wwinv = sb("wwinv", [P, H, VD])
        wproj = sb("wproj", [P, NG, C])
        spare = sb("spare", [P, 4])
        idle = sb("idle", [P, 4])

        x0 = sb("x0", [P, TB, C])
        x1 = sb("x1", [P, TB, C])
        x2 = sb("x2", [P, TB, C])
        x3 = sb("x3", [P, TB, C])
        y = sb("y", [P, TB, C])
        stats = sb("stats", [P, TB, 6])
        mv = sb("mv", [P, TB, 2])
        var = sb("var", [P, 4])
        rstd = sb("rstd", [P, 4])
        xn = sb("xn", [P, TB, C])
        xnT = sb("xnT", [P, T])
        qk = sb("qk", [P, TB, 2 * C])
        rest_q = sb("rest_q", [P, C])
        rest_k = sb("rest_k", [P, C])
        qstack = sb("qstack", [P, TB, H, PARTS, DA], BF16)
        kstack = sb("kstack", [P, TB, H, PARTS, DA], BF16)
        va = sb("va", [P, TB, H, DA + 1])
        negm = sb("negm", [P, TB, H])
        negm_sel = sb("negm_sel", [P, TB, H])
        shift = sb("shift", [48, 4, T], BF16)
        probs = sb("probs", [P, 2, 3, 512])
        rden = sb("rden", [P, 2, TB, G])
        ya = sb("ya", [P, TB, C])
        yaT = sb("yaT", [P, T])
        th = sb("th", [P, 2, T])
        hmid = sb("hmid", [P, 2, T])
        hT = sb("hT", [P, HC, T])
        small = sb("small", [P, TB, SMALL])
        imp = sb("imp", [P, T])
        work = sb("work", [P, T])
        icol = sb("icol", [P, TB])
        rank = sb("rank", [P, TB])
        keep = sb("keep", [P, TB])
        pos = sb("pos", [P, TB])
        onehot = sb("onehot", [P, TB, KEEP])
        z = sb("z", [P, 3])
        zmax = sb("zmax", [P, 1])
        zexp = sb("zexp", [P, 3])
        gate = sb("gate", [P, 3])
        square_sum = sb("square_sum", [P, 4])
        nrm = sb("nrm", [P, TB, P])
        nT = sb("nT", [P, T])
        full = sb("full", [P, TB, H, DB])
        k1full = sb("k1full", [P, TB, H, DB])
        ksfull = sb("ksfull", [KEEP, H, DB])
        swapped = sb("swapped", [P, 2, G, ROPE])
        kr = sb("kr", [P, TB, ROPE])
        kr_swapped = sb("kr_swapped", [P, TB, ROPE])
        qT = sb("qT", [DB, H, T])
        k1T = sb("k1T", [DB, H, T])
        kwT = sb("kwT", [DB, H, T])
        qTa = k1T[0:KA, :, :].bitcast(BF16)[:, :, 0:T]
        kTa = k1T[0:KA, :, :].bitcast(BF16)[:, :, T:2 * T]
        ksT = sb("ksT", [DB, H, KEEP])
        xselT = sb("xselT", [P, KEEP])
        v1 = sb("v1", [P, TB, H, VD + 1])
        vw = sb("vw", [P, TB, H, VD + 1])
        vsel = sb("vsel", [P, NG, G, VD + 1])
        staged = full[:, :, :, :].rearrange("p n h d -> p (n h d)")[:, 0:(2 + H + NG) * P]
        part = k1full[:, :, :, :].rearrange("p n h d -> p (n h d)")\
            .rearrange("p (a n h d) -> p a n h d", a=3, n=TB, h=H)
        oT = sb("oT", [P, NG, T])

        misc = [bank("misc0"), bank("misc1")]
        sq = [bank("sq0"), bank("sq1")]
        sk = [bank("sk0"), bank("sk1")]
        ob = [bank("ob0"), bank("ob1")]

        s = {name: ctx.enter_context(nc.semaphore(f"s_{name}"))
             for name in (*PER_TURN, "c_loaded", "w_turned", "w_copied", "set_dve", "set_pool")}

        def at(i, name, n):
            return s[name], i * PER_TURN[name] + n + (FIRST_STORED if name == "stored" else 0)

        def halves(ap):
            return ap.bitcast(BF16)[:, 1::2]

        USES = [
            dict(m="A_m0", k=KA, q=qTa, key=kTa, v=va, d=DA, scale=DA ** -0.5, view=lambda ap: ap),
            dict(m="B_m10", k=DB, q=qT, key=k1T, v=v1, d=VD, scale=DB ** -0.5, view=halves),
            dict(m="B_m30", k=DB, q=qT, key=kwT, v=vw, d=VD, scale=DB ** -0.5, view=halves),
        ]
        SEL = len(USES)
        GROUPS = [(u, g) for u in range(SEL + 1) for g in range(NG)]

        def misc_count(name):
            n = MISC_AT[name]
            engine = MISC[n][1]
            return f"misc_{engine}", misc_emptied(engine, n + 1)

        TURNED = [
            ("L0_attn_a_W_attn", False, wqkv, HC), ("L0_attn_a_W_proj", False, wout, 1),
            ("L0_ffn_w_gate", True, wgate, HC), ("L0_ffn_w_up", True, wup, HC), ("L0_ffn_w_down", True, wdown, HC),
        ]
        heads = "p (h d) -> p h d"
        LOADED = [
            (ident[:, :], a["c_ident"]), (staged[:, 0:2 * P], a["c_masks"]), (staged[0:48, 2 * P:], a["c_rows"]),
            (before[:, :, :], a["c_before"]),
            (before_k[:, :], a["c_before_k"]), (slots[:, :], a["c_slots"]), (cosx[:, :, :], a["c_cos"]),
            (sinx[:, :, :], a["c_sin"]),
            (bqkv[:, :], a["L0_attn_a_b_attn"].partition_broadcast(P)),
            (bout[:, :], a["L0_attn_a_b_proj"].partition_broadcast(P)),
            (wsmall[:, 0:QL], a["L0_attn_b_w_cq"]), (wsmall[:, QL:KR], a["L0_attn_b_w_ckv"]),
            (wsmall[:, KR:GT], a["L0_attn_b_w_krope"]), (wsmall[:, GT:SMALL], a["L0_attn_b_w_gate"]),
            (wimp[:, :], a["L0_attn_b_w_imp"]),
            (gcol[0:QL, :], a["L0_attn_b_g_qnorm"].rearrange("(p a) -> p a", a=1)),
            (gcol[QL:P, :], a["L0_attn_b_g_kvnorm"].rearrange("(p a) -> p a", a=1)),
            (wq[:, :, 0:NOPE], a["L0_attn_b_w_dq_nope"].rearrange(heads, h=H)),
            (wq[:, :, NOPE:DB], a["L0_attn_b_w_dq_rope"].rearrange(heads, h=H)),
            (wkv[QL:P, 0, :, :], a["L0_attn_b_w_dk_nope"].rearrange(heads, h=H)),
            (wkv[QL:P, 1, :, :], a["L0_attn_b_w_dv"].rearrange(heads, h=H)),
            (wselk[:, :, :], a["L0_attn_b_w_selk"].rearrange(heads, h=H)),
            (wselv[:, :, :], a["L0_attn_b_w_selv"].rearrange(heads, h=H)),
            (wwink[:, :, :], a["L0_attn_b_w_wink"].rearrange(heads, h=H)),
            (wwinv[:, :, :], a["L0_attn_b_w_winv"].rearrange(heads, h=H)),
            (wproj[:, :, :], a["L0_attn_b_w_proj"].rearrange("(n p) c -> p n c", p=P)),
        ]

        def of_tokens(ap):
            return ap.rearrange("(n p) c -> p n c", p=P)

        block = ctx.enter_context(nc.Block())

        @block.sync
        def _(sp):
            for dst, src in LOADED:
                sp.dma_start(dst, src).then_inc(s["c_loaded"], 16)
            for n, (name, integer, _, k) in enumerate(TURNED):
                if n:
                    sp.wait_ge(s["w_turned"], n)
                src = a[name]
                src = src.rearrange("p (n c) -> p n c", c=P) if src.shape[0] == P else of_tokens(src)
                sp.dma_start((w_int if integer else w_raw)[:, 0:k, :], src).then_inc(s["c_loaded"], 16)
            sp.dma_start(x0[:, :, :], of_tokens(a["L0_attn_a_x"][0, :, :])).then_inc(s["x_loaded"], 16)
            with sp.Fori(0, NSEQ - 1) as i:
                sp.wait_ge(*at(i, "x_used", 1))
                sp.dma_start(x0[:, :, :], of_tokens(a["L0_attn_a_x"][i + 1, :, :])).then_inc(s["x_loaded"], 16)
                sp.wait_ge(*at(i, *misc_count("F1_out0")))
                sp.dma_start(of_tokens(out[i, :, :]), y[:, :, :]).then_inc(s["stored"], 16)
            sp.wait_ge(*at(NSEQ - 1, *misc_count("F1_out0")))
            sp.dma_start(of_tokens(out[NSEQ - 1, :, :]), y[:, :, :]).then_inc(s["stored"], 16)
            sp.wait_ge(*at(NSEQ, "stored", 0))

        @block.tensor
        def _(pe):
            for n, (name, integer, dst, k) in enumerate(TURNED):
                pe.wait_ge(s["c_loaded"], 16 * (len(LOADED) + n + 1))
                if integer:
                    pe.wait_ge(s["set_dve"], n - 1)
                if n:
                    pe.wait_ge(s["w_copied"], n)
                for c in range(k):
                    mm = pe.transpose(misc[0][:, c * P:(c + 1) * P], w_raw[:, c, :], ident[:, :])
                mm.then_inc(s["w_turned"], 1)
            pe.wait_ge(s["w_copied"], len(TURNED))
            pe.wait_ge(s["set_dve"], 4)
            pe.wait_ge(s["set_pool"], 1)

            with pe.Fori(0, NSEQ) as i:
                def fill(name):
                    n = MISC_AT[name]
                    if n >= 2:
                        pe.wait_ge(*at(i, *misc_count(MISC[n - 2][0])))
                    return misc[n % 2]

                def carry_waits():
                    pe.ldweights(ident_h[:, :], tile_position=(0, 0))

                def filled(mm):
                    mm.then_inc(s["misc_full"], 1)

                def taken(name):
                    pe.wait_ge(*at(i, *misc_count(name)))

                def normed(name, k):
                    b = fill(name)
                    pe.wait_ge(*at(i, "xn", k + 1))
                    for tb in range(TB):
                        mm = pe.transpose(b[:, tb * P:(tb + 1) * P], xn[:, tb, :], ident[:, :])
                    filled(mm)
                    taken(name)

                def max_scores(u, g):
                    use = USES[u]
                    k, view = use["k"], use["view"]
                    for t in range(3):
                        n = 3 * (NG * u + g) + t
                        if n >= 2:
                            pe.wait_ge(*at(i, "max_found", n - 1))
                        b = sq[n % 2]
                        hs = range(G * g, G * g + G) if t == 0 else range(G * g + 2 * t - 2, G * g + 2 * t)
                        qb, w = (0, P) if t == 0 else (1, T)
                        for j, h in enumerate(hs):
                            pe.matmul(b[:, j * w:(j + 1) * w], view(use["q"][0:k, h, qb * P:(qb + 1) * P]),
                                      view(use["key"][0:k, h, 0:w]), start=(j == 0), stop=False,
                                      skip_group_check=True)
                        diagonal = b[:, :].rearrange("p (j w) -> p j w", w=w)[:, :, w - P:w]
                        pe.matmul(diagonal, ident_h[:, :], mask_q[:, :].unsqueeze(1).broadcast_to((P, len(hs), P)),
                                  start=False, stop=True, skip_group_check=True).then_inc(s["max_scores"], 1)

                def turn_maxima(name, count, m):
                    b = fill(name)
                    pe.wait_ge(*at(i, "max_found", count))
                    for tb in range(TB):
                        mm = pe.transpose(b[0:H, tb * P:(tb + 1) * P], m[:, tb, :], ident[:, :])
                    filled(mm)

                def t_scores(u, g):
                    use = USES[u]
                    k = use["k"]
                    if g == 0:
                        taken(use["m"])
                    for t in range(3):
                        n = 3 * (NG * u + g) + t
                        if n >= 2:
                            pe.wait_ge(*at(i, "probs", n - 1))
                        b = sk[n % 2]
                        hs = range(G * g, G * g + G) if t == 0 else range(G * g + 2 * t - 2, G * g + 2 * t)
                        kb, q0 = (1, P) if t == 0 else (0, 0)
                        w = T - q0
                        for j, h in enumerate(hs):
                            cols = b[:, j * w:(j + 1) * w]
                            pe.matmul(cols, row_of[:, h, :], shift[:, u, q0:T],
                                      start=(j == 0), stop=False, skip_group_check=True)
                            pe.matmul(cols, use["key"][0:k, h, kb * P:(kb + 1) * P], use["q"][0:k, h, q0:T],
                                      start=False, stop=False, skip_group_check=True)
                        diagonal = b[:, :].rearrange("p (j w) -> p j w", w=w)[:, :, 0:P]
                        pe.matmul(diagonal, ident_h[:, :], mask_k[:, :].unsqueeze(1).broadcast_to((P, len(hs), P)),
                                  start=False, stop=True, skip_group_check=True).then_inc(s["t_scores"], 1)

                def pv(u, g):
                    use = USES[u]
                    n = NG * u + g
                    w = use["d"] + 1
                    pe.wait_ge(*at(i, "probs", 3 * n + 3))
                    if n >= 2:
                        pe.wait_ge(*at(i, "o_used", n - 1))
                    pr = probs[:, n % 2, :, :]
                    for j in range(G):
                        h = G * g + j
                        low = pr[:, 1 + j // 2, (j % 2) * T:(j % 2 + 1) * T]
                        for qb in range(TB):
                            o = ob[n % 2][:, (qb * G + j) * w:(qb * G + j + 1) * w]
                            mm = pe.matmul(o, low[:, qb * P:(qb + 1) * P], use["v"][:, 0, h, :],
                                           start=True, stop=(qb == 0))
                            if qb:
                                mm = pe.matmul(o, pr[:, 0, j * P:(j + 1) * P], use["v"][:, 1, h, :],
                                               start=False, stop=True)
                    mm.then_inc(s["pv"], 1)

                def turn_heads(name, src, n, sem, count):
                    tb, g = n // NG, n % NG
                    b = fill(f"{name}{n}")
                    pe.wait_ge(*at(i, sem, count))
                    for j in range(G):
                        mm = pe.transpose(b[0:DB, j * P:(j + 1) * P], src[:, tb, G * g + j, :], ident[:, :])
                    filled(mm)

                def project_heads(name, n, lhsT, w, rows):
                    b = fill(name)
                    g = n % NG
                    filled(pe.matmul(b[0:rows, 0:G * DB], lhsT, w[:, G * g:G * g + G, :], start=True, stop=True))

                def ffn(f):
                    normed(f"F{f}_xT0", 1 + 2 * f)
                    for c in range(HC):
                        b = fill(f"F{f}_h{c}")
                        pe.matmul(b[:, 0:T], wgate[:, c * P:(c + 1) * P], xnT[:, :], start=True, stop=True)
                        filled(pe.matmul(b[:, T:2 * T], wup[:, c * P:(c + 1) * P], xnT[:, :], start=True, stop=True))
                    b = fill(f"F{f}_out0")
                    taken(f"F{f}_h{HC - 1}")
                    for tb in range(TB):
                        for c in range(HC):
                            mm = pe.matmul(b[:, tb * P:(tb + 1) * P], hT[:, c, tb * P:(tb + 1) * P],
                                           wdown[:, c * C:(c + 1) * C], start=(c == 0), stop=(c == HC - 1))
                    filled(mm)

                normed("A_xT0", 0)
                for tb in range(TB):
                    b = fill(f"A_qkv{tb}")
                    filled(pe.matmul(b[:, 0:3 * C], xnT[:, tb * P:(tb + 1) * P], wqkv[:, :], start=True, stop=True))
                for n in range(8):
                    tb, is_k, half = n // 4, n // 2 % 2, n % 2
                    b = fill(f"A_qkT{n}")[0:KA, :].bitcast(BF16)
                    pe.wait_ge(*at(i, "a_k" if is_k else "a_q", tb + 1))
                    carry_waits()
                    stack = kstack if is_k else qstack
                    for j in range(H // 2):
                        mm = pe.transpose(b[:, j * P:(j + 1) * P],
                                          stack[:, tb, half * 8 + j, :, :].rearrange("p s d -> p (s d)"), ident_h[:, :])
                    filled(mm)
                taken("A_qkT7")
                for g in range(NG):
                    max_scores(0, g)
                turn_maxima("A_m0", 3 * NG, negm)
                for g in range(NG):
                    t_scores(0, g)
                    if g:
                        pv(0, g - 1)
                pv(0, NG - 1)
                b = fill("A_yT0")
                pe.wait_ge(*at(i, "o_used", NG))
                for tb in range(TB):
                    mm = pe.transpose(b[:, tb * P:(tb + 1) * P], ya[:, tb, :], ident[:, :])
                filled(mm)
                b = fill("A_out0")
                taken("A_yT0")
                for tb in range(TB):
                    mm = pe.matmul(b[:, tb * P:(tb + 1) * P], yaT[:, tb * P:(tb + 1) * P], wout[:, :],
                                   start=True, stop=True)
                filled(mm)

                ffn(0)

                normed("B_xT0", 2)
                b = fill("B_small0")
                for tb in range(TB):
                    mm = pe.matmul(b[:, tb * SMALL:(tb + 1) * SMALL], xnT[:, tb * P:(tb + 1) * P], wsmall[:, :],
                                   start=True, stop=True)
                filled(mm)
                b = fill("B_imp0")
                filled(pe.matmul(b[:, 0:T], wimp_all[:, :], xnT[:, :], start=True, stop=True))
                b = fill("B_gate0")
                taken("B_small0")
                for tb in range(TB):
                    mm = pe.matmul(b[:, 0:3], mean_of[:, :], small[:, tb, GT:SMALL], start=(tb == 0), stop=(tb == 1))
                filled(mm)
                b = fill("B_nT0")
                pe.wait_ge(*at(i, "nrm", 1))
                for tb in range(TB):
                    mm = pe.transpose(b[:, tb * P:(tb + 1) * P], nrm[:, tb, :], ident[:, :])
                filled(mm)
                taken("B_nT0")
                for n in range(TB * NG):
                    tb = n // NG
                    project_heads(f"B_q{n}", n, nT[0:QL, tb * P:(tb + 1) * P], wq, P)
                for n in range(2 * TB):
                    tb = n // 2
                    b = fill(f"B_kv{n}")
                    filled(pe.matmul(b[:, :], nT[QL:P, tb * P:(tb + 1) * P],
                                     wkv[QL:P, n % 2, :, :].rearrange("p h d -> p (h d)"), start=True, stop=True))
                for n in range(TB * NG):
                    turn_heads("B_qT", full, n, "roped", n + 1)
                taken("B_kv2")
                for n in range(TB * NG):
                    turn_heads("B_k1T", k1full, n, "k1_full", n // NG + 1)
                taken("B_k1T7")
                for g in range(NG):
                    max_scores(1, g)
                    for n in (2 * g, 2 * g + 1):
                        tb = n // NG
                        project_heads(f"B_w{n}", n, xnT[:, tb * P:(tb + 1) * P], wwink, P)
                for tb in range(TB):
                    b = fill(f"B_vw{tb}")
                    filled(pe.matmul(b[:, :], xnT[:, tb * P:(tb + 1) * P], wwinv[:, :, :].rearrange("p h d -> p (h d)"),
                                     start=True, stop=True))
                for n in range(TB * NG):
                    turn_heads("B_wT", full, n, "roped", TB * NG + n + 1)
                turn_maxima("B_m10", 6 * NG, negm)
                b = fill("B_pos0")
                pe.wait_ge(*at(i, "picked", 1))
                pe.matmul(b[:, 0:1], before_k[:, :], keep[:, 0:1], start=True, stop=True)
                pe.matmul(b[:, 1:2], ones[:, :], keep[:, 0:1], start=True, stop=False)
                filled(pe.matmul(b[:, 1:2], before_k[:, :], keep[:, 1:2], start=False, stop=True))
                b = fill("B_sel0")
                pe.wait_ge(*at(i, "onehot", 1))
                for tb in range(TB):
                    mm = pe.matmul(b[:, 0:KEEP], xn[:, tb, :], onehot[:, tb, :], start=(tb == 0), stop=(tb == 1))
                filled(mm)
                taken("B_sel0")
                for g in range(NG):
                    project_heads(f"B_ks{g}", g, xselT[:, :], wselk, KEEP)
                b = fill("B_vs0")
                for j in range(G):
                    mm = pe.matmul(b[KEEP * j:KEEP * (j + 1), 0:NG * VD], xselT[:, :], wselv[:, j::G, :],
                                   start=True, stop=True)
                filled(mm)
                b = fill("B_ksT0")
                pe.wait_ge(*at(i, "roped", 2 * TB * NG + NG))
                carry_waits()
                for h in range(H):
                    mm = pe.transpose(b[0:DB, h * KEEP:(h + 1) * KEEP], ksfull[:, h, :], ident[0:KEEP, 0:KEEP])
                filled(mm)
                taken("B_wT7")
                for g in range(NG):
                    t_scores(1, g)
                    max_scores(2, g)
                    if g:
                        pv(1, g - 1)
                pv(1, NG - 1)
                taken("B_ksT0")
                for tb in range(TB):
                    n = 9 * NG + tb
                    pe.wait_ge(*at(i, "max_found", n - 1))
                    for h in range(H):
                        mm = pe.matmul(sq[n % 2][:, h * KEEP:(h + 1) * KEEP], halves(qT[:, h, tb * P:(tb + 1) * P]),
                                       halves(ksT[:, h, :]), start=(h == 0), stop=(h == H - 1),
                                       skip_group_check=True)
                    mm.then_inc(s["max_scores"], 1)
                turn_maxima("B_m30", 9 * NG, negm)
                turn_maxima("B_m20", 9 * NG + TB, negm_sel)
                for g in range(NG):
                    t_scores(2, g)
                    if g:
                        pv(2, g - 1)
                pv(2, NG - 1)
                taken("B_m20")
                for t in range(2):
                    n = 9 * NG + t
                    pe.wait_ge(*at(i, "probs", n - 1))
                    for e in range(2):
                        g = 2 * t + e
                        cols = sk[n % 2][:, e * T:(e + 1) * T]
                        pe.matmul(cols, row_of_sel[:, g, :], shift[:, SEL, :], start=(e == 0), stop=False,
                                  skip_group_check=True)
                        for j in range(G):
                            mm = pe.matmul(cols[KEEP * j:KEEP * (j + 1), :], ksT[:, G * g + j, :], qT[:, G * g + j, :],
                                           start=False, stop=True, skip_group_check=True)
                    mm.then_inc(s["t_scores"], 1)
                for g in range(NG):
                    n = NG * SEL + g
                    w = G * (VD + 1)
                    pe.wait_ge(*at(i, "probs", 9 * NG + g // 2 + 1))
                    pe.wait_ge(*at(i, "o_used", n - 1))
                    pr = probs[:, 0, g // 2, (g % 2) * T:(g % 2 + 1) * T]
                    for tb in range(TB):
                        mm = pe.matmul(ob[n % 2][:, tb * w:(tb + 1) * w], pr[:, tb * P:(tb + 1) * P],
                                       vsel[:, g, :, :].rearrange("p j d -> p (j d)"), start=True, stop=True)
                    mm.then_inc(s["pv"], 1)
                pe.wait_ge(*at(i, "b_sum", 1))
                for tb in range(TB):
                    b = fill(f"B_oT{tb}")
                    for n in range(NG):
                        mm = pe.transpose(b[:, n * P:(n + 1) * P],
                                          part[:, 0, tb, G * n:G * n + G, :].rearrange("p h d -> p (h d)"), ident[:, :])
                    filled(mm)
                b = fill("B_out0")
                taken("B_oT1")
                for tb in range(TB):
                    for n in range(NG):
                        mm = pe.matmul(b[:, tb * P:(tb + 1) * P], oT[:, n, tb * P:(tb + 1) * P], wproj[:, n, :],
                                       start=(n == 0), stop=(n == NG - 1))
                filled(mm)

                ffn(1)

        @block.scalar
        def _(act):
            for n, (name, integer, dst, k) in enumerate(TURNED):
                act.wait_ge(s["w_turned"], n + 1)
                act.activation(dst[:, :], misc[0][:, 0:k * P], ACT.Copy).then_inc(s["w_copied"], 1)

            with act.Fori(0, NSEQ) as i:
                def empty(name, *copies):
                    n = MISC_AT[name]
                    act.wait_ge(*at(i, "misc_full", n + 1))
                    for dst, src in copies:
                        ins = act.activation(dst, src(misc[n % 2]), ACT.Copy)
                    ins.then_inc(s["misc_act"], 1)

                def heads_out(name, dst, n):
                    tb, g = n // NG, n % NG
                    empty(f"{name}{n}", (dst[:, G * g:G * g + G, tb * P:(tb + 1) * P],
                                         lambda b: b[0:DB, :].rearrange("p (j t) -> p j t", t=P)))

                def exps(u, g):
                    n = NG * u + g
                    for t in range(3):
                        act.wait_ge(*at(i, "t_scores", 3 * n + t + 1))
                        if t == 0 and n >= 2:
                            act.wait_ge(*at(i, "pv", n - 1))
                        act.activation(probs[:, n % 2, t, :], sk[(3 * n + t) % 2][:, :], ACT.Exp,
                                       scale=USES[u]["scale"]).then_inc(s["probs"], 1)

                def ffn(f):
                    empty(f"F{f}_xT0", (xnT[:, :], lambda b: b[:, 0:T]))
                    for c in range(HC):
                        n = MISC_AT[f"F{f}_h{c}"]
                        act.wait_ge(*at(i, "misc_full", n + 1))
                        act.activation(th[:, c % 2, :], misc[n % 2][:, 0:T], ACT.Tanh, scale=0.5)\
                            .then_inc(s["tanh"], 1)

                empty("A_xT0", (xnT[:, :], lambda b: b[:, 0:T]))
                for n in range(8):
                    tb, is_k, half = n // 4, n // 2 % 2, n % 2
                    empty(f"A_qkT{n}", ((kTa if is_k else qTa)[:, half * 8:half * 8 + 8, tb * P:(tb + 1) * P],
                                        lambda b: b[0:KA, :].bitcast(BF16).rearrange("p (j t) -> p j t", t=P)))
                for g in range(NG):
                    exps(0, g)
                empty("A_yT0", (yaT[:, :], lambda b: b[:, 0:T]))
                ffn(0)
                empty("B_xT0", (xnT[:, :], lambda b: b[:, 0:T]))
                empty("B_small0", (small[:, :, :].rearrange("p n c -> p (n c)"), lambda b: b[:, 0:TB * SMALL]))
                empty("B_imp0", (imp[:, :], lambda b: b[:, 0:T]))
                act.wait_ge(*at(i, *misc_count("B_gate0")))
                act.activation(zexp[:, :], z[:, :], ACT.Exp).then_inc(s["z_exp"], 1)
                empty("B_nT0", (nT[:, :], lambda b: b[:, 0:T]))
                for n in range(2 * TB):
                    tb = n // 2
                    dst = v1[:, tb, :, 0:VD] if n % 2 else k1full[:, tb, :, 0:NOPE]
                    empty(f"B_kv{n}", (dst, lambda b: b[:, :].rearrange("p (h d) -> p h d", h=H)))
                for n in range(TB * NG):
                    heads_out("B_qT", qT, n)
                for n in range(TB * NG):
                    heads_out("B_k1T", k1T, n)
                for tb in range(TB):
                    empty(f"B_vw{tb}", (vw[:, tb, :, 0:VD], lambda b: b[:, :].rearrange("p (h d) -> p h d", h=H)))
                for n in range(TB * NG):
                    heads_out("B_wT", kwT, n)
                empty("B_sel0", (xselT[:, :], lambda b: b[:, 0:KEEP]))
                empty("B_ksT0", (ksT[:, :, :].rearrange("p h t -> p (h t)"), lambda b: b[0:DB, :]))
                for u in (1, 2):
                    for g in range(NG):
                        exps(u, g)
                for t in range(2):
                    n = 9 * NG + t
                    act.wait_ge(*at(i, "t_scores", n + 1))
                    if t == 0:
                        act.wait_ge(*at(i, "pv", NG * SEL - 1))
                    act.activation(probs[:, 0, t, :], sk[n % 2][:, :], ACT.Exp, scale=DB ** -0.5)\
                        .then_inc(s["probs"], 1)
                for tb in range(TB):
                    empty(f"B_oT{tb}", (oT[:, :, tb * P:(tb + 1) * P],
                                        lambda b: b[:, :].rearrange("p (n t) -> p n t", t=P)))
                ffn(1)

        @block.vector
        def _(dve):
            for n, (name, integer, _, k) in enumerate(TURNED):
                if integer:
                    dve.wait_ge(s["c_loaded"], 16 * (len(LOADED) + n + 1))
                    dve.tensor_scalar(w_raw[:, :, :], w_int[:, :, :], FFN_SCALE, None, ALU.mult)\
                        .then_inc(s["set_dve"], 1)
            dve.tensor_copy(ident_h[:, :], ident[:, :])
            dve.tensor_copy(mask_q[:, :], staged[:, 0:P])
            dve.tensor_copy(mask_k[:, :], staged[:, P:2 * P])
            dve.tensor_copy(row_of[:, :, :].rearrange("p h k -> p (h k)"), staged[0:48, 2 * P:(2 + H) * P])
            dve.tensor_copy(row_of_sel[:, :, :].rearrange("p g k -> p (g k)"), staged[0:48, (2 + H) * P:])
            dve.tensor_scalar(wq[:, :, :], wq[:, :, :], gcol[0:QL, 0:1], None, ALU.mult)
            dve.tensor_scalar(wkv[QL:P, :, :, :], wkv[QL:P, :, :, :], gcol[QL:P, 0:1], None, ALU.mult)
            dve.tensor_scalar(wsmall[:, KR:GT], wsmall[:, KR:GT], 1.0 / H, None, ALU.mult)
            dve.wait_ge(s["set_pool"], 1)
            for j in range(G):
                dve.memset(vsel[KEEP * j:KEEP * (j + 1), :, j, VD:VD + 1], 1.0)
            for v in (va, v1, vw):
                d = v.shape[3] - 1
                dve.memset(v[:, :, :, d:d + 1], 1.0)
            dve.memset(ones[:, :], 1.0)
            dve.memset(mean_of[:, :], 1.0 / T)
            dve.memset(wimp_all[:, :], 1.0).then_inc(s["dve_step"], 1)
            dve.wait_ge(s["dve_step"], 1)
            dve.memset(spare[:, 0:1], 0.0).then_inc(s["stored"], FIRST_STORED)
            dve.tensor_scalar(wimp_all[:, :], wimp_all[:, :], wimp[:, 0:1], None, ALU.mult).then_inc(s["set_dve"], 1)

            with dve.Fori(0, NSEQ) as i:
                step = [0]

                def then(ins):
                    step[0] += 1
                    ins.then_inc(s["dve_step"], 1)
                    dve.wait_ge(s["dve_step"], i * PER_TURN["dve_step"] + step[0] + 1)

                def full_bank(name):
                    n = MISC_AT[name]
                    dve.wait_ge(*at(i, "misc_full", n + 1))
                    return misc[n % 2]

                def emptied(ins):
                    ins.then_inc(s["misc_dve"], 1)

                def written(name):
                    dve.wait_ge(*at(i, *misc_count(name)))

                def norm(x, k, at_var):
                    for tb in range(TB):
                        ins = dve.bn_stats(stats[:, tb, :], x[:, tb, :])
                    then(ins)
                    dve.memset(spare[:, 1:2], 0.0)
                    for tb in range(TB):
                        ins = dve.bn_aggr(mv[:, tb, :], stats[:, tb, :])
                    then(ins)
                    dve.tensor_scalar(var[:, 0:TB], mv[:, :, 1], LN_EPS, None, ALU.add).then_inc(s["var"], 1)
                    dve.wait_ge(*at(i, "rstd", at_var + 1))
                    for tb in range(TB):
                        ins = dve.tensor_scalar(xn[:, tb, :], x[:, tb, :], mv[:, tb, 0:1], rstd[:, tb:tb + 1],
                                                ALU.subtract, ALU.mult)
                    ins.then_inc(s["xn"], 1)

                def maxima(u, g):
                    for t in range(3):
                        n = 3 * (NG * u + g) + t
                        dve.wait_ge(*at(i, "max_scores", n + 1))
                        h0, k, w = (G * g, G, P) if t == 0 else (G * g + 2 * t - 2, 2, T)
                        dve.tensor_reduce(negm[:, 0 if t == 0 else 1, h0:h0 + k],
                                          sq[n % 2][:, :].rearrange("p (j w) -> p j w", w=w), AX_X, ALU.max,
                                          negate=True).then_inc(s["max_found"], 1)

                def shifts(name, u):
                    b = full_bank(name)
                    then(dve.tensor_copy(shift[0:H, u, :], b[0:H, 0:T]))
                    emptied(dve.tensor_tensor(shift[32:32 + H, u, :], b[0:H, 0:T], shift[0:H, u, :], ALU.subtract))

                def scale_out(u, g, d, dst, by_gate):
                    n = NG * u + g
                    dve.wait_ge(*at(i, "pv", n + 1))
                    rd = rden[:, n % 2, :, :]
                    o = ob[n % 2][:, 0:TB * G * (d + 1)].rearrange("p (n j d) -> p n j d", n=TB, j=G)
                    then(dve.reciprocal(rd, o[:, :, :, d]))
                    if by_gate is not None:
                        then(dve.tensor_scalar(rd, rd, by_gate, None, ALU.mult))
                    dve.tensor_tensor(dst, o[:, :, :, 0:d], rd.unsqueeze(3).broadcast_to((P, TB, G, d)),
                                      ALU.mult).then_inc(s["o_used"], 1)

                def rope(name, n, dst, tb, rows, g):
                    b = full_bank(name)
                    v = b[0:rows, 0:G * DB].rearrange("p (j d) -> p j d", j=G)
                    if n >= 2:
                        dve.wait_ge(*at(i, "roped", n - 1))
                    dve.tensor_tensor(dst, v, cosx[0:rows, tb, :].unsqueeze(1).broadcast_to((rows, G, DB)), ALU.mult)
                    halves_swapped = v[:, :, NOPE:DB].rearrange("p j (e d) -> p j e d", e=2)[:, :, ::-1, :]
                    sines = sinx[0:rows, tb, :].rearrange("p (e d) -> p e d", e=2).unsqueeze(1)
                    emptied(dve.tensor_tensor(
                        swapped[0:rows, n % 2, :, :].rearrange("p j (e d) -> p j e d", e=2), halves_swapped,
                        sines.broadcast_to((rows, G, 2, ROPE // 2)), ALU.mult))

                def ffn(f, x, dst):
                    norm(x, 1 + 2 * f, 1 if f == 0 else 4)
                    for c in range(HC):
                        b = full_bank(f"F{f}_h{c}")
                        dve.wait_ge(*at(i, "tanh", HC * f + c + 1))
                        then(dve.scalar_tensor_tensor(out=hmid[:, c % 2, :], in0=th[:, c % 2, :], scalar=1.0,
                                                      in1=b[:, 0:T], op0=ALU.add, op1=ALU.mult))
                        emptied(dve.scalar_tensor_tensor(out=hT[:, c, :], in0=hmid[:, c % 2, :], scalar=0.5,
                                                         in1=b[:, T:2 * T], op0=ALU.mult, op1=ALU.mult))
                    b = full_bank(f"F{f}_out0")
                    if f:
                        dve.wait_ge(*at(i, "stored", 0))
                    ins = dve.tensor_tensor(dst[:, :, :], b[:, 0:T].rearrange("p (n c) -> p n c", c=C), x[:, :, :],
                                            ALU.add)
                    emptied(ins)
                    written(f"F{f}_out0")

                dve.wait_ge(*at(i, "x_loaded", 16))
                norm(x0, 0, 0)
                for tb in range(TB):
                    b = full_bank(f"A_qkv{tb}")
                    dve.tensor_tensor(va[:, tb, :, 0:DA], b[:, 2 * C:3 * C].rearrange("p (h d) -> p h d", h=H),
                                      bqkv[:, 2 * C:3 * C].rearrange("p (h d) -> p h d", h=H), ALU.add)
                    emptied(dve.tensor_tensor(qk[:, tb, :], b[:, 0:2 * C], bqkv[:, 0:2 * C], ALU.add))
                for tb in range(TB):
                    q = qk[:, tb, 0:C].rearrange("p (h d) -> p h d", h=H)
                    r = rest_q[:, :].rearrange("p (h d) -> p h d", h=H)
                    dve.wait_ge(*at(i, "misc_dve", misc_count(f"A_qkv{tb}")[1]))
                    then(dve.tensor_copy(qstack[:, tb, :, 0:3, :], q.unsqueeze(2).broadcast_to((P, H, 3, DA))))
                    then(dve.tensor_tensor(r, q, qstack[:, tb, :, 0, :], ALU.subtract))
                    then(dve.tensor_copy(qstack[:, tb, :, 3:5, :], r.unsqueeze(2).broadcast_to((P, H, 2, DA))))
                    dve.tensor_tensor(qstack[:, tb, :, 5, :], r, qstack[:, tb, :, 3, :], ALU.subtract)\
                        .then_inc(s["a_q"], 1)
                    if tb == 0:
                        dve.wait_ge(*at(i, "a_q", 1))
                for g in range(NG):
                    maxima(0, g)
                shifts("A_m0", 0)
                for g in range(NG):
                    scale_out(0, g, DA, ya[:, :, G * DA * g:G * DA * (g + 1)].rearrange("p n (j d) -> p n j d", j=G),
                              None)
                b = full_bank("A_out0")
                emptied(dve.tensor_tensor(x1[:, :, :], b[:, 0:T].rearrange("p (n c) -> p n c", c=C), x0[:, :, :], ALU.add))
                written("A_out0")
                dve.tensor_tensor(x1[:, :, :], x1[:, :, :], bout[:, :].unsqueeze(1).broadcast_to((P, TB, C)), ALU.add)\
                    .then_inc(s["x_used"], 1)
                dve.wait_ge(*at(i, "x_used", 1))
                ffn(0, x1, x2)

                norm(x2, 2, 2)
                dve.wait_ge(*at(i, *misc_count("B_small0")))
                for j, (c0, c1) in enumerate(((0, QL), (QL, KR))):
                    for tb in range(TB):
                        ins = dve.tensor_tensor_reduce(work[:, 0:c1 - c0], small[:, tb, c0:c1], small[:, tb, c0:c1],
                                                       1.0, 0.0, ALU.mult, ALU.add, square_sum[:, TB * j + tb:TB * j + tb + 1])
                        then(ins)
                dve.tensor_scalar(var[:, 0:2], square_sum[:, 0:2], 1.0 / QL, RMS_EPS, ALU.mult, ALU.add)
                dve.tensor_scalar(var[:, 2:4], square_sum[:, 2:4], 1.0 / KVL, RMS_EPS, ALU.mult, ALU.add)\
                    .then_inc(s["var"], 1)
                b = full_bank("B_gate0")
                then(dve.tensor_reduce(zmax[:, :], b[:, 0:3], AX_X, ALU.max))
                emptied(dve.tensor_scalar(z[:, :], b[:, 0:3], zmax[:, 0:1], None, ALU.subtract))
                dve.wait_ge(*at(i, "rstd", 4))
                for tb in range(TB):
                    dve.tensor_scalar(nrm[:, tb, 0:QL], small[:, tb, 0:QL], rstd[:, tb:tb + 1], None, ALU.mult)
                    ins = dve.tensor_scalar(nrm[:, tb, QL:P], small[:, tb, QL:KR], rstd[:, 2 + tb:3 + tb], None, ALU.mult)
                ins.then_inc(s["nrm"], 1)
                dve.wait_ge(*at(i, "z_exp", 1))
                then(dve.tensor_reduce(zmax[:, :], zexp[:, :], AX_X, ALU.add))
                then(dve.reciprocal(zmax[:, :], zmax[:, :]))
                then(dve.tensor_scalar(gate[:, :], zexp[:, :], zmax[:, 0:1], None, ALU.mult))
                k = small[:, :, KR:GT]
                dve.tensor_tensor(kr[:, :, :], k, cosx[:, :, NOPE:DB], ALU.mult)
                then(dve.tensor_tensor(kr_swapped[:, :, :].rearrange("p n (e d) -> p n e d", e=2),
                                       k.rearrange("p n (e d) -> p n e d", e=2)[:, :, ::-1, :],
                                       sinx[:, :, :].rearrange("p n (e d) -> p n e d", e=2), ALU.mult))
                dve.tensor_tensor(kr[:, :, :], kr[:, :, :], kr_swapped[:, :, :], ALU.add).then_inc(s["krope"], 1)
                dve.wait_ge(*at(i, *misc_count("B_imp0")))
                for tb in range(TB):
                    then(dve.tensor_tensor_reduce(work[:, 0:P], imp[:, tb * P:(tb + 1) * P], ident[:, :], 1.0, 0.0,
                                                  ALU.mult, ALU.add, icol[:, tb:tb + 1]))
                    then(dve.scalar_tensor_tensor(out=work[:, :], in0=imp[:, :], scalar=icol[:, tb:tb + 1],
                                                  in1=before[:, tb, :], op0=ALU.is_equal, op1=ALU.mult))
                    then(dve.scalar_tensor_tensor(out=work[:, :], in0=imp[:, :], scalar=icol[:, tb:tb + 1],
                                                  in1=work[:, :], op0=ALU.is_gt, op1=ALU.add))
                    then(dve.tensor_reduce(rank[:, tb:tb + 1], work[:, :], AX_X, ALU.add))
                dve.tensor_scalar(keep[:, :], rank[:, :], float(KEEP), None, ALU.is_lt).then_inc(s["picked"], 1)
                for n in range(TB * NG):
                    tb, g = n // NG, n % NG
                    rope(f"B_q{n}", n, full[:, tb, G * g:G * g + G, :], tb, P, g)
                for g in range(NG):
                    maxima(1, g)
                    for n in (2 * g, 2 * g + 1):
                        tb, gg = n // NG, n % NG
                        rope(f"B_w{n}", TB * NG + n, full[:, tb, G * gg:G * gg + G, :], tb, P, gg)
                shifts("B_m10", 1)
                b = full_bank("B_pos0")
                emptied(dve.tensor_copy(pos[:, :], b[:, 0:TB]))
                written("B_pos0")
                for tb in range(TB):
                    ins = dve.tensor_scalar(onehot[:, tb, :], slots[:, :], pos[:, tb:tb + 1], keep[:, tb:tb + 1],
                                            ALU.is_equal, ALU.mult)
                ins.then_inc(s["onehot"], 1)
                for g in range(NG):
                    rope(f"B_ks{g}", 2 * TB * NG + g, ksfull[:, G * g:G * g + G, :], 0, KEEP, g)
                b = full_bank("B_vs0")
                for j in range(G):
                    rows = slice(KEEP * j, KEEP * (j + 1))
                    ins = dve.tensor_copy(vsel[rows, :, j, 0:VD], b[rows, 0:NG * VD].rearrange("p (g d) -> p g d", g=NG))
                emptied(ins)
                for g in range(NG):
                    maxima(2, g)
                    if g:
                        scale_out(1, g - 1, VD, part[:, 0, :, G * (g - 1):G * g, :], gate[:, 0:1])
                scale_out(1, NG - 1, VD, part[:, 0, :, G * (NG - 1):H, :], gate[:, 0:1])
                for tb in range(TB):
                    n = 9 * NG + tb
                    dve.wait_ge(*at(i, "max_scores", n + 1))
                    dve.tensor_reduce(negm_sel[:, tb, :], sq[n % 2][:, :].rearrange("p (h w) -> p h w", w=KEEP), AX_X,
                                      ALU.max, negate=True).then_inc(s["max_found"], 1)
                shifts("B_m30", 2)
                shifts("B_m20", SEL)
                for g in range(NG):
                    scale_out(2, g, VD, part[:, 2, :, G * g:G * g + G, :], gate[:, 2:3])
                for g in range(NG):
                    scale_out(SEL, g, VD, part[:, 1, :, G * g:G * g + G, :], gate[:, 1:2])
                b = full_bank("B_out0")
                emptied(dve.tensor_tensor(x3[:, :, :], b[:, 0:T].rearrange("p (n c) -> p n c", c=C), x2[:, :, :], ALU.add))
                written("B_out0")
                ffn(1, x3, y)
                assert step[0] == PER_TURN["dve_step"], step[0]

        @block.gpsimd
        def _(pool):
            pool.memset(shift[:, :, :], 0.0)
            pool.memset(idle[:, :], 0.0)
            pool.memset(vsel[:, :, :, :], 0.0).then_inc(s["pool_step"], 1)
            pool.memset(minus_half[:, :], -0.5).then_inc(s["set_pool"], 1)
            pool.wait_ge(s["set_pool"], 1)

            with pool.Fori(0, NSEQ) as i:
                step = [0]

                def then(ins):
                    step[0] += 1
                    ins.then_inc(s["pool_step"], 1)
                    pool.wait_ge(s["pool_step"], i * PER_TURN["pool_step"] + step[0] + 1)

                def carry_waits():
                    pool.tensor_tensor(idle[:, 2:3], idle[:, 0:1], idle[:, 1:2], ALU.add)

                def rsqrt(k, n):
                    pool.wait_ge(*at(i, "var", k + 1))
                    pool.tensor_tensor(rstd[:, 0:n], var[:, 0:n], minus_half[:, 0:n], ALU.pow).then_inc(s["rstd"], 1)

                def add_swapped(n, name, dst, rows):
                    pool.wait_ge(*at(i, *misc_count(name)))
                    pool.tensor_tensor(dst, dst, swapped[0:rows, n % 2, :, :], ALU.add).then_inc(s["roped"], 1)

                rsqrt(0, TB)
                for tb in range(TB):
                    k = qk[:, tb, C:2 * C].rearrange("p (h d) -> p h d", h=H)
                    r = rest_k[:, :].rearrange("p (h d) -> p h d", h=H)
                    pool.wait_ge(*at(i, *misc_count(f"A_qkv{tb}")))
                    carry_waits()
                    pool.tensor_copy(kstack[:, tb, :, 3, :], k)
                    pool.tensor_copy(kstack[:, tb, :, 5, :], k)
                    then(pool.tensor_copy(kstack[:, tb, :, 0, :], k))
                    then(pool.tensor_tensor(r, k, kstack[:, tb, :, 0, :], ALU.subtract))
                    carry_waits()
                    pool.tensor_copy(kstack[:, tb, :, 4, :], r)
                    then(pool.tensor_copy(kstack[:, tb, :, 1, :], r))
                    pool.tensor_tensor(kstack[:, tb, :, 2, :], r, kstack[:, tb, :, 1, :], ALU.subtract)\
                        .then_inc(s["a_k"], 1)
                    pool.wait_ge(*at(i, "a_k", tb + 1))
                rsqrt(1, TB)
                rsqrt(2, TB)
                rsqrt(3, 2 * TB)
                pool.wait_ge(*at(i, "krope", 1))
                carry_waits()
                for tb in range(TB):
                    pool.tensor_copy(k1full[:, tb, :, NOPE:DB], kr[:, tb, :].unsqueeze(1).broadcast_to((P, H, ROPE)))\
                        .then_inc(s["k1_full"], 1)
                for w in range(2):
                    for n in range(TB * NG):
                        tb, g = n // NG, n % NG
                        add_swapped(TB * NG * w + n, f"B_{'qw'[w]}{n}", full[:, tb, G * g:G * g + G, NOPE:DB], P)
                for g in range(NG):
                    add_swapped(2 * TB * NG + g, f"B_ks{g}", ksfull[:, G * g:G * g + G, NOPE:DB], KEEP)
                pool.wait_ge(*at(i, "o_used", 3 * NG))
                then(pool.tensor_tensor(part[:, 0, :, :, :], part[:, 0, :, :, :], part[:, 2, :, :, :], ALU.add))
                pool.wait_ge(*at(i, "o_used", 4 * NG))
                pool.tensor_tensor(part[:, 0, :, :, :], part[:, 0, :, :, :], part[:, 1, :, :, :], ALU.add)\
                    .then_inc(s["b_sum"], 1)
                rsqrt(4, TB)
                assert step[0] == PER_TURN["pool_step"], step[0]


def constants():
    i, j = np.arange(P)[:, None], np.arange(P)[None, :]
    row_of = np.zeros((48, H, P), np.float32)
    row_of_sel = np.zeros((48, NG, P), np.float32)
    for h in range(H):
        for first in (0, 32):
            row_of[first + h, h, :] = 1
            row_of_sel[first + h, h // G, KEEP * (h % G):KEEP * (h % G + 1)] = 1
    token = np.arange(TB)[None, :, None] * P + np.arange(P)[:, None, None]
    freq = (1.0 / np.float32(10000.0) ** (np.arange(0, ROPE, 2, dtype=np.float32) / np.float32(ROPE))).astype(np.float32)
    angle = token.astype(np.float32) * freq
    cos, sin = np.cos(angle).astype(np.float32), np.sin(angle).astype(np.float32)
    return {
        "c_ident": np.eye(P, dtype=np.float32),
        "c_masks": np.concatenate([np.where(j > i, BIG, 0), np.where(i > j, BIG, 0)], axis=1).astype(np.float32),
        "c_rows": np.concatenate([row_of.reshape(48, -1), row_of_sel.reshape(48, -1)], axis=1),
        "c_before": (np.arange(T)[None, None, :] < token).astype(np.float32),
        "c_before_k": (i < j).astype(np.float32),
        "c_slots": np.tile(np.arange(KEEP, dtype=np.float32), (P, 1)),
        "c_cos": np.concatenate([np.ones((P, TB, NOPE), np.float32), cos, cos], axis=2),
        "c_sin": np.concatenate([-sin, sin], axis=2),
    }


INPUTS = ["L0_attn_a_x", "L0_attn_a_W_attn", "L0_attn_a_b_attn", "L0_attn_a_W_proj", "L0_attn_a_b_proj",
          "L0_attn_b_w_cq", "L0_attn_b_g_qnorm", "L0_attn_b_w_dq_nope", "L0_attn_b_w_dq_rope", "L0_attn_b_w_ckv",
          "L0_attn_b_g_kvnorm", "L0_attn_b_w_dk_nope", "L0_attn_b_w_dv", "L0_attn_b_w_krope", "L0_attn_b_w_imp",
          "L0_attn_b_w_selk", "L0_attn_b_w_selv", "L0_attn_b_w_wink", "L0_attn_b_w_winv", "L0_attn_b_w_gate",
          "L0_attn_b_w_proj", "L0_ffn_w_gate", "L0_ffn_w_up", "L0_ffn_w_down"]


def kernel(**inputs):
    import concourse.bacc as bacc
    from concourse.bass_utils import run_bass_kernel_spmd

    nc = bacc.Bacc("TRN2", target_bir_lowering=False, num_devices=1)
    arrays = {name: np.ascontiguousarray(inputs[name]) for name in INPUTS}
    arrays.update(constants())
    args = {name: nc.dram_tensor(name, v.shape, mybir.dt.from_np(v.dtype), kind="ExternalInput").ap()
            for name, v in arrays.items()}
    out = nc.dram_tensor("out", (NSEQ, T, C), F32, kind="ExternalOutput").ap()
    build(nc, args, out)
    r = run_bass_kernel_spmd(nc, [arrays], core_ids=[0])
    return r.results[0]["out"]
```

```python
from contextlib import ExitStack

import numpy as np

import concourse.bass as bass
from concourse import mybir

F32 = mybir.dt.float32
BF16 = mybir.dt.bfloat16
I32 = mybir.dt.int32
ALU = mybir.AluOpType
ACT = mybir.ActivationFunctionType
AX_X = mybir.AxisListType.X

NSEQ, T, C = 32, 256, 128
TURNS = NSEQ + 1
P = 128
TB = T // P
H = 16
DA = C // H
HID = 384
HC = HID // P
QL, KVL = 96, 32
NOPE, ROPE, VD = 32, 64, 32
DB = NOPE + ROPE
KEEP = 32
G = 4
NG = H // G
SA, SB = 64, DB
PARTS = 6
KA = PARTS * DA
SMALL = QL + KVL + ROPE + 3
KR, GT = QL + KVL, QL + KVL + ROPE
BIG = -1e30
FFN_SCALE = 1.0 / 127.0
LN_EPS, RMS_EPS = 1e-5, 1e-6


def steps(text):
    return [(w.split(":")[0], int(w.split(":")[1]) if ":" in w else 0) for w in text.split()]


ORDER = steps("""
    A_norm B_t1:0 B_rank B_w:0 B_w:1 A_xT B_w:2 B_w:3 B_t1:1 A_qkv:0 B_wT:0 B_pos B_pv1:0 B_w:4 A_qkv:1
    B_wT:1 B_sel A_split:0 B_w:5 B_wT:2 B_w:6 B_t1:2 B_wT:3 A_split:1 B_w:7 B_wT:4 B_wT:5 B_vw:0 B_pv1:1
    A_turn:0 A_turn:1 B_max3:0 A_turn:2 A_turn:3 B_wT:6 B_wT:7 B_t1:3 B_vw:1 A_turn:4 A_turn:5
    B_max3:1 B_pv1:2 A_turn:6 A_turn:7 B_ks:0 B_max3:2 B_ks:1 A_max:0 B_pv1:3 B_ks:2 B_max3:3 B_ks:3
    A_max:1 B_vs B_m3 A_max:2 B_ksT A_max:3 B_s2:0 A_m B_s2:1
    B_t3:0 A_t:0 B_p2:0 B_pv3:0 A_t:1 A_pv:0 B_p2:1 A_t:2 A_pv:1 B_pv2:0 A_t:3 A_pv:2 B_pv2:1 B_t3:1 A_pv:3
    B_pv2:2 B_pv2:3 B_t3:2 A_yT B_pv3:1 A_out F0_norm B_t3:3 F0_xT B_pv3:2 B_keep F0_h:0 F0_h:1 B_pv3:3
    F0_h:2 B_oT:0 B_oT:1 F0_out B_norm B_out F1_norm B_xT B_small B_imp F1_xT B_gate B_rms F1_h:0 B_nT F1_h:1
    B_q:0 F1_h:2 B_kv:0 B_q:1 B_kv:1 B_krope B_k1r:0 B_k1r:1 F1_out
    B_q:2 B_qT:0 B_kv:2 B_q:3 B_qT:1 B_k1T:0 B_k1T:2 B_kv:3 B_q:4 B_qT:2 B_k1T:1 B_k1T:3 B_q:5 B_qT:3
    B_max1:0 B_q:6 B_k1T:4 B_qT:4 B_k1T:5 B_q:7 B_qT:5 B_max1:1 B_k1T:6 B_k1T:7 B_qT:6 B_max1:2 B_qT:7 B_max1:3 B_m1
""")

_HEADS = dict(A_max=3, B_max1=3, B_max3=3, B_s2=1)
_T = dict(A_t=3, B_t1=3, B_t3=3)
_PV = dict(A_pv=1, B_pv1=1, B_pv2=1, B_pv3=1)
_ACT = "A_xT A_turn A_yT F0_xT B_xT B_small B_imp B_nT B_m1 B_m3 B_kv B_qT B_k1T B_vw B_wT B_sel B_ksT B_p2 B_oT F1_xT"
_DVE = "A_qkv A_m A_out F0_h F0_out B_gate B_q B_w B_pos B_ks B_vs B_out F1_h F1_out"
MISC_BY = {**dict.fromkeys(_ACT.split(), "act"), **dict.fromkeys(_DVE.split(), "dve")}
_NORM = dict(A_norm=1, F0_norm=1, B_norm=1, F1_norm=1)

GIVES = {
    "misc_full": dict.fromkeys(MISC_BY, 1),
    "misc_act": {k: 1 for k, e in MISC_BY.items() if e == "act"},
    "misc_dve": {k: 1 for k, e in MISC_BY.items() if e == "dve"},
    "sq_full": _HEADS, "sq_used": _HEADS, "sk_full": _T, "probs": _T,
    "ob_full": _PV, "ob_used": _PV,
    "var": {**_NORM, "B_rms": 1}, "rstd": {**_NORM, "B_rms": 1}, "xn": _NORM, "nrm": {"B_rms": 1},
    "q_split": {"A_split": 1}, "k_split": {"A_split": 1},
    "x_loaded": {"A_norm": 16}, "x_used": {"A_out": 1}, "kept": {"B_keep": 1}, "stored": {"F1_out": 16},
    "low_left": {"A_m": 1}, "shift_set": {"A_m": 1},
    "tanh": {"F0_h": 1, "F1_h": 1},
    "roped": dict(B_q=1, B_w=1, B_ks=1), "krope": {"B_krope": 1}, "k1_full": {"B_k1r": 1},
    "z_exp": {"B_gate": 1}, "picked": {"B_rank": 1}, "onehot": {"B_pos": 1},
    "p2": {"B_s2": 1}, "summed": {"B_pv2": 1, "B_pv3": 1},
}
CHAINS = {"dve_step": 68, "pool_step": 6}


def begun(sem, step):
    return sum(GIVES[sem].get(name, 0) for name, _ in ORDER[:ORDER.index(step)])


def done(sem, name, n=0):
    return begun(sem, (name, n)) + GIVES[sem][name]


PER_TURN = {sem: sum(gives.get(name, 0) for name, _ in ORDER) for sem, gives in GIVES.items()} | CHAINS
MISC_STEPS = [step for step in ORDER if step[0] in MISC_BY]
PV_STEPS = [step for step in ORDER if step[0] in ("A_pv", "B_pv1", "B_pv3")]
RING = 4
RING_STEPS = [step for step in ORDER if step[0] in ("B_q", "B_w")]


def ring_of(name, n):
    return RING_STEPS.index((name, n)) % RING


AHEAD = {"misc_act": 1, "misc_dve": 1, "stored": 16}


def build(nc, a, out):
    ctx = ExitStack()
    with ctx:
        def sb(name, shape, dt=F32):
            return ctx.enter_context(nc.sbuf_tensor(name, shape, dt))

        def bank(name):
            return ctx.enter_context(nc.psum_tensor(name, [P, 512], F32))

        ident = sb("ident", [P, P])
        ident_h = sb("ident_h", [P, P], BF16)
        mask_q = sb("mask_q", [P, P], BF16)
        mask_k = sb("mask_k", [P, P], BF16)
        before = sb("before", [P, TB, T])
        before_k = sb("before_k", [P, P])
        ones = sb("ones", [P, P])
        mean_of = sb("mean_of", [P, P])
        slots = sb("slots", [P, KEEP])
        cosx = sb("cosx", [P, TB, DB])
        sinx = sb("sinx", [P, TB, ROPE])
        minus_half = sb("minus_half", [P, 4])
        wqkv = sb("wqkv", [P, 3 * C])
        bqkv = sb("bqkv", [P, 3 * C])
        wout = sb("wout", [P, C])
        bout = sb("bout", [P, C])
        wgate = sb("wgate", [P, HID])
        wup = sb("wup", [P, HID])
        wdown = sb("wdown", [P, HC * C])
        wsmall = sb("wsmall", [P, SMALL])
        wimp = sb("wimp", [P, 1])
        wimp_all = sb("wimp_all", [P, P])
        gcol = sb("gcol", [P, 1])
        wq = sb("wq", [QL, H, DB])
        wkv = sb("wkv", [P, 2, H, NOPE])
        wselk = sb("wselk", [P, H, DB])
        wselv = sb("wselv", [P, H, VD])
        wwink = sb("wwink", [P, H, DB])
        wwinv = sb("wwinv", [P, H, VD])
        wproj = sb("wproj", [P, NG, C])
        spare = sb("spare", [P, 4])
        idle = sb("idle", [P, 4])
        idle_p = sb("idle_p", [P, 4])

        x0 = sb("x0", [P, TB, C])
        x1 = sb("x1", [P, TB, C])
        x2 = sb("x2", [P, TB, C])
        x2_old = sb("x2_old", [P, TB, C])
        x3 = sb("x3", [P, TB, C])
        y = sb("y", [P, TB, C])
        stats = sb("stats", [P, TB, 6])
        mv = sb("mv", [P, TB, 2])
        var = sb("var", [P, 4])
        rstd = sb("rstd", [P, 4])
        xn = sb("xn", [P, TB, C])
        xnT = sb("xnT", [P, T])
        xn_b = sb("xn_b", [P, TB, C])
        xnT_b = sb("xnT_b", [P, T])
        qk = sb("qk", [P, TB, 2 * C])
        rest_q = sb("rest_q", [P, C])
        rest_k = sb("rest_k", [P, C])
        qstack = sb("qstack", [P, TB, H, PARTS, DA], BF16)
        kstack = sb("kstack", [P, TB, H, PARTS, DA], BF16)
        va = sb("va", [P, TB, H, DA + 1])
        negs_a = sb("negs_a", [P, TB, P])
        negs_b = sb("negs_b", [P, TB, P])
        negs_high = sb("negs_high", [P, TB, H], BF16)
        shift_a = sb("shift_a", [P, T], BF16)
        qTa = sb("qTa", [SA + 2 * H, H, T], BF16)
        kTa = sb("kTa", [SA + 2 * H, H, T], BF16)
        negm_sel = sb("negm_sel", [P, TB, H])
        probs = sb("probs", [P, 2, 3, 512])
        rden = sb("rden", [P, 2, TB, G])
        ya = sb("ya", [P, TB, C])
        yaT = sb("yaT", [P, T])
        th = sb("th", [P, 2, T])
        hmid = sb("hmid", [P, 2, T])
        hT = sb("hT", [P, HC, T])
        small = sb("small", [P, TB, SMALL])
        imp = sb("imp", [P, T])
        work = sb("work", [P, T])
        icol = sb("icol", [P, TB])
        rank = sb("rank", [P, TB])
        keep = sb("keep", [P, TB])
        pos = sb("pos", [P, TB])
        onehot = sb("onehot", [P, TB, KEEP])
        z = sb("z", [P, 3])
        zmax = sb("zmax", [P, 1])
        zexp = sb("zexp", [P, 3])
        gate = sb("gate", [P, 3])
        square_sum = sb("square_sum", [P, 4])
        nrm = sb("nrm", [P, TB, P])
        nT = sb("nT", [P, T])
        full = sb("full", [P, RING, G, DB])
        k1full = sb("k1full", [P, TB, H, DB])
        ksfull = sb("ksfull", [KEEP, H, DB])
        swapped = sb("swapped", [P, 2, G, ROPE])
        kr = sb("kr", [P, TB, ROPE])
        kr_swapped = sb("kr_swapped", [P, TB, ROPE])
        qT = sb("qT", [P, H, T])
        k1T = sb("k1T", [P, H, T])
        kwT = sb("kwT", [P, H, T])
        ksT = sb("ksT", [DB, H, KEEP])
        xselT = sb("xselT", [P, KEEP])
        v1 = sb("v1", [P, TB, H, VD + 1])
        vw = sb("vw", [P, TB, H, VD + 1])
        vsel = sb("vsel", [P, NG, G, VD + 1])
        staged = k1full[:, :, :, :].rearrange("p n h d -> p (n h d)")[:, 0:2 * P + 2 * H]
        heads_of_rows = staged[:, 2 * P:].rearrange("p (u h) -> p u h", u=2)
        w_raw = probs[:, 0, 0, 0:HID].rearrange("p (n c) -> p n c", c=P)
        w_int = probs[:, 0, 1, 0:HID].rearrange("p (n c) -> p n c", c=P).bitcast(I32)
        part = k1full[:, :, :, :].rearrange("p n h d -> p (n h d)")\
            .rearrange("p (a n h d) -> p a n h d", a=3, n=TB, h=H)
        oT = sb("oT", [P, NG, T])
        p2T = oT

        misc = [bank("misc0"), bank("misc1")]
        sq = [bank("sq0"), bank("sq1")]
        sk = [bank("sk0"), bank("sk1")]
        ob = [bank("ob0"), bank("ob1")]

        s = {name: ctx.enter_context(nc.semaphore(f"s_{name}"))
             for name in (*PER_TURN, "c_loaded", "w_turned", "w_copied", "set_dve", "set_pool")}

        def at(i, sem, n):
            return s[sem], i * PER_TURN[sem] + n + AHEAD.get(sem, 0)

        def halves(ap):
            return ap.bitcast(BF16)[:, 1::2]

        USES = {
            "A": dict(t="A_t", k=KA, kt=SA + 2 * H, q=qTa, key=kTa, v=va, d=DA, scale=DA ** -0.5, view=lambda ap: ap),
            "1": dict(t="B_t1", k=DB, kt=P, q=qT, key=k1T, v=v1, d=VD, scale=DB ** -0.5, view=halves),
            "3": dict(t="B_t3", k=DB, kt=P, q=qT, key=kwT, v=vw, d=VD, scale=DB ** -0.5, view=halves),
        }

        def misc_of(name, n=0):
            return misc[begun("misc_full", (name, n)) % 2]

        def emptied(name, n=0):
            return f"misc_{MISC_BY[name]}", done(f"misc_{MISC_BY[name]}", name, n)

        def bank_heads(g, t):
            return (range(G * g, G * g + G), P) if t == 0 else (range(G * g + 2 * t - 2, G * g + 2 * t), T)

        def half_of_probs(t_name, g):
            return begun("sk_full", (t_name, g)) // 3 % 2

        TURNED = [
            ("L0_attn_a_W_attn", False, wqkv, HC), ("L0_attn_a_W_proj", False, wout, 1),
            ("L0_ffn_w_gate", True, wgate, HC), ("L0_ffn_w_up", True, wup, HC), ("L0_ffn_w_down", True, wdown, HC),
        ]
        heads = "p (h d) -> p h d"
        LOADED = [
            (ident[:, :], a["c_ident"]), (staged[:, 0:2 * P], a["c_masks"]), (staged[:, 2 * P:], a["c_heads"]),
            (before[:, :, :], a["c_before"]),
            (before_k[:, :], a["c_before_k"]), (slots[:, :], a["c_slots"]), (cosx[:, :, :], a["c_cos"]),
            (sinx[:, :, :], a["c_sin"]),
            (bqkv[:, :], a["L0_attn_a_b_attn"].partition_broadcast(P)),
            (bout[:, :], a["L0_attn_a_b_proj"].partition_broadcast(P)),
            (wsmall[:, 0:QL], a["L0_attn_b_w_cq"]), (wsmall[:, QL:KR], a["L0_attn_b_w_ckv"]),
            (wsmall[:, KR:GT], a["L0_attn_b_w_krope"]), (wsmall[:, GT:SMALL], a["L0_attn_b_w_gate"]),
            (wimp[:, :], a["L0_attn_b_w_imp"]),
            (gcol[0:QL, :], a["L0_attn_b_g_qnorm"].rearrange("(p a) -> p a", a=1)),
            (gcol[QL:P, :], a["L0_attn_b_g_kvnorm"].rearrange("(p a) -> p a", a=1)),
            (wq[:, :, 0:NOPE], a["L0_attn_b_w_dq_nope"].rearrange(heads, h=H)),
            (wq[:, :, NOPE:DB], a["L0_attn_b_w_dq_rope"].rearrange(heads, h=H)),
            (wkv[QL:P, 0, :, :], a["L0_attn_b_w_dk_nope"].rearrange(heads, h=H)),
            (wkv[QL:P, 1, :, :], a["L0_attn_b_w_dv"].rearrange(heads, h=H)),
            (wselk[:, :, :], a["L0_attn_b_w_selk"].rearrange(heads, h=H)),
            (wselv[:, :, :], a["L0_attn_b_w_selv"].rearrange(heads, h=H)),
            (wwink[:, :, :], a["L0_attn_b_w_wink"].rearrange(heads, h=H)),
            (wwinv[:, :, :], a["L0_attn_b_w_winv"].rearrange(heads, h=H)),
            (wproj[:, :, :], a["L0_attn_b_w_proj"].rearrange("(n p) c -> p n c", p=P)),
        ]

        def of_tokens(ap):
            return ap.rearrange("(n p) c -> p n c", p=P)

        block = ctx.enter_context(nc.Block())

        @block.sync
        def _(sp):
            for dst, src in LOADED:
                sp.dma_start(dst, src).then_inc(s["c_loaded"], 16)
            for n, (name, integer, _, k) in enumerate(TURNED):
                if n:
                    sp.wait_ge(s["w_turned"], n)
                src = a[name]
                src = src.rearrange("p (n c) -> p n c", c=P) if src.shape[0] == P else of_tokens(src)
                sp.dma_start((w_int if integer else w_raw)[:, 0:k, :], src).then_inc(s["c_loaded"], 16)

            def load(n):
                sp.dma_start(x0[:, :, :], of_tokens(a["L0_attn_a_x"][n, :, :])).then_inc(s["x_loaded"], 16)

            def store(i):
                sp.wait_ge(*at(i, *emptied("F1_out")))
                sp.dma_start(of_tokens(out[i - 1, :, :]), y[:, :, :]).then_inc(s["stored"], 16)

            load(0)
            sp.wait_ge(*at(0, "x_used", 1))
            load(1)
            with sp.Fori(1, NSEQ - 1) as i:
                sp.wait_ge(*at(i, "x_used", 1))
                load(i + 1)
                store(i)
            sp.wait_ge(*at(NSEQ - 1, "x_used", 1))
            load(NSEQ - 1)
            store(NSEQ - 1)
            store(NSEQ)
            sp.wait_ge(*at(TURNS, "stored", 0))

        @block.tensor
        def _(pe):
            for n, (name, integer, dst, k) in enumerate(TURNED):
                pe.wait_ge(s["c_loaded"], 16 * (len(LOADED) + n + 1))
                if integer:
                    pe.wait_ge(s["set_dve"], n - 1)
                if n:
                    pe.wait_ge(s["w_copied"], n)
                for c in range(k):
                    mm = pe.transpose(misc[0][:, c * P:(c + 1) * P], w_raw[:, c, :], ident[:, :])
                mm.then_inc(s["w_turned"], 1)
            pe.wait_ge(s["w_copied"], len(TURNED))
            pe.wait_ge(s["set_dve"], 4)
            pe.wait_ge(s["set_pool"], 1)

            with pe.Fori(0, TURNS) as i:
                def fill(name, n=0):
                    m = begun("misc_full", (name, n))
                    if m >= 2:
                        pe.wait_ge(*at(i, *emptied(*MISC_STEPS[m - 2])))
                    else:
                        pe.wait_ge(*at(i, "misc_act", 0))
                        pe.wait_ge(*at(i, "misc_dve", 0))
                    return misc[m % 2]

                def filled(mm):
                    mm.then_inc(s["misc_full"], 1)

                def taken(name, n=0):
                    pe.wait_ge(*at(i, *emptied(name, n)))

                def carry_waits():
                    pe.ldweights(ident_h[:, :], tile_position=(0, 0))

                def turn_tokens(name, src, sem=None, count=0):
                    b = fill(name)
                    if sem:
                        pe.wait_ge(*at(i, sem, count))
                    for tb in range(TB):
                        mm = pe.transpose(b[:, tb * P:(tb + 1) * P], src[:, tb, :], ident[:, :])
                    filled(mm)

                def max_scores(name, g, use):
                    k, view = use["k"], use["view"]
                    for t in range(3):
                        n = begun("sq_full", (name, g)) + t
                        if n >= 2:
                            pe.wait_ge(*at(i, "sq_used", n - 1))
                        b = sq[n % 2]
                        (hs, w), qb = bank_heads(g, t), int(t > 0)
                        for j, h in enumerate(hs):
                            pe.matmul(b[:, j * w:(j + 1) * w], view(use["q"][0:k, h, qb * P:(qb + 1) * P]),
                                      view(use["key"][0:k, h, 0:w]), start=(j == 0), stop=False,
                                      skip_group_check=True)
                        diagonal = b[:, :].rearrange("p (j w) -> p j w", w=w)[:, :, w - P:w]
                        pe.matmul(diagonal, ident_h[:, :], mask_q[:, :].unsqueeze(1).broadcast_to((P, len(hs), P)),
                                  start=False, stop=True, skip_group_check=True).then_inc(s["sq_full"], 1)


                def t_scores(g, use):
                    k = use["kt"]
                    for t in range(3):
                        n = begun("sk_full", (use["t"], g)) + t
                        if n >= 2:
                            pe.wait_ge(*at(i, "probs", n - 1))
                        b = sk[n % 2]
                        hs, w = bank_heads(g, t)
                        kb = int(t == 0)
                        for j, h in enumerate(hs):
                            cols = b[:, j * w:(j + 1) * w]
                            pe.matmul(cols, use["key"][0:k, h, kb * P:(kb + 1) * P], use["q"][0:k, h, T - w:T],
                                      start=(j == 0), stop=False, skip_group_check=True)
                        diagonal = b[:, :].rearrange("p (j w) -> p j w", w=w)[:, :, 0:P]
                        pe.matmul(diagonal, ident_h[:, :], mask_k[:, :].unsqueeze(1).broadcast_to((P, len(hs), P)),
                                  start=False, stop=True, skip_group_check=True).then_inc(s["sk_full"], 1)

                def pv_bank(name, g):
                    n = begun("ob_full", (name, g))
                    if n >= 2:
                        pe.wait_ge(*at(i, "ob_used", n - 1))
                    return ob[n % 2]

                def pv(name, g, use):
                    w = use["d"] + 1
                    pe.wait_ge(*at(i, "probs", done("probs", use["t"], g)))
                    b = pv_bank(name, g)
                    pr = probs[:, half_of_probs(use["t"], g), :, :]
                    for j in range(G):
                        h = G * g + j
                        low = pr[:, 1 + j // 2, (j % 2) * T:(j % 2 + 1) * T]
                        for qb in range(TB):
                            o = b[:, (qb * G + j) * w:(qb * G + j + 1) * w]
                            mm = pe.matmul(o, low[:, qb * P:(qb + 1) * P], use["v"][:, 0, h, :],
                                           start=True, stop=(qb == 0))
                            if qb:
                                mm = pe.matmul(o, pr[:, 0, j * P:(j + 1) * P], use["v"][:, 1, h, :],
                                               start=False, stop=True)
                    mm.then_inc(s["ob_full"], 1)

                def project_heads(name, n, g, lhsT, w, rows):
                    b = fill(name, n)
                    filled(pe.matmul(b[0:rows, 0:G * DB], lhsT, w[:, G * g:G * g + G, :], start=True, stop=True))

                def turn_heads(name, n, src):
                    for j in range(G):
                        mm = pe.transpose(misc_of(name, n)[0:DB, j * P:(j + 1) * P], src(j), ident[:, :])
                    filled(mm)

                def turn_roped(name, n, source):
                    fill(name, n)
                    pe.wait_ge(*at(i, "roped", done("roped", source, n)))
                    turn_heads(name, n, lambda j: full[:, ring_of(source, n), j, :])

                def hidden(f, c):
                    b = fill(f"F{f}_h", c)
                    if c == 0:
                        taken(f"F{f}_xT")
                    pe.matmul(b[:, 0:T], wgate[:, c * P:(c + 1) * P], xnT[:, :], start=True, stop=True)
                    filled(pe.matmul(b[:, T:2 * T], wup[:, c * P:(c + 1) * P], xnT[:, :], start=True, stop=True))

                def ffn_out(f):
                    b = fill(f"F{f}_out")
                    taken(f"F{f}_h", HC - 1)
                    for tb in range(TB):
                        for c in range(HC):
                            mm = pe.matmul(b[:, tb * P:(tb + 1) * P], hT[:, c, tb * P:(tb + 1) * P],
                                           wdown[:, c * C:(c + 1) * C], start=(c == 0), stop=(c == HC - 1))
                    filled(mm)

                def a_qkv(tb):
                    b = fill("A_qkv", tb)
                    taken("A_xT")
                    filled(pe.matmul(b[:, 0:3 * C], xnT[:, tb * P:(tb + 1) * P], wqkv[:, :], start=True, stop=True))

                def a_turn(n):
                    tb, is_k, half = n // 4, n // 2 % 2, n % 2
                    b = fill("A_turn", n)[0:KA, :].bitcast(BF16)
                    pe.wait_ge(*at(i, "k_split" if is_k else "q_split", tb + 1))
                    carry_waits()
                    stack = kstack if is_k else qstack
                    for j in range(H // 2):
                        mm = pe.transpose(b[:, j * P:(j + 1) * P],
                                          stack[:, tb, half * 8 + j, :, :].rearrange("p s d -> p (s d)"), ident_h[:, :])
                    filled(mm)

                def a_max(g):
                    if g == 0:
                        taken("A_turn", 7)
                    max_scores("A_max", g, USES["A"])

                def a_t(g):
                    if g == 0:
                        pe.wait_ge(*at(i, "shift_set", 1))
                    t_scores(g, USES["A"])

                def a_out(_):
                    b = fill("A_out")
                    taken("A_yT")
                    for tb in range(TB):
                        mm = pe.matmul(b[:, tb * P:(tb + 1) * P], yaT[:, tb * P:(tb + 1) * P], wout[:, :],
                                       start=True, stop=True)
                    filled(mm)

                def b_small(_):
                    b = fill("B_small")
                    taken("B_xT")
                    for tb in range(TB):
                        mm = pe.matmul(b[:, tb * SMALL:(tb + 1) * SMALL], xnT_b[:, tb * P:(tb + 1) * P], wsmall[:, :],
                                       start=True, stop=True)
                    filled(mm)

                def b_imp(_):
                    b = fill("B_imp")
                    filled(pe.matmul(b[:, 0:T], wimp_all[:, :], xnT_b[:, :], start=True, stop=True))

                def b_gate(_):
                    b = fill("B_gate")
                    taken("B_small")
                    for tb in range(TB):
                        mm = pe.matmul(b[:, 0:3], mean_of[:, :], small[:, tb, GT:SMALL], start=(tb == 0), stop=(tb == 1))
                    filled(mm)

                def b_q(n):
                    g, tb = n // 2, n % 2
                    if n == 0:
                        taken("B_nT")
                    project_heads("B_q", n, g, nT[0:QL, tb * P:(tb + 1) * P], wq, P)

                def b_kv(n):
                    tb, is_v = n // 2, n % 2
                    b = fill("B_kv", n)
                    filled(pe.matmul(b[:, :], nT[QL:P, tb * P:(tb + 1) * P],
                                     wkv[QL:P, is_v, :, :].rearrange("p h d -> p (h d)"), start=True, stop=True))

                def b_k1T(n):
                    g, tb = n // 2, n % 2
                    fill("B_k1T", n)
                    taken("B_kv", 2 * tb)
                    pe.wait_ge(*at(i, "k1_full", tb + 1))
                    turn_heads("B_k1T", n, lambda j: k1full[:, tb, G * g + j, :])

                def b_w(n):
                    g, tb = n // 2, n % 2
                    project_heads("B_w", n, g, xnT_b[:, tb * P:(tb + 1) * P], wwink, P)

                def b_vw(tb):
                    b = fill("B_vw", tb)
                    filled(pe.matmul(b[:, :], xnT_b[:, tb * P:(tb + 1) * P], wwinv[:, :, :].rearrange("p h d -> p (h d)"),
                                     start=True, stop=True))

                def b_pos(_):
                    b = fill("B_pos")
                    pe.wait_ge(*at(i, "picked", 1))
                    pe.matmul(b[:, 0:1], before_k[:, :], keep[:, 0:1], start=True, stop=True)
                    pe.matmul(b[:, 1:2], ones[:, :], keep[:, 0:1], start=True, stop=False)
                    filled(pe.matmul(b[:, 1:2], before_k[:, :], keep[:, 1:2], start=False, stop=True))

                def b_sel(_):
                    b = fill("B_sel")
                    pe.wait_ge(*at(i, "onehot", 1))
                    for tb in range(TB):
                        mm = pe.matmul(b[:, 0:KEEP], xn_b[:, tb, :], onehot[:, tb, :], start=(tb == 0), stop=(tb == 1))
                    filled(mm)

                def b_ks(g):
                    if g == 0:
                        taken("B_sel")
                    project_heads("B_ks", g, g, xselT[:, :], wselk, KEEP)

                def b_vs(_):
                    b = fill("B_vs")
                    for j in range(G):
                        mm = pe.matmul(b[KEEP * j:KEEP * (j + 1), 0:NG * VD], xselT[:, :], wselv[:, j::G, :],
                                       start=True, stop=True)
                    filled(mm)

                def b_ksT(_):
                    b = fill("B_ksT")
                    pe.wait_ge(*at(i, "roped", done("roped", "B_ks", NG - 1)))
                    carry_waits()
                    for h in range(H):
                        mm = pe.transpose(b[0:DB, h * KEEP:(h + 1) * KEEP], ksfull[:, h, :], ident[0:KEEP, 0:KEEP])
                    filled(mm)

                def b_s2(tb):
                    if tb == 0:
                        taken("B_ksT")
                    n = begun("sq_full", ("B_s2", tb))
                    pe.wait_ge(*at(i, "sq_used", n - 1))
                    for h in range(H):
                        mm = pe.matmul(sq[n % 2][:, h * KEEP:(h + 1) * KEEP], qT[0:DB, h, tb * P:(tb + 1) * P],
                                       ksT[:, h, :], start=True, stop=True)
                    mm.then_inc(s["sq_full"], 1)

                def b_p2(tb):
                    b = fill("B_p2", tb)
                    pe.wait_ge(*at(i, "p2", tb + 1))
                    for g in range(NG):
                        mm = pe.transpose(b[:, g * P:(g + 1) * P],
                                          part[:, 1, tb, G * g:G * g + G, :].rearrange("p h d -> p (h d)"), ident[:, :])
                    filled(mm)

                def b_pv2(g):
                    if g == 0:
                        taken("B_p2", 1)
                        taken("B_vs")
                    b = pv_bank("B_pv2", g)
                    w = G * (VD + 1)
                    for tb in range(TB):
                        mm = pe.matmul(b[:, tb * w:(tb + 1) * w], p2T[:, g, tb * P:(tb + 1) * P],
                                       vsel[:, g, :, :].rearrange("p j d -> p (j d)"), start=True, stop=True)
                    mm.then_inc(s["ob_full"], 1)

                def b_max3(g):
                    taken("B_wT", 2 * g + 1)
                    max_scores("B_max3", g, USES["3"])

                def b_max1(g):
                    taken("B_qT", 2 * g + 1)
                    taken("B_k1T", 2 * g + 1)
                    max_scores("B_max1", g, USES["1"])

                def b_t3(g):
                    if g == 0:
                        taken("B_m3")
                    t_scores(g, USES["3"])

                def b_t1(g):
                    if g == 0:
                        pe.wait_ge(*at(i, "misc_act", 0))
                    t_scores(g, USES["1"])

                def b_pv3(g):
                    if g == 0:
                        taken("B_vw", 1)
                    pv("B_pv3", g, USES["3"])

                def b_oT(tb):
                    b = fill("B_oT", tb)
                    if tb == 0:
                        pe.wait_ge(*at(i, "summed", PER_TURN["summed"]))
                    for n in range(NG):
                        mm = pe.transpose(b[:, n * P:(n + 1) * P],
                                          part[:, 0, tb, G * n:G * n + G, :].rearrange("p h d -> p (h d)"), ident[:, :])
                    filled(mm)

                def b_out(_):
                    b = fill("B_out")
                    taken("B_oT", 1)
                    for tb in range(TB):
                        for n in range(NG):
                            mm = pe.matmul(b[:, tb * P:(tb + 1) * P], oT[:, n, tb * P:(tb + 1) * P], wproj[:, n, :],
                                           start=(n == 0), stop=(n == NG - 1))
                    filled(mm)

                part_of = dict(
                    A_xT=lambda _: turn_tokens("A_xT", xn, "xn", done("xn", "A_norm")),
                    A_qkv=a_qkv, A_turn=a_turn, A_max=a_max,
                    A_m=lambda _: turn_tokens("A_m", negs_a, "low_left", 1),
                    A_t=a_t, A_pv=lambda g: pv("A_pv", g, USES["A"]),
                    A_yT=lambda _: turn_tokens("A_yT", ya, "ob_used", done("ob_used", "A_pv", NG - 1)),
                    A_out=a_out,
                    F0_xT=lambda _: turn_tokens("F0_xT", xn, "xn", done("xn", "F0_norm")),
                    F0_h=lambda c: hidden(0, c), F0_out=lambda _: ffn_out(0),
                    B_xT=lambda _: turn_tokens("B_xT", xn_b, "xn", done("xn", "B_norm")),
                    B_small=b_small, B_imp=b_imp, B_gate=b_gate,
                    B_nT=lambda _: turn_tokens("B_nT", nrm, "nrm", 1),
                    B_q=b_q, B_kv=b_kv, B_qT=lambda n: turn_roped("B_qT", n, "B_q"), B_k1T=b_k1T,
                    B_w=b_w, B_vw=b_vw, B_wT=lambda n: turn_roped("B_wT", n, "B_w"),
                    B_max1=b_max1, B_m1=lambda _: turn_tokens("B_m1", negs_b, "sq_used", done("sq_used", "B_max1", NG - 1)),
                    B_pos=b_pos, B_sel=b_sel, B_ks=b_ks, B_vs=b_vs, B_ksT=b_ksT, B_s2=b_s2, B_p2=b_p2, B_pv2=b_pv2,
                    B_max3=b_max3, B_m3=lambda _: turn_tokens("B_m3", negs_b, "sq_used", done("sq_used", "B_max3", NG - 1)),
                    B_t1=b_t1, B_pv1=lambda g: pv("B_pv1", g, USES["1"]), B_t3=b_t3, B_pv3=b_pv3,
                    B_oT=b_oT, B_out=b_out,
                    F1_xT=lambda _: turn_tokens("F1_xT", xn, "xn", done("xn", "F1_norm")),
                    F1_h=lambda c: hidden(1, c), F1_out=lambda _: ffn_out(1),
                )
                for name, n in ORDER:
                    if name in part_of:
                        part_of[name](n)

        @block.scalar
        def _(act):
            for n, (name, integer, dst, k) in enumerate(TURNED):
                act.wait_ge(s["w_turned"], n + 1)
                act.activation(dst[:, :], misc[0][:, 0:k * P], ACT.Copy).then_inc(s["w_copied"], 1)

            act.activation(idle[:, 0:1], ident[:, 0:1], ACT.Copy).then_inc(s["misc_act"], AHEAD["misc_act"])

            with act.Fori(0, TURNS) as i:
                def empty(name, n, dst, src):
                    act.wait_ge(*at(i, "misc_full", done("misc_full", name, n)))
                    act.activation(dst, src(misc_of(name, n)), ACT.Copy).then_inc(s["misc_act"], 1)

                def tokens_out(name, dst):
                    empty(name, 0, dst[:, :], lambda b: b[:, 0:T])

                def heads_out(name, n, dst):
                    g, tb = n // 2, n % 2
                    empty(name, n, dst[0:DB, G * g:G * g + G, tb * P:(tb + 1) * P],
                          lambda b: b[0:DB, :].rearrange("p (j t) -> p j t", t=P))

                def shifts_out(name):
                    empty(name, 0, qT[SB:P, :, :], lambda b: b[SB:P, 0:T].unsqueeze(1).broadcast_to((P - SB, H, T)))

                def values_out(name, n, dst):
                    empty(name, n, dst, lambda b: b[:, :].rearrange("p (h d) -> p h d", h=H))

                def exps(g, use):
                    first = begun("sk_full", (use["t"], g))
                    for t in range(3):
                        act.wait_ge(*at(i, "sk_full", first + t + 1))
                        if t == 0 and first >= 6:
                            act.wait_ge(*at(i, "ob_full", done("ob_full", *PV_STEPS[first // 3 - 2])))
                        act.activation(probs[:, half_of_probs(use["t"], g), t, :], sk[(first + t) % 2][:, :], ACT.Exp,
                                       scale=use["scale"]).then_inc(s["probs"], 1)

                def hidden(f, c):
                    act.wait_ge(*at(i, "misc_full", done("misc_full", f"F{f}_h", c)))
                    act.activation(th[:, c % 2, :], misc_of(f"F{f}_h", c)[:, 0:T], ACT.Tanh, scale=0.5)\
                        .then_inc(s["tanh"], 1)

                def a_turn(n):
                    tb, is_k, half = n // 4, n // 2 % 2, n % 2
                    empty("A_turn", n, (kTa if is_k else qTa)[0:KA, half * 8:half * 8 + 8, tb * P:(tb + 1) * P],
                          lambda b: b[0:KA, :].bitcast(BF16).rearrange("p (j t) -> p j t", t=P))

                def b_keep(_):
                    act.wait_ge(*at(i, "misc_dve", 0))
                    act.activation(x2_old[:, :, :], x2[:, :, :], ACT.Copy).then_inc(s["kept"], 1)

                def b_gate(_):
                    act.wait_ge(*at(i, *emptied("B_gate")))
                    act.activation(zexp[:, :], z[:, :], ACT.Exp).then_inc(s["z_exp"], 1)

                def b_s2(tb):
                    act.wait_ge(*at(i, "sq_used", done("sq_used", "B_s2", tb)))
                    act.activation(part[:, 1, tb, :, :], part[:, 1, tb, :, :], ACT.Exp, scale=DB ** -0.5)\
                        .then_inc(s["p2"], 1)

                def b_kv(n):
                    tb, is_v = n // 2, n % 2
                    values_out("B_kv", n, v1[:, tb, :, 0:VD] if is_v else k1full[:, tb, :, 0:NOPE])

                def four_out(name, tb, dst):
                    empty(name, tb, dst[:, :, tb * P:(tb + 1) * P], lambda b: b[:, :].rearrange("p (n t) -> p n t", t=P))

                part_of = dict(
                    A_xT=lambda _: tokens_out("A_xT", xnT), A_turn=a_turn, A_t=lambda g: exps(g, USES["A"]),
                    A_yT=lambda _: tokens_out("A_yT", yaT),
                    F0_xT=lambda _: tokens_out("F0_xT", xnT), F0_h=lambda c: hidden(0, c),
                    F1_xT=lambda _: tokens_out("F1_xT", xnT), F1_h=lambda c: hidden(1, c),
                    B_keep=b_keep, B_xT=lambda _: tokens_out("B_xT", xnT_b),
                    B_small=lambda _: empty("B_small", 0, small[:, :, :].rearrange("p n c -> p (n c)"),
                                            lambda b: b[:, 0:TB * SMALL]),
                    B_imp=lambda _: tokens_out("B_imp", imp), B_gate=b_gate, B_nT=lambda _: tokens_out("B_nT", nT),
                    B_kv=b_kv, B_qT=lambda n: heads_out("B_qT", n, qT), B_k1T=lambda n: heads_out("B_k1T", n, k1T),
                    B_vw=lambda tb: values_out("B_vw", tb, vw[:, tb, :, 0:VD]),
                    B_wT=lambda n: heads_out("B_wT", n, kwT),
                    B_sel=lambda _: empty("B_sel", 0, xselT[:, :], lambda b: b[:, 0:KEEP]),
                    B_ksT=lambda _: empty("B_ksT", 0, ksT[:, :, :].rearrange("p h t -> p (h t)"), lambda b: b[0:DB, :]),
                    B_m1=lambda _: shifts_out("B_m1"), B_m3=lambda _: shifts_out("B_m3"),
                    B_s2=b_s2, B_p2=lambda tb: four_out("B_p2", tb, p2T),
                    B_t1=lambda g: exps(g, USES["1"]), B_t3=lambda g: exps(g, USES["3"]),
                    B_oT=lambda tb: four_out("B_oT", tb, oT),
                )
                for name, n in ORDER:
                    if name in part_of:
                        part_of[name](n)

        @block.vector
        def _(dve):
            for n, (name, integer, _, k) in enumerate(TURNED):
                if integer:
                    dve.wait_ge(s["c_loaded"], 16 * (len(LOADED) + n + 1))
                    dve.tensor_scalar(w_raw[:, :, :], w_int[:, :, :], FFN_SCALE, None, ALU.mult)\
                        .then_inc(s["set_dve"], 1)
            dve.tensor_copy(ident_h[:, :], ident[:, :])
            dve.tensor_copy(mask_q[:, :], staged[:, 0:P])
            dve.tensor_copy(mask_k[:, :], staged[:, P:2 * P])
            for keys, rows, use in ((kTa, slice(SA, SA + 2 * H), 0), (k1T, slice(SB, P), 0), (kwT, slice(SB, P), 1)):
                dve.tensor_copy(keys[rows, :, :], heads_of_rows[rows, use, :].unsqueeze(2).broadcast_to((2 * H, H, T)))
            dve.tensor_scalar(wq[:, :, :], wq[:, :, :], gcol[0:QL, 0:1], None, ALU.mult)
            dve.tensor_scalar(wkv[QL:P, :, :, :], wkv[QL:P, :, :, :], gcol[QL:P, 0:1], None, ALU.mult)
            dve.tensor_scalar(wsmall[:, KR:GT], wsmall[:, KR:GT], 1.0 / H, None, ALU.mult)
            dve.wait_ge(s["set_pool"], 1)
            for j in range(G):
                dve.memset(vsel[KEEP * j:KEEP * (j + 1), :, j, VD:VD + 1], 1.0)
            for v in (va, v1, vw):
                d = v.shape[3] - 1
                dve.memset(v[:, :, :, d:d + 1], 1.0)
            dve.memset(ones[:, :], 1.0)
            dve.memset(mean_of[:, :], 1.0 / T)
            dve.memset(wimp_all[:, :], 1.0).then_inc(s["dve_step"], 1)
            dve.wait_ge(s["dve_step"], 1)
            dve.memset(k1T[0:DB, :, :], 0.0)
            for data in (qT, x2, xn_b, negs_a, negs_b):
                dve.memset(data[:, :, :], 0.0)
            dve.memset(qTa[KA - 16:SA, :, :], 0.0)
            dve.memset(kTa[KA - 16:SA, :, :], 0.0)
            for data in (xnT_b, imp, gate):
                dve.memset(data[:, :], 0.0)
            dve.memset(v1[:, :, :, 0:VD], 0.0)
            dve.memset(spare[:, 0:1], 0.0).then_inc(s["stored"], 2 * AHEAD["stored"])
            dve.memset(spare[:, 2:3], 0.0).then_inc(s["misc_dve"], AHEAD["misc_dve"])
            dve.tensor_scalar(wimp_all[:, :], wimp_all[:, :], wimp[:, 0:1], None, ALU.mult).then_inc(s["set_dve"], 1)

            with dve.Fori(0, TURNS) as i:
                chain = [0]

                def then(ins):
                    chain[0] += 1
                    ins.then_inc(s["dve_step"], 1)
                    dve.wait_ge(s["dve_step"], i * PER_TURN["dve_step"] + chain[0] + 1)

                def full_bank(name, n=0):
                    dve.wait_ge(*at(i, "misc_full", done("misc_full", name, n)))
                    return misc_of(name, n)

                def empties(ins):
                    ins.then_inc(s["misc_dve"], 1)

                def written(name, n=0):
                    dve.wait_ge(*at(i, *emptied(name, n)))

                def norm(name, x, dst):
                    for tb in range(TB):
                        ins = dve.bn_stats(stats[:, tb, :], x[:, tb, :])
                    then(ins)
                    dve.memset(spare[:, 1:2], 0.0)
                    for tb in range(TB):
                        ins = dve.bn_aggr(mv[:, tb, :], stats[:, tb, :])
                    then(ins)
                    dve.tensor_scalar(var[:, 0:TB], mv[:, :, 1], LN_EPS, None, ALU.add).then_inc(s["var"], 1)
                    dve.wait_ge(*at(i, "rstd", done("rstd", name)))
                    for tb in range(TB):
                        ins = dve.tensor_scalar(dst[:, tb, :], x[:, tb, :], mv[:, tb, 0:1], rstd[:, tb:tb + 1],
                                                ALU.subtract, ALU.mult)
                    ins.then_inc(s["xn"], 1)

                def maxima(name, g, dst, first):
                    for t in range(3):
                        n = begun("sq_full", (name, g)) + t
                        dve.wait_ge(*at(i, "sq_full", n + 1))
                        hs, w = bank_heads(g, t)
                        dve.tensor_reduce(dst[:, int(t > 0), first + hs[0]:first + hs[-1] + 1],
                                          sq[n % 2][:, :].rearrange("p (j w) -> p j w", w=w), AX_X, ALU.max,
                                          negate=True).then_inc(s["sq_used"], 1)

                def a_m(_):
                    negs = negs_a[:, :, SA:SA + H]
                    then(dve.tensor_copy(negs_high[:, :, :], negs))
                    dve.tensor_tensor(negs_a[:, :, SA + H:SA + 2 * H], negs, negs_high[:, :, :], ALU.subtract)\
                        .then_inc(s["low_left"], 1)
                    b = full_bank("A_m")
                    rows = slice(SA, SA + 2 * H)
                    empties(dve.tensor_copy(shift_a[rows, :], b[rows, 0:T]))
                    written("A_m")
                    dve.tensor_copy(qTa[rows, :, :], shift_a[rows, :].unsqueeze(1).broadcast_to((2 * H, H, T)))\
                        .then_inc(s["shift_set"], 1)

                def scale_out(name, g, d, dst, by_gate):
                    n = begun("ob_full", (name, g))
                    dve.wait_ge(*at(i, "ob_full", n + 1))
                    rd = rden[:, n % 2, :, :]
                    o = ob[n % 2][:, 0:TB * G * (d + 1)].rearrange("p (n j d) -> p n j d", n=TB, j=G)
                    then(dve.reciprocal(rd, o[:, :, :, d]))
                    if by_gate is not None:
                        then(dve.tensor_scalar(rd, rd, by_gate, None, ALU.mult))
                    dve.tensor_tensor(dst, o[:, :, :, 0:d], rd.unsqueeze(3).broadcast_to((P, TB, G, d)),
                                      ALU.mult).then_inc(s["ob_used"], 1)

                def branch_out(name, g, a_part):
                    scale_out(name, g, VD, part[:, a_part, :, G * g:G * g + G, :], gate[:, a_part:a_part + 1])

                def rope(name, n, dst, tb, rows):
                    b = full_bank(name, n)
                    v = b[0:rows, 0:G * DB].rearrange("p (j d) -> p j d", j=G)
                    r = begun("roped", (name, n))
                    if r >= 2:
                        dve.wait_ge(*at(i, "roped", r - 1))
                    dve.tensor_tensor(dst, v, cosx[0:rows, tb, :].unsqueeze(1).broadcast_to((rows, G, DB)), ALU.mult)
                    halves_swapped = v[:, :, NOPE:DB].rearrange("p j (e d) -> p j e d", e=2)[:, :, ::-1, :]
                    sines = sinx[0:rows, tb, :].rearrange("p (e d) -> p e d", e=2).unsqueeze(1)
                    empties(dve.tensor_tensor(
                        swapped[0:rows, r % 2, :, :].rearrange("p j (e d) -> p j e d", e=2), halves_swapped,
                        sines.broadcast_to((rows, G, 2, ROPE // 2)), ALU.mult))

                def rope_ring(name, n):
                    before_it = RING_STEPS.index((name, n)) - RING
                    if before_it >= 0:
                        source, m = RING_STEPS[before_it]
                        dve.wait_ge(*at(i, "misc_full", done("misc_full", source + "T", m)))
                    rope(name, n, full[:, ring_of(name, n), :, :], n % 2, P)

                def hidden(f, c):
                    b = full_bank(f"F{f}_h", c)
                    dve.wait_ge(*at(i, "tanh", done("tanh", f"F{f}_h", c)))
                    then(dve.scalar_tensor_tensor(out=hmid[:, c % 2, :], in0=th[:, c % 2, :], scalar=1.0,
                                                  in1=b[:, 0:T], op0=ALU.add, op1=ALU.mult))
                    empties(dve.scalar_tensor_tensor(out=hT[:, c, :], in0=hmid[:, c % 2, :], scalar=0.5,
                                                     in1=b[:, T:2 * T], op0=ALU.mult, op1=ALU.mult))

                def add_out(name, x, dst):
                    b = full_bank(name)
                    empties(dve.tensor_tensor(dst[:, :, :], b[:, 0:T].rearrange("p (n c) -> p n c", c=C), x[:, :, :],
                                              ALU.add))
                    written(name)

                def a_norm(_):
                    dve.wait_ge(*at(i, "x_loaded", 16))
                    norm("A_norm", x0, xn)

                def a_qkv(tb):
                    b = full_bank("A_qkv", tb)
                    dve.tensor_tensor(va[:, tb, :, 0:DA], b[:, 2 * C:3 * C].rearrange("p (h d) -> p h d", h=H),
                                      bqkv[:, 2 * C:3 * C].rearrange("p (h d) -> p h d", h=H), ALU.add)
                    empties(dve.tensor_tensor(qk[:, tb, :], b[:, 0:2 * C], bqkv[:, 0:2 * C], ALU.add))

                def a_split(tb):
                    q = qk[:, tb, 0:C].rearrange("p (h d) -> p h d", h=H)
                    r = rest_q[:, :].rearrange("p (h d) -> p h d", h=H)
                    written("A_qkv", tb)
                    then(dve.tensor_copy(qstack[:, tb, :, 0:3, :], q.unsqueeze(2).broadcast_to((P, H, 3, DA))))
                    then(dve.tensor_tensor(r, q, qstack[:, tb, :, 0, :], ALU.subtract))
                    then(dve.tensor_copy(qstack[:, tb, :, 3:5, :], r.unsqueeze(2).broadcast_to((P, H, 2, DA))))
                    dve.tensor_tensor(qstack[:, tb, :, 5, :], r, qstack[:, tb, :, 3, :], ALU.subtract)\
                        .then_inc(s["q_split"], 1)
                    dve.wait_ge(*at(i, "q_split", tb + 1))

                def a_out(_):
                    add_out("A_out", x0, x1)
                    dve.tensor_tensor(x1[:, :, :], x1[:, :, :], bout[:, :].unsqueeze(1).broadcast_to((P, TB, C)), ALU.add)\
                        .then_inc(s["x_used"], 1)

                def f0_norm(_):
                    dve.wait_ge(*at(i, "x_used", 1))
                    norm("F0_norm", x1, xn)

                def f0_out(_):
                    dve.wait_ge(*at(i, "kept", 1))
                    add_out("F0_out", x1, x2)

                def f1_out(_):
                    dve.wait_ge(*at(i, "stored", 0))
                    add_out("F1_out", x3, y)

                def b_gate(_):
                    b = full_bank("B_gate")
                    then(dve.tensor_reduce(zmax[:, :], b[:, 0:3], AX_X, ALU.max))
                    empties(dve.tensor_scalar(z[:, :], b[:, 0:3], zmax[:, 0:1], None, ALU.subtract))

                def b_rms(_):
                    dve.wait_ge(*at(i, *emptied("B_small")))
                    for j, (c0, c1) in enumerate(((0, QL), (QL, KR))):
                        for tb in range(TB):
                            then(dve.tensor_tensor_reduce(work[:, 0:c1 - c0], small[:, tb, c0:c1], small[:, tb, c0:c1],
                                                          1.0, 0.0, ALU.mult, ALU.add,
                                                          square_sum[:, TB * j + tb:TB * j + tb + 1]))
                    dve.tensor_scalar(var[:, 0:2], square_sum[:, 0:2], 1.0 / QL, RMS_EPS, ALU.mult, ALU.add)
                    dve.tensor_scalar(var[:, 2:4], square_sum[:, 2:4], 1.0 / KVL, RMS_EPS, ALU.mult, ALU.add)\
                        .then_inc(s["var"], 1)
                    dve.wait_ge(*at(i, "rstd", done("rstd", "B_rms")))
                    for tb in range(TB):
                        dve.tensor_scalar(nrm[:, tb, 0:QL], small[:, tb, 0:QL], rstd[:, tb:tb + 1], None, ALU.mult)
                        ins = dve.tensor_scalar(nrm[:, tb, QL:P], small[:, tb, QL:KR], rstd[:, 2 + tb:3 + tb], None,
                                                ALU.mult)
                    ins.then_inc(s["nrm"], 1)
                    dve.wait_ge(*at(i, "z_exp", 1))
                    then(dve.tensor_reduce(zmax[:, :], zexp[:, :], AX_X, ALU.add))
                    then(dve.reciprocal(zmax[:, :], zmax[:, :]))
                    then(dve.tensor_scalar(gate[:, :], zexp[:, :], zmax[:, 0:1], None, ALU.mult))

                def b_krope(_):
                    k = small[:, :, KR:GT]
                    dve.tensor_tensor(kr[:, :, :], k, cosx[:, :, NOPE:DB], ALU.mult)
                    then(dve.tensor_tensor(kr_swapped[:, :, :].rearrange("p n (e d) -> p n e d", e=2),
                                           k.rearrange("p n (e d) -> p n e d", e=2)[:, :, ::-1, :],
                                           sinx[:, :, :].rearrange("p n (e d) -> p n e d", e=2), ALU.mult))
                    dve.tensor_tensor(kr[:, :, :], kr[:, :, :], kr_swapped[:, :, :], ALU.add).then_inc(s["krope"], 1)

                def b_rank(_):
                    dve.wait_ge(*at(i, "misc_act", 0))
                    for tb in range(TB):
                        then(dve.tensor_tensor_reduce(work[:, 0:P], imp[:, tb * P:(tb + 1) * P], ident[:, :], 1.0, 0.0,
                                                      ALU.mult, ALU.add, icol[:, tb:tb + 1]))
                        then(dve.scalar_tensor_tensor(out=work[:, :], in0=imp[:, :], scalar=icol[:, tb:tb + 1],
                                                      in1=before[:, tb, :], op0=ALU.is_equal, op1=ALU.mult))
                        then(dve.scalar_tensor_tensor(out=work[:, :], in0=imp[:, :], scalar=icol[:, tb:tb + 1],
                                                      in1=work[:, :], op0=ALU.is_gt, op1=ALU.add))
                        then(dve.tensor_reduce(rank[:, tb:tb + 1], work[:, :], AX_X, ALU.add))
                    dve.tensor_scalar(keep[:, :], rank[:, :], float(KEEP), None, ALU.is_lt).then_inc(s["picked"], 1)

                def b_pos(_):
                    b = full_bank("B_pos")
                    empties(dve.tensor_copy(pos[:, :], b[:, 0:TB]))
                    written("B_pos")
                    for tb in range(TB):
                        ins = dve.tensor_scalar(onehot[:, tb, :], slots[:, :], pos[:, tb:tb + 1], keep[:, tb:tb + 1],
                                                ALU.is_equal, ALU.mult)
                    ins.then_inc(s["onehot"], 1)

                def b_vs(_):
                    b = full_bank("B_vs")
                    for j in range(G):
                        rows = slice(KEEP * j, KEEP * (j + 1))
                        ins = dve.tensor_copy(vsel[rows, :, j, 0:VD], b[rows, 0:NG * VD].rearrange("p (g d) -> p g d", g=NG))
                    empties(ins)

                def b_s2(tb):
                    n = begun("sq_full", ("B_s2", tb))
                    dve.wait_ge(*at(i, "sq_full", n + 1))
                    b = sq[n % 2][:, :].rearrange("p (h w) -> p h w", w=KEEP)
                    then(dve.tensor_reduce(negm_sel[:, tb, :], b, AX_X, ALU.max, negate=True))
                    dve.tensor_tensor(part[:, 1, tb, :, :], b, negm_sel[:, tb, :].unsqueeze(2).broadcast_to((P, H, KEEP)),
                                      ALU.add).then_inc(s["sq_used"], 1)

                part_of = dict(
                    A_norm=a_norm, A_qkv=a_qkv, A_split=a_split, A_max=lambda g: maxima("A_max", g, negs_a, SA),
                    A_m=a_m,
                    A_pv=lambda g: scale_out("A_pv", g, DA, ya[:, :, G * DA * g:G * DA * (g + 1)]
                                             .rearrange("p n (j d) -> p n j d", j=G), None),
                    A_out=a_out, F0_norm=f0_norm, F0_h=lambda c: hidden(0, c), F0_out=f0_out,
                    B_norm=lambda _: norm("B_norm", x2, xn_b), B_gate=b_gate, B_rms=b_rms, B_krope=b_krope,
                    B_q=lambda n: rope_ring("B_q", n), B_w=lambda n: rope_ring("B_w", n),
                    B_max1=lambda g: maxima("B_max1", g, negs_b, SB),
                    B_rank=b_rank, B_pos=b_pos, B_ks=lambda g: rope("B_ks", g, ksfull[:, G * g:G * g + G, :], 0, KEEP),
                    B_vs=b_vs, B_s2=b_s2, B_max3=lambda g: maxima("B_max3", g, negs_b, SB + H),
                    B_pv1=lambda g: branch_out("B_pv1", g, 0), B_pv2=lambda g: branch_out("B_pv2", g, 1),
                    B_pv3=lambda g: branch_out("B_pv3", g, 2),
                    B_out=lambda _: add_out("B_out", x2_old, x3),
                    F1_norm=lambda _: norm("F1_norm", x3, xn), F1_h=lambda c: hidden(1, c), F1_out=f1_out,
                )
                for name, n in ORDER:
                    if name in part_of:
                        part_of[name](n)
                assert chain[0] == PER_TURN["dve_step"], chain[0]

        @block.gpsimd
        def _(pool):
            pool.memset(idle_p[:, :], 0.0)
            pool.memset(vsel[:, :, :, :], 0.0).then_inc(s["pool_step"], 1)
            pool.memset(minus_half[:, :], -0.5).then_inc(s["set_pool"], 1)
            pool.wait_ge(s["set_pool"], 1)

            with pool.Fori(0, TURNS) as i:
                chain = [0]

                def then(ins):
                    chain[0] += 1
                    ins.then_inc(s["pool_step"], 1)
                    pool.wait_ge(s["pool_step"], i * PER_TURN["pool_step"] + chain[0] + 1)

                def carry_waits():
                    pool.tensor_tensor(idle_p[:, 2:3], idle_p[:, 0:1], idle_p[:, 1:2], ALU.add)

                def rsqrt(name, n):
                    pool.wait_ge(*at(i, "var", done("var", name)))
                    pool.tensor_tensor(rstd[:, 0:n], var[:, 0:n], minus_half[:, 0:n], ALU.pow).then_inc(s["rstd"], 1)

                def a_split(tb):
                    k = qk[:, tb, C:2 * C].rearrange("p (h d) -> p h d", h=H)
                    r = rest_k[:, :].rearrange("p (h d) -> p h d", h=H)
                    pool.wait_ge(*at(i, *emptied("A_qkv", tb)))
                    carry_waits()
                    pool.tensor_copy(kstack[:, tb, :, 3, :], k)
                    pool.tensor_copy(kstack[:, tb, :, 5, :], k)
                    then(pool.tensor_copy(kstack[:, tb, :, 0, :], k))
                    then(pool.tensor_tensor(r, k, kstack[:, tb, :, 0, :], ALU.subtract))
                    carry_waits()
                    pool.tensor_copy(kstack[:, tb, :, 4, :], r)
                    then(pool.tensor_copy(kstack[:, tb, :, 1, :], r))
                    pool.tensor_tensor(kstack[:, tb, :, 2, :], r, kstack[:, tb, :, 1, :], ALU.subtract)\
                        .then_inc(s["k_split"], 1)
                    pool.wait_ge(*at(i, "k_split", tb + 1))

                def b_k1r(tb):
                    if tb == 0:
                        pool.wait_ge(*at(i, "krope", 1))
                        pool.wait_ge(*at(i, "misc_full", done("misc_full", "B_oT", 1)))
                        carry_waits()
                    pool.tensor_copy(k1full[:, tb, :, NOPE:DB], kr[:, tb, :].unsqueeze(1).broadcast_to((P, H, ROPE)))\
                        .then_inc(s["k1_full"], 1)

                def add_swapped(name, n, dst, rows):
                    pool.wait_ge(*at(i, *emptied(name, n)))
                    pool.tensor_tensor(dst, dst, swapped[0:rows, begun("roped", (name, n)) % 2, :, :], ALU.add)\
                        .then_inc(s["roped"], 1)

                def add_branch(name, g, a_part):
                    pool.wait_ge(*at(i, "ob_used", done("ob_used", name, g)))
                    if begun("summed", (name, g)):
                        pool.wait_ge(*at(i, "summed", begun("summed", (name, g))))
                    first, other = (part[:, k, :, G * g:G * g + G, :] for k in (0, a_part))
                    pool.tensor_tensor(first, first, other, ALU.add).then_inc(s["summed"], 1)

                part_of = dict(
                    A_norm=lambda _: rsqrt("A_norm", TB), F0_norm=lambda _: rsqrt("F0_norm", TB),
                    B_norm=lambda _: rsqrt("B_norm", TB), F1_norm=lambda _: rsqrt("F1_norm", TB),
                    B_rms=lambda _: rsqrt("B_rms", 2 * TB), A_split=a_split, B_k1r=b_k1r,
                    B_q=lambda n: add_swapped("B_q", n, full[:, ring_of("B_q", n), :, NOPE:DB], P),
                    B_w=lambda n: add_swapped("B_w", n, full[:, ring_of("B_w", n), :, NOPE:DB], P),
                    B_ks=lambda g: add_swapped("B_ks", g, ksfull[:, G * g:G * g + G, NOPE:DB], KEEP),
                    B_pv2=lambda g: add_branch("B_pv2", g, 1), B_pv3=lambda g: add_branch("B_pv3", g, 2),
                )
                for name, n in ORDER:
                    if name in part_of:
                        part_of[name](n)
                assert chain[0] == PER_TURN["pool_step"], chain[0]


def constants():
    i, j = np.arange(P)[:, None], np.arange(P)[None, :]
    heads_of_rows = np.zeros((P, 2, H), np.float32)
    for h in range(H):
        heads_of_rows[[SA + h, SA + H + h, SB + h], 0, h] = 1
        heads_of_rows[SB + H + h, 1, h] = 1
    token = np.arange(TB)[None, :, None] * P + np.arange(P)[:, None, None]
    freq = (1.0 / np.float32(10000.0) ** (np.arange(0, ROPE, 2, dtype=np.float32) / np.float32(ROPE))).astype(np.float32)
    angle = token.astype(np.float32) * freq
    cos, sin = np.cos(angle).astype(np.float32), np.sin(angle).astype(np.float32)
    return {
        "c_ident": np.eye(P, dtype=np.float32),
        "c_masks": np.concatenate([np.where(j > i, BIG, 0), np.where(i > j, BIG, 0)], axis=1).astype(np.float32),
        "c_heads": heads_of_rows.reshape(P, -1),
        "c_before": (np.arange(T)[None, None, :] < token).astype(np.float32),
        "c_before_k": (i < j).astype(np.float32),
        "c_slots": np.tile(np.arange(KEEP, dtype=np.float32), (P, 1)),
        "c_cos": np.concatenate([np.ones((P, TB, NOPE), np.float32), cos, cos], axis=2),
        "c_sin": np.concatenate([-sin, sin], axis=2),
    }


INPUTS = ["L0_attn_a_x", "L0_attn_a_W_attn", "L0_attn_a_b_attn", "L0_attn_a_W_proj", "L0_attn_a_b_proj",
          "L0_attn_b_w_cq", "L0_attn_b_g_qnorm", "L0_attn_b_w_dq_nope", "L0_attn_b_w_dq_rope", "L0_attn_b_w_ckv",
          "L0_attn_b_g_kvnorm", "L0_attn_b_w_dk_nope", "L0_attn_b_w_dv", "L0_attn_b_w_krope", "L0_attn_b_w_imp",
          "L0_attn_b_w_selk", "L0_attn_b_w_selv", "L0_attn_b_w_wink", "L0_attn_b_w_winv", "L0_attn_b_w_gate",
          "L0_attn_b_w_proj", "L0_ffn_w_gate", "L0_ffn_w_up", "L0_ffn_w_down"]


def kernel(**inputs):
    import concourse.bacc as bacc
    from concourse.bass_utils import run_bass_kernel_spmd

    nc = bacc.Bacc("TRN2", target_bir_lowering=False, num_devices=1)
    arrays = {name: np.ascontiguousarray(inputs[name]) for name in INPUTS}
    arrays.update(constants())
    args = {name: nc.dram_tensor(name, v.shape, mybir.dt.from_np(v.dtype), kind="ExternalInput").ap()
            for name, v in arrays.items()}
    out = nc.dram_tensor("out", (NSEQ, T, C), F32, kind="ExternalOutput").ap()
    build(nc, args, out)
    r = run_bass_kernel_spmd(nc, [arrays], core_ids=[0])
    return r.results[0]["out"]
```

```python
from contextlib import ExitStack

import numpy as np

import concourse.bass as bass
from concourse import mybir

F32 = mybir.dt.float32
BF16 = mybir.dt.bfloat16
I32 = mybir.dt.int32
ALU = mybir.AluOpType
ACT = mybir.ActivationFunctionType
AX_X = mybir.AxisListType.X

NSEQ, T, C = 32, 256, 128
TURNS = NSEQ + 2
P = 128
TB = T // P
H = 16
DA = C // H
HID = 384
HC = HID // P
QL, KVL = 96, 32
NOPE, ROPE, VD = 32, 64, 32
DB = ROPE + NOPE
KEEP = 32
G = 4
NG = H // G
SA, SB = 64, DB
PARTS = 6
KA = PARTS * DA
SMALL = QL + KVL + ROPE + 3
KR, GT = QL + KVL, QL + KVL + ROPE
BIG = -1e30
FFN_SCALE = 1.0 / 127.0
LN_EPS, RMS_EPS = 1e-5, 1e-6


def steps(text):
    return [(w.split(":")[0], int(w.split(":")[1]) if ":" in w else 0) for w in text.split()]


ORDER = steps("""
    A_norm B_v:0 B_krope B_gate B_q:0 F1_norm A_xT B_krT A_qkv:0 B_qT:0 A_split:0 F1_xT B_q:1 B_rank B_q:2
    B_kn:0 F1_h:0 A_turn:0 B_qT:1 A_qkv:1 F1_h:1 B_q:3 A_turn:1 B_max1:0 B_qT:2 A_turn:2 A_split:1 A_turn:3
    B_q:4 B_qT:3 B_pos A_turn:4 F1_h:2 A_turn:5 B_v:1 B_q:5 B_qT:4 B_q:6 A_turn:6 B_q:7 A_turn:7 B_max1:1
    A_max:0 B_w:0 B_qT:5 A_max:1 B_qT:6 A_max:2 B_soft B_kn:1 A_max:3 B_wT:0 A_m B_w:1 B_w:2 B_sel A_t:0
    B_max1:2 B_ks:0 A_t:1 B_qT:7 A_pv:0 B_wT:1 B_max1:3 B_keep B_w:3 B_m1 F1_out A_pv:1 B_ks:1 B_t1:0 A_t:2
    B_w:4 B_max3:0 B_pv1:0 B_w:5 A_t:3 B_ks:2 B_w:6 B_wT:2 B_wT:3 A_pv:2 B_t1:1 B_ks:3 B_wT:4 A_pv:3 B_t1:2 A_yT
    B_pv1:1 B_wT:5 A_out B_wT:6 B_max3:1 B_w:7 B_t1:3 F0_norm B_ksT B_wT:7 B_max3:2 F0_xT B_max3:3 F0_h:0 B_m3
    B_s2:0 F0_h:1 B_pv1:2 B_vw:0 B_vs F0_h:2 B_t3:0 B_p2:0 B_s2:1 B_vw:1 F0_out B_pv1:3 B_norm B_p2:1 B_t3:1
    B_pv3:0 B_pv2:0 B_t3:2 B_xT B_pv3:1 B_small B_pv3:2 B_pv2:1 B_t3:3 B_rms B_pv2:2 B_pv3:3 B_pv2:3 B_imp B_nT
    B_oT:0 B_oT:1 B_out
""")

_HEADS = dict(A_max=3, B_max1=3, B_max3=3, B_s2=1)
_T = dict(A_t=3, B_t1=3, B_t3=3)
_ACT = "A_xT A_turn A_yT F0_xT B_xT B_small B_imp B_nT B_m1 B_m3 B_kn B_v B_krT B_qT B_vw B_wT B_sel B_ksT B_p2 B_oT F1_xT"
_DVE = "A_qkv A_m A_out F0_h F0_out B_gate B_q B_w B_pos B_ks B_vs B_out F1_h F1_out " \
    "A_pv B_pv1 B_pv2 B_pv3"
EMPTIED_BY = {**dict.fromkeys(_ACT.split(), "act"), **dict.fromkeys(_DVE.split(), "dve")}
_NORM = dict(A_norm=1, F0_norm=1, B_norm=1, F1_norm=1)

GIVES = {
    "act_full": {k: 1 for k, e in EMPTIED_BY.items() if e == "act"},
    "act_used": {k: 1 for k, e in EMPTIED_BY.items() if e == "act"},
    "dve_full": {k: 1 for k, e in EMPTIED_BY.items() if e == "dve"},
    "dve_used": {k: 1 for k, e in EMPTIED_BY.items() if e == "dve"},
    "sq_full": _HEADS, "sq_used": _HEADS, "sk_full": _T, "probs": _T,
    "var": {**_NORM, "B_rms": 1}, "rstd": {**_NORM, "B_rms": 1}, "xn": _NORM, "nrm": {"B_rms": 1},
    "q_split": {"A_split": 1}, "k_split": {"A_split": 1},
    "x_loaded": {"A_norm": 16}, "x_used": {"A_out": 1}, "kept": {"B_keep": 1}, "stored": {"F1_out": 16},
    "low_left": {"A_m": 1}, "shift_set": {"A_m": 1},
    "tanh": {"F0_h": 1, "F1_h": 1},
    "roped": dict(B_q=1, B_w=1, B_ks=1), "krope": {"B_krope": 1},
    "z_exp": {"B_soft": 1}, "picked": {"B_rank": 1}, "onehot": {"B_pos": 1},
    "p2": {"B_s2": 1}, "summed": {"B_pv2": 1, "B_pv3": 1},
}
CHAINS = {"dve_step": 68, "pool_step": 6}


def total(sem, order):
    return sum(GIVES[sem].get(name, 0) for name, _ in order)


PER_TURN = {sem: total(sem, ORDER) for sem in GIVES} | CHAINS
NEWEST = ("B_norm", "B_xT", "B_small", "B_imp", "B_rms", "B_nT")
ONLY_NEWEST = [step for step in ORDER if step[0] in NEWEST or step[0][:2] in ("A_", "F0")]
NO_NEWEST = [step for step in ORDER if step not in ONLY_NEWEST]
ONLY_OLDEST = [step for step in ORDER if step[0].startswith("F1_")]


class Walk:

    def first(self):
        self.short = dict.fromkeys(PER_TURN, 0)
        self.order, self.before = ONLY_NEWEST, ORDER
        yield 0
        self.fell_short()
        self.order, self.before = ORDER, ONLY_NEWEST
        yield 1
        self.before = ORDER

    def last(self):
        self.order = NO_NEWEST
        yield NSEQ
        self.fell_short()
        self.order, self.before = ONLY_OLDEST, NO_NEWEST
        yield NSEQ + 1
        self.fell_short()

    def fell_short(self):
        for sem in PER_TURN:
            given = self.chain.get(sem, 0) if sem in CHAINS else total(sem, self.order)
            self.short[sem] += PER_TURN[sem] - given

    def fills(self, by, before=False):
        return [step for step in (self.before if before else self.order) if EMPTIED_BY.get(step[0]) == by]

    def among(self, step, names):
        return [other for other in self.order if other[0] in names].index(step)


walk = Walk()
walk.chain = {}


def begun(sem, step):
    return total(sem, walk.order[:walk.order.index(step)])


def done(sem, name, n=0):
    return begun(sem, (name, n)) + GIVES[sem][name]


PV = ("A_pv", "B_pv1", "B_pv3")
RING = 4
RING_STEPS = [step for step in ORDER if step[0] in ("B_q", "B_w")]


def ring_of(name, n):
    return RING_STEPS.index((name, n)) % RING


AHEAD = {"act_used": PER_TURN["act_used"], "dve_used": PER_TURN["dve_used"], "stored": 16}


def build(nc, a, out):
    ctx = ExitStack()
    with ctx:
        def sb(name, shape, dt=F32):
            return ctx.enter_context(nc.sbuf_tensor(name, shape, dt))

        def bank(name):
            return ctx.enter_context(nc.psum_tensor(name, [P, 512], F32))

        ident = sb("ident", [P, P])
        ident_h = sb("ident_h", [P, P], BF16)
        mask_q = sb("mask_q", [P, P], BF16)
        mask_k = sb("mask_k", [P, P], BF16)
        before = sb("before", [P, TB, T])
        before_k = sb("before_k", [P, P])
        ones = sb("ones", [P, P])
        mean_of = sb("mean_of", [P, P])
        slots = sb("slots", [P, KEEP])
        cosx = sb("cosx", [P, TB, DB])
        sinx = sb("sinx", [P, TB, ROPE])
        minus_half = sb("minus_half", [P, 4])
        wqkv = sb("wqkv", [P, 3 * C])
        bqkv = sb("bqkv", [P, 3 * C])
        wout = sb("wout", [P, C])
        bout = sb("bout", [P, C])
        wgate = sb("wgate", [P, HID])
        wup = sb("wup", [P, HID])
        wdown = sb("wdown", [P, HC * C])
        wsmall = sb("wsmall", [P, SMALL])
        wimp = sb("wimp", [P, 1])
        wimp_all = sb("wimp_all", [P, P])
        gcol = sb("gcol", [P, 1])
        wq = sb("wq", [QL, H, DB])
        wkv = sb("wkv", [P, 2, H, NOPE])
        wselk = sb("wselk", [P, H, DB])
        wselv = sb("wselv", [P, H, VD])
        wwink = sb("wwink", [P, H, DB])
        wwinv = sb("wwinv", [P, H, VD])
        wproj = sb("wproj", [P, NG, C])
        spare = sb("spare", [P, 4])
        idle = sb("idle", [P, 4])
        idle_p = sb("idle_p", [P, 4])

        x0 = sb("x0", [P, TB, C])
        x1 = sb("x1", [P, TB, C])
        x2 = sb("x2", [P, TB, C])
        x2_old = sb("x2_old", [P, TB, C])
        x3 = sb("x3", [P, TB, C])
        y = sb("y", [P, TB, C])
        stats = sb("stats", [P, TB, 6])
        mv = sb("mv", [P, TB, 2])
        var = sb("var", [P, 4])
        rstd = sb("rstd", [P, 4])
        xn = sb("xn", [P, TB, C])
        xnT = sb("xnT", [P, T])
        xn_f = sb("xn_f", [P, TB, C])
        xnT_f = sb("xnT_f", [P, T])
        xn_b = sb("xn_b", [P, TB, C])
        xnT_b = sb("xnT_b", [P, T])
        qk = sb("qk", [P, TB, 2 * C])
        rest_q = sb("rest_q", [P, C])
        rest_k = sb("rest_k", [P, C])
        qstack = sb("qstack", [P, TB, H, PARTS, DA], BF16)
        kstack = sb("kstack", [P, TB, H, PARTS, DA], BF16)
        va = sb("va", [P, TB, H, DA + 1])
        negs_a = sb("negs_a", [P, TB, P])
        negs_b = sb("negs_b", [P, TB, P])
        negs_high = sb("negs_high", [P, TB, H], BF16)
        shift_a = sb("shift_a", [P, T], BF16)
        qTa = sb("qTa", [SA + 2 * H, H, T], BF16)
        kTa = sb("kTa", [SA + 2 * H, H, T], BF16)
        negm_sel = sb("negm_sel", [P, TB, H])
        probs = sb("probs", [P, 2, 3, 512])
        rden = sb("rden", [P, 2, TB, G])
        ya = sb("ya", [P, TB, C])
        yaT = sb("yaT", [P, T])
        th = sb("th", [P, 2, T])
        hmid = sb("hmid", [P, 2, T])
        hT = sb("hT", [P, HC, T])
        small = sb("small", [P, TB, SMALL])
        imp = sb("imp", [P, T])
        work = sb("work", [P, T])
        icol = sb("icol", [P, TB])
        rank = sb("rank", [P, TB])
        keep = sb("keep", [P, TB])
        pos = sb("pos", [P, TB])
        onehot = sb("onehot", [P, TB, KEEP])
        z = sb("z", [P, 3])
        zmax = sb("zmax", [P, 1])
        zexp = sb("zexp", [P, 3])
        gate = sb("gate", [P, 3])
        square_sum = sb("square_sum", [P, 4])
        nrm = sb("nrm", [P, TB, P])
        nT = sb("nT", [P, T])
        full = sb("full", [P, RING, G, DB])
        part = sb("part", [P, 3, TB, H, VD])
        ksfull = sb("ksfull", [KEEP, H, DB])
        swapped = sb("swapped", [P, 2, G, ROPE])
        kr = sb("kr", [P, TB, ROPE])
        kr_swapped = sb("kr_swapped", [P, TB, ROPE])
        qT = sb("qT", [P, H, T])
        k1T = sb("k1T", [P, H, T])
        kwT = sb("kwT", [P, H, T])
        ksT = sb("ksT", [DB, H, KEEP])
        xselT = sb("xselT", [P, KEEP])
        v1 = sb("v1", [P, TB, H, VD + 1])
        vw = sb("vw", [P, TB, H, VD + 1])
        vsel = sb("vsel", [P, NG, G, VD + 1])
        staged = part[:, :, :, :, :].rearrange("p a n h d -> p (a n h d)")[:, 0:2 * P + 2 * H]
        heads_of_rows = staged[:, 2 * P:].rearrange("p (u h) -> p u h", u=2)
        w_raw = probs[:, 0, 0, 0:HID].rearrange("p (n c) -> p n c", c=P)
        w_int = probs[:, 0, 1, 0:HID].rearrange("p (n c) -> p n c", c=P).bitcast(I32)
        oT = sb("oT", [P, NG, T])
        p2T = oT

        emptied_banks = {by: [bank(f"by_{by}{n}") for n in range(2)] for by in ("act", "dve")}
        sq = [bank("sq0"), bank("sq1")]
        sk = [bank("sk0"), bank("sk1")]

        s = {name: ctx.enter_context(nc.semaphore(f"s_{name}"))
             for name in (*PER_TURN, "c_loaded", "w_turned", "w_copied", "set_dve", "set_pool")}

        def at(i, sem, n):
            return s[sem], i * PER_TURN[sem] + n + AHEAD.get(sem, 0) - walk.short[sem]

        def halves(ap):
            return ap.bitcast(BF16)[:, 1::2]

        USES = {
            "A": dict(t="A_t", k=KA, kt=SA + 2 * H, q=qTa, key=kTa, v=va, d=DA, scale=DA ** -0.5, view=lambda ap: ap),
            "1": dict(t="B_t1", k=DB, kt=P, q=qT, key=k1T, v=v1, d=VD, scale=DB ** -0.5, view=halves),
            "3": dict(t="B_t3", k=DB, kt=P, q=qT, key=kwT, v=vw, d=VD, scale=DB ** -0.5, view=halves),
        }

        def bank_of(name, n=0):
            by = EMPTIED_BY[name]
            return emptied_banks[by][begun(f"{by}_full", (name, n)) % 2]

        def was_filled(name, n=0):
            return f"{EMPTIED_BY[name]}_full", done(f"{EMPTIED_BY[name]}_full", name, n)

        def emptied(name, n=0):
            return f"{EMPTIED_BY[name]}_used", done(f"{EMPTIED_BY[name]}_used", name, n)

        def emptied_before(name, n=0):
            sem = f"{EMPTIED_BY[name]}_used"
            if (name, n) not in walk.before:
                return sem, 0
            return sem, -total(sem, walk.before[walk.before.index((name, n)) + 1:])

        def bank_heads(g, t):
            return (range(G * g, G * g + G), P) if t == 0 else (range(G * g + 2 * t - 2, G * g + 2 * t), T)

        def half_of_probs(t_name, g):
            return begun("sk_full", (t_name, g)) // 3 % 2

        TURNED = [
            ("L0_attn_a_W_attn", False, wqkv, HC), ("L0_attn_a_W_proj", False, wout, 1),
            ("L0_ffn_w_gate", True, wgate, HC), ("L0_ffn_w_up", True, wup, HC), ("L0_ffn_w_down", True, wdown, HC),
        ]
        ONES_IN_KEYS = [(kTa, slice(SA, SA + 2 * H), 0), (k1T, slice(SB, P), 0), (kwT, slice(SB, P), 1)]
        heads = "p (h d) -> p h d"
        LOADED = [
            (ident[:, :], a["c_ident"]), (staged[:, 0:2 * P], a["c_masks"]), (staged[:, 2 * P:], a["c_heads"]),
            (before[:, :, :], a["c_before"]),
            (before_k[:, :], a["c_before_k"]), (slots[:, :], a["c_slots"]), (cosx[:, :, :], a["c_cos"]),
            (sinx[:, :, :], a["c_sin"]),
            (bqkv[:, :], a["L0_attn_a_b_attn"].partition_broadcast(P)),
            (bout[:, :], a["L0_attn_a_b_proj"].partition_broadcast(P)),
            (wsmall[:, 0:QL], a["L0_attn_b_w_cq"]), (wsmall[:, QL:KR], a["L0_attn_b_w_ckv"]),
            (wsmall[:, KR:GT], a["L0_attn_b_w_krope"]), (wsmall[:, GT:SMALL], a["L0_attn_b_w_gate"]),
            (wimp[:, :], a["L0_attn_b_w_imp"]),
            (gcol[0:QL, :], a["L0_attn_b_g_qnorm"].rearrange("(p a) -> p a", a=1)),
            (gcol[QL:P, :], a["L0_attn_b_g_kvnorm"].rearrange("(p a) -> p a", a=1)),
            (wq[:, :, ROPE:DB], a["L0_attn_b_w_dq_nope"].rearrange(heads, h=H)),
            (wq[:, :, 0:ROPE], a["L0_attn_b_w_dq_rope"].rearrange(heads, h=H)),
            (wkv[QL:P, 0, :, :], a["L0_attn_b_w_dk_nope"].rearrange(heads, h=H)),
            (wkv[QL:P, 1, :, :], a["L0_attn_b_w_dv"].rearrange(heads, h=H)),
            (wselk[:, :, ROPE:DB], a["L0_attn_b_w_selk"].rearrange(heads, h=H)[:, :, 0:NOPE]),
            (wselk[:, :, 0:ROPE], a["L0_attn_b_w_selk"].rearrange(heads, h=H)[:, :, NOPE:DB]),
            (wselv[:, :, :], a["L0_attn_b_w_selv"].rearrange(heads, h=H)),
            (wwink[:, :, ROPE:DB], a["L0_attn_b_w_wink"].rearrange(heads, h=H)[:, :, 0:NOPE]),
            (wwink[:, :, 0:ROPE], a["L0_attn_b_w_wink"].rearrange(heads, h=H)[:, :, NOPE:DB]),
            (wwinv[:, :, :], a["L0_attn_b_w_winv"].rearrange(heads, h=H)),
            (wproj[:, :, :], a["L0_attn_b_w_proj"].rearrange("(n p) c -> p n c", p=P)),
        ]

        def of_tokens(ap):
            return ap.rearrange("(n p) c -> p n c", p=P)

        block = ctx.enter_context(nc.Block())

        @block.sync
        def _(sp):
            for dst, src in LOADED:
                sp.dma_start(dst, src).then_inc(s["c_loaded"], 16)
            for n, (name, integer, _, k) in enumerate(TURNED):
                if n:
                    sp.wait_ge(s["w_turned"], n)
                src = a[name]
                src = src.rearrange("p (n c) -> p n c", c=P) if src.shape[0] == P else of_tokens(src)
                sp.dma_start((w_int if integer else w_raw)[:, 0:k, :], src).then_inc(s["c_loaded"], 16)

            def load(n):
                sp.dma_start(x0[:, :, :], of_tokens(a["L0_attn_a_x"][n, :, :])).then_inc(s["x_loaded"], 16)

            def store(i):
                sp.wait_ge(*at(i, *emptied("F1_out")))
                sp.dma_start(of_tokens(out[i - 2, :, :]), y[:, :, :]).then_inc(s["stored"], 16)

            load(0)
            for i in walk.first():
                sp.wait_ge(*at(i, "x_used", 1))
                load(i + 1)
            with sp.Fori(2, NSEQ - 1) as i:
                sp.wait_ge(*at(i, "x_used", 1))
                load(i + 1)
                store(i)
            store(NSEQ - 1)
            for i in walk.last():
                store(i)
            sp.wait_ge(*at(TURNS, "stored", 0))

        @block.tensor
        def _(pe):
            for n, (name, integer, dst, k) in enumerate(TURNED):
                pe.wait_ge(s["c_loaded"], 16 * (len(LOADED) + n + 1))
                if integer:
                    pe.wait_ge(s["set_dve"], n - 1)
                if n:
                    pe.wait_ge(s["w_copied"], n)
                for c in range(k):
                    mm = pe.transpose(emptied_banks["act"][0][:, c * P:(c + 1) * P], w_raw[:, c, :], ident[:, :])
                mm.then_inc(s["w_turned"], 1)
            pe.wait_ge(s["w_copied"], len(TURNED))
            pe.wait_ge(s["set_dve"], 4)
            pe.wait_ge(s["set_pool"], 1)

            def turn(i):
                filling = [None]

                def fill(name, n=0, needs=None):
                    filling[0] = by = EMPTIED_BY[name]
                    m = begun(f"{by}_full", (name, n))
                    if m >= 2:
                        sem, count = emptied(*walk.fills(by)[m - 2])
                    else:
                        sem, count = emptied_before(*walk.fills(by, before=True)[m::2][-1])
                    if needs and needs[0] == sem:
                        count = max(count, needs[1])
                    elif needs:
                        pe.wait_ge(*at(i, *needs))
                    pe.wait_ge(*at(i, sem, count))
                    return emptied_banks[by][m % 2]

                def filled(mm):
                    mm.then_inc(s[f"{filling[0]}_full"], 1)

                def taken(name, n=0):
                    pe.wait_ge(*at(i, *emptied(name, n)))

                def carry_waits():
                    pe.ldweights(ident_h[:, :], tile_position=(0, 0))

                def turn_tokens(name, src, sem, count):
                    b = fill(name, needs=(sem, count))
                    for tb in range(TB):
                        mm = pe.transpose(b[:, tb * P:(tb + 1) * P], src[:, tb, :], ident[:, :])
                    filled(mm)

                def max_scores(name, g, use):
                    k, view = use["k"], use["view"]
                    for t in range(3):
                        n = begun("sq_full", (name, g)) + t
                        if n >= 2:
                            pe.wait_ge(*at(i, "sq_used", n - 1))
                        b = sq[n % 2]
                        (hs, w), qb = bank_heads(g, t), int(t > 0)
                        for j, h in enumerate(hs):
                            pe.matmul(b[:, j * w:(j + 1) * w], view(use["q"][0:k, h, qb * P:(qb + 1) * P]),
                                      view(use["key"][0:k, h, 0:w]), start=(j == 0), stop=False,
                                      skip_group_check=True)
                        diagonal = b[:, :].rearrange("p (j w) -> p j w", w=w)[:, :, w - P:w]
                        pe.matmul(diagonal, ident_h[:, :], mask_q[:, :].unsqueeze(1).broadcast_to((P, len(hs), P)),
                                  start=False, stop=True, skip_group_check=True).then_inc(s["sq_full"], 1)


                def t_scores(g, use):
                    k = use["kt"]
                    for t in range(3):
                        n = begun("sk_full", (use["t"], g)) + t
                        if n >= 2:
                            pe.wait_ge(*at(i, "probs", n - 1))
                        b = sk[n % 2]
                        hs, w = bank_heads(g, t)
                        kb = int(t == 0)
                        for j, h in enumerate(hs):
                            cols = b[:, j * w:(j + 1) * w]
                            pe.matmul(cols, use["key"][0:k, h, kb * P:(kb + 1) * P], use["q"][0:k, h, T - w:T],
                                      start=(j == 0), stop=False, skip_group_check=True)
                        diagonal = b[:, :].rearrange("p (j w) -> p j w", w=w)[:, :, 0:P]
                        pe.matmul(diagonal, ident_h[:, :], mask_k[:, :].unsqueeze(1).broadcast_to((P, len(hs), P)),
                                  start=False, stop=True, skip_group_check=True).then_inc(s["sk_full"], 1)

                def pv(name, g, use):
                    w = use["d"] + 1
                    pe.wait_ge(*at(i, "probs", done("probs", use["t"], g)))
                    b = fill(name, g)
                    pr = probs[:, half_of_probs(use["t"], g), :, :]
                    for j in range(G):
                        h = G * g + j
                        low = pr[:, 1 + j // 2, (j % 2) * T:(j % 2 + 1) * T]
                        for qb in range(TB):
                            o = b[:, (qb * G + j) * w:(qb * G + j + 1) * w]
                            mm = pe.matmul(o, low[:, qb * P:(qb + 1) * P], use["v"][:, 0, h, :],
                                           start=True, stop=(qb == 0))
                            if qb:
                                mm = pe.matmul(o, pr[:, 0, j * P:(j + 1) * P], use["v"][:, 1, h, :],
                                               start=False, stop=True)
                    filled(mm)

                def project_heads(name, n, g, lhsT, w, rows, needs=None):
                    b = fill(name, n, needs)
                    filled(pe.matmul(b[0:rows, 0:G * DB], lhsT, w[:, G * g:G * g + G, :], start=True, stop=True))

                def turn_heads(name, n, src):
                    for j in range(G):
                        mm = pe.transpose(bank_of(name, n)[0:DB, j * P:(j + 1) * P], src(j), ident[:, :])
                    filled(mm)

                def turn_roped(name, n, source):
                    fill(name, n)
                    pe.wait_ge(*at(i, "roped", done("roped", source, n)))
                    turn_heads(name, n, lambda j: full[:, ring_of(source, n), j, :])

                def hidden(f, c):
                    xT = (xnT, xnT_f)[f]
                    b = fill(f"F{f}_h", c, needs=emptied(f"F{f}_xT") if c == 0 else None)
                    pe.matmul(b[:, 0:T], wgate[:, c * P:(c + 1) * P], xT[:, :], start=True, stop=True)
                    filled(pe.matmul(b[:, T:2 * T], wup[:, c * P:(c + 1) * P], xT[:, :], start=True, stop=True))

                def ffn_out(f):
                    b = fill(f"F{f}_out", needs=emptied(f"F{f}_h", HC - 1))
                    for tb in range(TB):
                        for c in range(HC):
                            mm = pe.matmul(b[:, tb * P:(tb + 1) * P], hT[:, c, tb * P:(tb + 1) * P],
                                           wdown[:, c * C:(c + 1) * C], start=(c == 0), stop=(c == HC - 1))
                    filled(mm)

                def a_qkv(tb):
                    b = fill("A_qkv", tb, needs=emptied("A_xT"))
                    filled(pe.matmul(b[:, 0:3 * C], xnT[:, tb * P:(tb + 1) * P], wqkv[:, :], start=True, stop=True))

                def a_turn(n):
                    tb, is_k, half = n // 4, n // 2 % 2, n % 2
                    b = fill("A_turn", n)[0:KA, :].bitcast(BF16)
                    pe.wait_ge(*at(i, "k_split" if is_k else "q_split", tb + 1))
                    carry_waits()
                    stack = kstack if is_k else qstack
                    for j in range(H // 2):
                        mm = pe.transpose(b[:, j * P:(j + 1) * P],
                                          stack[:, tb, half * 8 + j, :, :].rearrange("p s d -> p (s d)"), ident_h[:, :])
                    filled(mm)

                def a_max(g):
                    if g == 0:
                        taken("A_turn", 7)
                    max_scores("A_max", g, USES["A"])

                def a_t(g):
                    if g == 0:
                        pe.wait_ge(*at(i, "shift_set", 1))
                    t_scores(g, USES["A"])

                def a_out(_):
                    b = fill("A_out", needs=emptied("A_yT"))
                    for tb in range(TB):
                        mm = pe.matmul(b[:, tb * P:(tb + 1) * P], yaT[:, tb * P:(tb + 1) * P], wout[:, :],
                                       start=True, stop=True)
                    filled(mm)

                def b_small(_):
                    b = fill("B_small", needs=emptied("B_xT"))
                    for tb in range(TB):
                        mm = pe.matmul(b[:, tb * SMALL:(tb + 1) * SMALL], xnT_b[:, tb * P:(tb + 1) * P], wsmall[:, :],
                                       start=True, stop=True)
                    filled(mm)

                def b_imp(_):
                    b = fill("B_imp")
                    filled(pe.matmul(b[:, 0:T], wimp_all[:, :], xnT_b[:, :], start=True, stop=True))

                def b_gate(_):
                    b = fill("B_gate", needs=emptied_before("B_small"))
                    for tb in range(TB):
                        mm = pe.matmul(b[:, 0:3], mean_of[:, :], small[:, tb, GT:SMALL], start=(tb == 0), stop=(tb == 1))
                    filled(mm)

                def b_q(n):
                    g, tb = n // 2, n % 2
                    project_heads("B_q", n, g, nT[0:QL, tb * P:(tb + 1) * P], wq, P,
                                  emptied_before("B_nT") if n == 0 else None)

                def b_kn(n):
                    b = fill("B_kn", n, needs=emptied_before("B_nT") if n == 0 else None)
                    for g in range(2 * n, 2 * n + 2):
                        mm = pe.matmul(b[:, g % 2 * T:(g % 2 + 1) * T],
                                       wkv[QL:P, 0, G * g:G * g + G, :].rearrange("p h d -> p (h d)"), nT[QL:P, :],
                                       start=True, stop=True)
                    filled(mm)

                def b_v(tb):
                    b = fill("B_v", tb, needs=emptied_before("B_nT") if tb == 0 else None)
                    filled(pe.matmul(b[:, :], nT[QL:P, tb * P:(tb + 1) * P],
                                     wkv[QL:P, 1, :, :].rearrange("p h d -> p (h d)"), start=True, stop=True))

                def b_krT(_):
                    b = fill("B_krT")
                    pe.wait_ge(*at(i, "krope", 1))
                    carry_waits()
                    for tb in range(TB):
                        mm = pe.transpose(b[0:ROPE, tb * P:(tb + 1) * P], kr[:, tb, :], ident[:, :])
                    filled(mm)

                def b_w(n):
                    g, tb = n // 2, n % 2
                    project_heads("B_w", n, g, xnT_b[:, tb * P:(tb + 1) * P], wwink, P,
                                  emptied_before("B_xT") if n == 0 else None)

                def b_vw(tb):
                    b = fill("B_vw", tb)
                    filled(pe.matmul(b[:, :], xnT_b[:, tb * P:(tb + 1) * P], wwinv[:, :, :].rearrange("p h d -> p (h d)"),
                                     start=True, stop=True))

                def b_pos(_):
                    b = fill("B_pos")
                    pe.wait_ge(*at(i, "picked", 1))
                    pe.matmul(b[:, 0:1], before_k[:, :], keep[:, 0:1], start=True, stop=True)
                    pe.matmul(b[:, 1:2], ones[:, :], keep[:, 0:1], start=True, stop=False)
                    filled(pe.matmul(b[:, 1:2], before_k[:, :], keep[:, 1:2], start=False, stop=True))

                def b_sel(_):
                    b = fill("B_sel")
                    pe.wait_ge(*at(i, "onehot", 1))
                    for tb in range(TB):
                        mm = pe.matmul(b[:, 0:KEEP], xn_b[:, tb, :], onehot[:, tb, :], start=(tb == 0), stop=(tb == 1))
                    filled(mm)

                def b_ks(g):
                    project_heads("B_ks", g, g, xselT[:, :], wselk, KEEP, emptied("B_sel") if g == 0 else None)

                def b_vs(_):
                    b = fill("B_vs")
                    for j in range(G):
                        mm = pe.matmul(b[KEEP * j:KEEP * (j + 1), 0:NG * VD], xselT[:, :], wselv[:, j::G, :],
                                       start=True, stop=True)
                    filled(mm)

                def b_ksT(_):
                    b = fill("B_ksT")
                    pe.wait_ge(*at(i, "roped", done("roped", "B_ks", NG - 1)))
                    carry_waits()
                    for h in range(H):
                        mm = pe.transpose(b[0:DB, h * KEEP:(h + 1) * KEEP], ksfull[:, h, :], ident[0:KEEP, 0:KEEP])
                    filled(mm)

                def b_s2(tb):
                    if tb == 0:
                        taken("B_ksT")
                    n = begun("sq_full", ("B_s2", tb))
                    pe.wait_ge(*at(i, "sq_used", n - 1))
                    for h in range(H):
                        mm = pe.matmul(sq[n % 2][:, h * KEEP:(h + 1) * KEEP], qT[0:DB, h, tb * P:(tb + 1) * P],
                                       ksT[:, h, :], start=True, stop=True)
                    mm.then_inc(s["sq_full"], 1)

                def b_p2(tb):
                    b = fill("B_p2", tb)
                    pe.wait_ge(*at(i, "p2", tb + 1))
                    for g in range(NG):
                        mm = pe.transpose(b[:, g * P:(g + 1) * P],
                                          part[:, 1, tb, G * g:G * g + G, :].rearrange("p h d -> p (h d)"), ident[:, :])
                    filled(mm)

                def b_pv2(g):
                    if g == 0:
                        taken("B_p2", 1)
                    b = fill("B_pv2", g, needs=emptied("B_vs") if g == 0 else None)
                    w = G * (VD + 1)
                    for tb in range(TB):
                        mm = pe.matmul(b[:, tb * w:(tb + 1) * w], p2T[:, g, tb * P:(tb + 1) * P],
                                       vsel[:, g, :, :].rearrange("p j d -> p (j d)"), start=True, stop=True)
                    filled(mm)

                def b_max3(g):
                    taken("B_wT", 2 * g + 1)
                    max_scores("B_max3", g, USES["3"])

                def b_max1(g):
                    needed = [("B_qT", 2 * g + 1), ("B_krT", 0), ("B_kn", g // 2)]
                    taken(*max(needed, key=ORDER.index))
                    max_scores("B_max1", g, USES["1"])

                def b_t3(g):
                    if g == 0:
                        taken("B_m3")
                    t_scores(g, USES["3"])

                def b_t1(g):
                    if g == 0:
                        taken("B_m1")
                    t_scores(g, USES["1"])

                def b_pv3(g):
                    if g == 0:
                        taken("B_vw", 1)
                    pv("B_pv3", g, USES["3"])

                def b_oT(tb):
                    b = fill("B_oT", tb, needs=("summed", PER_TURN["summed"]) if tb == 0 else None)
                    for n in range(NG):
                        mm = pe.transpose(b[:, n * P:(n + 1) * P],
                                          part[:, 0, tb, G * n:G * n + G, :].rearrange("p h d -> p (h d)"), ident[:, :])
                    filled(mm)

                def b_out(_):
                    b = fill("B_out", needs=emptied("B_oT", 1))
                    for tb in range(TB):
                        for n in range(NG):
                            mm = pe.matmul(b[:, tb * P:(tb + 1) * P], oT[:, n, tb * P:(tb + 1) * P], wproj[:, n, :],
                                           start=(n == 0), stop=(n == NG - 1))
                    filled(mm)

                part_of = dict(
                    A_xT=lambda _: turn_tokens("A_xT", xn, "xn", done("xn", "A_norm")),
                    A_qkv=a_qkv, A_turn=a_turn, A_max=a_max,
                    A_m=lambda _: turn_tokens("A_m", negs_a, "low_left", 1),
                    A_t=a_t, A_pv=lambda g: pv("A_pv", g, USES["A"]),
                    A_yT=lambda _: turn_tokens("A_yT", ya, *emptied("A_pv", NG - 1)),
                    A_out=a_out,
                    F0_xT=lambda _: turn_tokens("F0_xT", xn, "xn", done("xn", "F0_norm")),
                    F0_h=lambda c: hidden(0, c), F0_out=lambda _: ffn_out(0),
                    B_xT=lambda _: turn_tokens("B_xT", xn_b, "xn", done("xn", "B_norm")),
                    B_small=b_small, B_imp=b_imp, B_gate=b_gate,
                    B_nT=lambda _: turn_tokens("B_nT", nrm, "nrm", 1),
                    B_q=b_q, B_kn=b_kn, B_v=b_v, B_krT=b_krT, B_qT=lambda n: turn_roped("B_qT", n, "B_q"),
                    B_w=b_w, B_vw=b_vw, B_wT=lambda n: turn_roped("B_wT", n, "B_w"),
                    B_max1=b_max1, B_m1=lambda _: turn_tokens("B_m1", negs_b, "sq_used", done("sq_used", "B_max1", NG - 1)),
                    B_pos=b_pos, B_sel=b_sel, B_ks=b_ks, B_vs=b_vs, B_ksT=b_ksT, B_s2=b_s2, B_p2=b_p2, B_pv2=b_pv2,
                    B_max3=b_max3, B_m3=lambda _: turn_tokens("B_m3", negs_b, "sq_used", done("sq_used", "B_max3", NG - 1)),
                    B_t1=b_t1, B_pv1=lambda g: pv("B_pv1", g, USES["1"]), B_t3=b_t3, B_pv3=b_pv3,
                    B_oT=b_oT, B_out=b_out,
                    F1_xT=lambda _: turn_tokens("F1_xT", xn_f, "xn", done("xn", "F1_norm")),
                    F1_h=lambda c: hidden(1, c), F1_out=lambda _: ffn_out(1),
                )
                for name, n in walk.order:
                    if name in part_of:
                        part_of[name](n)

            for i in walk.first():
                turn(i)
            with pe.Fori(2, NSEQ) as i:
                turn(i)
            for i in walk.last():
                turn(i)

        @block.scalar
        def _(act):
            for n, (name, integer, dst, k) in enumerate(TURNED):
                act.wait_ge(s["w_turned"], n + 1)
                act.activation(dst[:, :], emptied_banks["act"][0][:, 0:k * P], ACT.Copy).then_inc(s["w_copied"], 1)
                if n < len(ONES_IN_KEYS):
                    keys, rows, use = ONES_IN_KEYS[n]
                    act.activation(keys[rows, :, :], heads_of_rows[rows, use, :].unsqueeze(2)
                                   .broadcast_to((2 * H, H, T)), ACT.Copy)

            act.activation(idle[:, 0:1], ident[:, 0:1], ACT.Copy).then_inc(s["act_used"], AHEAD["act_used"])

            def turn(i):
                def empty(name, n, dst, src):
                    act.wait_ge(*at(i, *was_filled(name, n)))
                    act.activation(dst, src(bank_of(name, n)), ACT.Copy).then_inc(s["act_used"], 1)

                def tokens_out(name, dst):
                    empty(name, 0, dst[:, :], lambda b: b[:, 0:T])

                def heads_out(name, n, dst):
                    g, tb = n // 2, n % 2
                    empty(name, n, dst[0:DB, G * g:G * g + G, tb * P:(tb + 1) * P],
                          lambda b: b[0:DB, :].rearrange("p (j t) -> p j t", t=P))

                def shifts_out(name):
                    empty(name, 0, qT[SB:P, :, :], lambda b: b[SB:P, 0:T].unsqueeze(1).broadcast_to((P - SB, H, T)))

                def values_out(name, n, dst):
                    empty(name, n, dst, lambda b: b[:, :].rearrange("p (h d) -> p h d", h=H))

                def exps(g, use):
                    first = begun("sk_full", (use["t"], g))
                    for t in range(3):
                        act.wait_ge(*at(i, "sk_full", first + t + 1))
                        if t == 0 and first >= 6:
                            used = [step for step in walk.order if step[0] in PV][first // 3 - 2]
                            act.wait_ge(*at(i, *was_filled(*used)))
                        act.activation(probs[:, half_of_probs(use["t"], g), t, :], sk[(first + t) % 2][:, :], ACT.Exp,
                                       scale=use["scale"]).then_inc(s["probs"], 1)

                def hidden(f, c):
                    if c >= 2:
                        act.wait_ge(*at(i, *emptied(f"F{f}_h", c - 2)))
                    act.wait_ge(*at(i, *was_filled(f"F{f}_h", c)))
                    act.activation(th[:, c % 2, :], bank_of(f"F{f}_h", c)[:, 0:T], ACT.Tanh, scale=0.5)\
                        .then_inc(s["tanh"], 1)

                def a_turn(n):
                    tb, is_k, half = n // 4, n // 2 % 2, n % 2
                    empty("A_turn", n, (kTa if is_k else qTa)[0:KA, half * 8:half * 8 + 8, tb * P:(tb + 1) * P],
                          lambda b: b[0:KA, :].bitcast(BF16).rearrange("p (j t) -> p j t", t=P))

                def b_keep(_):
                    act.wait_ge(*at(i, *emptied_before("F0_out")))
                    act.activation(x2_old[:, :, :], x2[:, :, :], ACT.Copy).then_inc(s["kept"], 1)

                def b_soft(_):
                    act.wait_ge(*at(i, *emptied("B_gate")))
                    act.activation(zexp[:, :], z[:, :], ACT.Exp).then_inc(s["z_exp"], 1)

                def b_s2(tb):
                    act.wait_ge(*at(i, "sq_used", done("sq_used", "B_s2", tb)))
                    act.activation(part[:, 1, tb, :, :], part[:, 1, tb, :, :], ACT.Exp, scale=DB ** -0.5)\
                        .then_inc(s["p2"], 1)

                def b_kn(n):
                    act.wait_ge(*at(i, *was_filled("B_kn", n)))
                    for j in range(G):
                        ins = act.activation(k1T[ROPE:DB, 2 * G * n + j:2 * G * (n + 1):G, :],
                                             bank_of("B_kn", n)[NOPE * j:NOPE * (j + 1), :]
                                             .rearrange("p (g t) -> p g t", t=T), ACT.Copy)
                    ins.then_inc(s["act_used"], 1)

                def b_krT(_):
                    empty("B_krT", 0, k1T[0:ROPE, :, :], lambda b: b[0:ROPE, 0:T].unsqueeze(1).broadcast_to((ROPE, H, T)))

                def four_out(name, tb, dst):
                    empty(name, tb, dst[:, :, tb * P:(tb + 1) * P], lambda b: b[:, :].rearrange("p (n t) -> p n t", t=P))

                part_of = dict(
                    A_xT=lambda _: tokens_out("A_xT", xnT), A_turn=a_turn, A_t=lambda g: exps(g, USES["A"]),
                    A_yT=lambda _: tokens_out("A_yT", yaT),
                    F0_xT=lambda _: tokens_out("F0_xT", xnT), F0_h=lambda c: hidden(0, c),
                    F1_xT=lambda _: tokens_out("F1_xT", xnT_f), F1_h=lambda c: hidden(1, c),
                    B_keep=b_keep, B_xT=lambda _: tokens_out("B_xT", xnT_b),
                    B_small=lambda _: empty("B_small", 0, small[:, :, :].rearrange("p n c -> p (n c)"),
                                            lambda b: b[:, 0:TB * SMALL]),
                    B_imp=lambda _: tokens_out("B_imp", imp), B_soft=b_soft, B_nT=lambda _: tokens_out("B_nT", nT),
                    B_kn=b_kn, B_krT=b_krT, B_v=lambda tb: values_out("B_v", tb, v1[:, tb, :, 0:VD]),
                    B_qT=lambda n: heads_out("B_qT", n, qT),
                    B_vw=lambda tb: values_out("B_vw", tb, vw[:, tb, :, 0:VD]),
                    B_wT=lambda n: heads_out("B_wT", n, kwT),
                    B_sel=lambda _: empty("B_sel", 0, xselT[:, :], lambda b: b[:, 0:KEEP]),
                    B_ksT=lambda _: empty("B_ksT", 0, ksT[:, :, :].rearrange("p h t -> p (h t)"), lambda b: b[0:DB, :]),
                    B_m1=lambda _: shifts_out("B_m1"), B_m3=lambda _: shifts_out("B_m3"),
                    B_s2=b_s2, B_p2=lambda tb: four_out("B_p2", tb, p2T),
                    B_t1=lambda g: exps(g, USES["1"]), B_t3=lambda g: exps(g, USES["3"]),
                    B_oT=lambda tb: four_out("B_oT", tb, oT),
                )
                for name, n in walk.order:
                    if name in part_of:
                        part_of[name](n)

            for i in walk.first():
                turn(i)
            with act.Fori(2, NSEQ) as i:
                turn(i)
            for i in walk.last():
                turn(i)

        @block.vector
        def _(dve):
            for n, (name, integer, _, k) in enumerate(TURNED):
                if integer:
                    dve.wait_ge(s["c_loaded"], 16 * (len(LOADED) + n + 1))
                    dve.tensor_scalar(w_raw[:, :, :], w_int[:, :, :], FFN_SCALE, None, ALU.mult)\
                        .then_inc(s["set_dve"], 1)
            dve.tensor_copy(ident_h[:, :], ident[:, :])
            dve.tensor_copy(mask_q[:, :], staged[:, 0:P])
            dve.tensor_copy(mask_k[:, :], staged[:, P:2 * P])
            dve.tensor_scalar(wq[:, :, :], wq[:, :, :], gcol[0:QL, 0:1], None, ALU.mult)
            dve.tensor_scalar(wkv[QL:P, :, :, :], wkv[QL:P, :, :, :], gcol[QL:P, 0:1], None, ALU.mult)
            dve.tensor_scalar(wsmall[:, KR:GT], wsmall[:, KR:GT], 1.0 / H, None, ALU.mult)
            dve.wait_ge(s["set_pool"], 1)
            for j in range(G):
                dve.memset(vsel[KEEP * j:KEEP * (j + 1), :, j, VD:VD + 1], 1.0)
            for v in (va, v1, vw):
                d = v.shape[3] - 1
                dve.memset(v[:, :, :, d:d + 1], 1.0)
            dve.memset(ones[:, :], 1.0)
            dve.memset(mean_of[:, :], 1.0 / T)
            dve.memset(wimp_all[:, :], 1.0).then_inc(s["dve_step"], 1)
            dve.wait_ge(s["dve_step"], 1)
            for data in (x3, negs_a, negs_b):
                dve.memset(data[:, :, :], 0.0)
            dve.memset(qTa[KA - 16:SA, :, :], 0.0)
            dve.memset(kTa[KA - 16:SA, :, :], 0.0)
            dve.memset(spare[:, 0:1], 0.0).then_inc(s["stored"], 2 * AHEAD["stored"])
            dve.memset(spare[:, 2:3], 0.0).then_inc(s["dve_used"], AHEAD["dve_used"])
            dve.wait_ge(s["dve_used"], AHEAD["dve_used"])
            dve.tensor_scalar(wimp_all[:, :], wimp_all[:, :], wimp[:, 0:1], None, ALU.mult).then_inc(s["set_dve"], 1)

            def turn(i):
                chain = [0]

                def then(ins):
                    chain[0] += 1
                    ins.then_inc(s["dve_step"], 1)
                    dve.wait_ge(s["dve_step"], i * PER_TURN["dve_step"] + chain[0] + 1 - walk.short["dve_step"])

                def full_bank(name, n=0):
                    dve.wait_ge(*at(i, *was_filled(name, n)))
                    return bank_of(name, n)

                def empties(ins):
                    ins.then_inc(s["dve_used"], 1)

                def written(name, n=0):
                    dve.wait_ge(*at(i, *emptied(name, n)))

                def norm(name, x, dst):
                    for tb in range(TB):
                        ins = dve.bn_stats(stats[:, tb, :], x[:, tb, :])
                    then(ins)
                    dve.memset(spare[:, 1:2], 0.0)
                    for tb in range(TB):
                        ins = dve.bn_aggr(mv[:, tb, :], stats[:, tb, :])
                    then(ins)
                    dve.tensor_scalar(var[:, 0:TB], mv[:, :, 1], LN_EPS, None, ALU.add).then_inc(s["var"], 1)
                    dve.wait_ge(*at(i, "rstd", done("rstd", name)))
                    for tb in range(TB):
                        ins = dve.tensor_scalar(dst[:, tb, :], x[:, tb, :], mv[:, tb, 0:1], rstd[:, tb:tb + 1],
                                                ALU.subtract, ALU.mult)
                    ins.then_inc(s["xn"], 1)

                def maxima(name, g, dst, first):
                    for t in range(3):
                        n = begun("sq_full", (name, g)) + t
                        dve.wait_ge(*at(i, "sq_full", n + 1))
                        hs, w = bank_heads(g, t)
                        dve.tensor_reduce(dst[:, int(t > 0), first + hs[0]:first + hs[-1] + 1],
                                          sq[n % 2][:, :].rearrange("p (j w) -> p j w", w=w), AX_X, ALU.max,
                                          negate=True).then_inc(s["sq_used"], 1)

                def a_m(_):
                    negs = negs_a[:, :, SA:SA + H]
                    dve.wait_ge(*at(i, "sq_used", done("sq_used", "A_max", NG - 1)))
                    then(dve.tensor_copy(negs_high[:, :, :], negs))
                    dve.tensor_tensor(negs_a[:, :, SA + H:SA + 2 * H], negs, negs_high[:, :, :], ALU.subtract)\
                        .then_inc(s["low_left"], 1)
                    b = full_bank("A_m")
                    rows = slice(SA, SA + 2 * H)
                    empties(dve.tensor_copy(shift_a[rows, :], b[rows, 0:T]))
                    written("A_m")
                    dve.tensor_copy(qTa[rows, :, :], shift_a[rows, :].unsqueeze(1).broadcast_to((2 * H, H, T)))\
                        .then_inc(s["shift_set"], 1)

                def scale_out(name, g, d, dst, by_gate):
                    rd = rden[:, walk.among((name, g), (*PV, "B_pv2")) % 2, :, :]
                    o = full_bank(name, g)[:, 0:TB * G * (d + 1)].rearrange("p (n j d) -> p n j d", n=TB, j=G)
                    then(dve.reciprocal(rd, o[:, :, :, d]))
                    if by_gate is not None:
                        then(dve.tensor_scalar(rd, rd, by_gate, None, ALU.mult))
                    dve.tensor_tensor(dst, o[:, :, :, 0:d], rd.unsqueeze(3).broadcast_to((P, TB, G, d)),
                                      ALU.mult).then_inc(s["dve_used"], 1)

                def branch_out(name, g, a_part):
                    scale_out(name, g, VD, part[:, a_part, :, G * g:G * g + G, :], gate[:, a_part:a_part + 1])

                def rope(name, n, dst, tb, rows):
                    b = full_bank(name, n)
                    v = b[0:rows, 0:G * DB].rearrange("p (j d) -> p j d", j=G)
                    r = begun("roped", (name, n))
                    if r >= 2:
                        dve.wait_ge(*at(i, "roped", r - 1))
                    dve.tensor_tensor(dst, v, cosx[0:rows, tb, :].unsqueeze(1).broadcast_to((rows, G, DB)), ALU.mult)
                    halves_swapped = v[:, :, 0:ROPE].rearrange("p j (e d) -> p j e d", e=2)[:, :, ::-1, :]
                    sines = sinx[0:rows, tb, :].rearrange("p (e d) -> p e d", e=2).unsqueeze(1)
                    empties(dve.tensor_tensor(
                        swapped[0:rows, r % 2, :, :].rearrange("p j (e d) -> p j e d", e=2), halves_swapped,
                        sines.broadcast_to((rows, G, 2, ROPE // 2)), ALU.mult))

                def rope_ring(name, n):
                    before_it = RING_STEPS.index((name, n)) - RING
                    if before_it >= 0:
                        source, m = RING_STEPS[before_it]
                        dve.wait_ge(*at(i, *was_filled(source + "T", m)))
                    rope(name, n, full[:, ring_of(name, n), :, :], n % 2, P)

                def hidden(f, c):
                    b = full_bank(f"F{f}_h", c)
                    dve.wait_ge(*at(i, "tanh", done("tanh", f"F{f}_h", c)))
                    then(dve.scalar_tensor_tensor(out=hmid[:, c % 2, :], in0=th[:, c % 2, :], scalar=1.0,
                                                  in1=b[:, 0:T], op0=ALU.add, op1=ALU.mult))
                    empties(dve.scalar_tensor_tensor(out=hT[:, c, :], in0=hmid[:, c % 2, :], scalar=0.5,
                                                     in1=b[:, T:2 * T], op0=ALU.mult, op1=ALU.mult))

                def add_out(name, x, dst):
                    b = full_bank(name)
                    empties(dve.tensor_tensor(dst[:, :, :], b[:, 0:T].rearrange("p (n c) -> p n c", c=C), x[:, :, :],
                                              ALU.add))
                    written(name)

                def a_norm(_):
                    dve.wait_ge(*at(i, "x_loaded", 16))
                    norm("A_norm", x0, xn)

                def a_qkv(tb):
                    b = full_bank("A_qkv", tb)
                    dve.tensor_tensor(va[:, tb, :, 0:DA], b[:, 2 * C:3 * C].rearrange("p (h d) -> p h d", h=H),
                                      bqkv[:, 2 * C:3 * C].rearrange("p (h d) -> p h d", h=H), ALU.add)
                    empties(dve.tensor_tensor(qk[:, tb, :], b[:, 0:2 * C], bqkv[:, 0:2 * C], ALU.add))

                def a_split(tb):
                    q = qk[:, tb, 0:C].rearrange("p (h d) -> p h d", h=H)
                    r = rest_q[:, :].rearrange("p (h d) -> p h d", h=H)
                    written("A_qkv", tb)
                    then(dve.tensor_copy(qstack[:, tb, :, 0:3, :], q.unsqueeze(2).broadcast_to((P, H, 3, DA))))
                    then(dve.tensor_tensor(r, q, qstack[:, tb, :, 0, :], ALU.subtract))
                    then(dve.tensor_copy(qstack[:, tb, :, 3:5, :], r.unsqueeze(2).broadcast_to((P, H, 2, DA))))
                    dve.tensor_tensor(qstack[:, tb, :, 5, :], r, qstack[:, tb, :, 3, :], ALU.subtract)\
                        .then_inc(s["q_split"], 1)
                    dve.wait_ge(*at(i, "q_split", tb + 1))

                def a_out(_):
                    add_out("A_out", x0, x1)
                    dve.tensor_tensor(x1[:, :, :], x1[:, :, :], bout[:, :].unsqueeze(1).broadcast_to((P, TB, C)), ALU.add)\
                        .then_inc(s["x_used"], 1)

                def f0_norm(_):
                    dve.wait_ge(*at(i, "x_used", 1))
                    norm("F0_norm", x1, xn)

                def f0_out(_):
                    if ("B_keep", 0) in walk.order:
                        dve.wait_ge(*at(i, "kept", 1))
                    add_out("F0_out", x1, x2)

                def f1_norm(_):
                    dve.wait_ge(*at(i, *emptied_before("B_out")))
                    norm("F1_norm", x3, xn_f)

                def f1_out(_):
                    dve.wait_ge(*at(i, "stored", 0))
                    add_out("F1_out", x3, y)

                def b_gate(_):
                    b = full_bank("B_gate")
                    then(dve.tensor_reduce(zmax[:, :], b[:, 0:3], AX_X, ALU.max))
                    empties(dve.tensor_scalar(z[:, :], b[:, 0:3], zmax[:, 0:1], None, ALU.subtract))

                def b_rms(_):
                    dve.wait_ge(*at(i, *emptied("B_small")))
                    for j, (c0, c1) in enumerate(((0, QL), (QL, KR))):
                        for tb in range(TB):
                            then(dve.tensor_tensor_reduce(work[:, 0:c1 - c0], small[:, tb, c0:c1], small[:, tb, c0:c1],
                                                          1.0, 0.0, ALU.mult, ALU.add,
                                                          square_sum[:, TB * j + tb:TB * j + tb + 1]))
                    dve.tensor_scalar(var[:, 0:2], square_sum[:, 0:2], 1.0 / QL, RMS_EPS, ALU.mult, ALU.add)
                    dve.tensor_scalar(var[:, 2:4], square_sum[:, 2:4], 1.0 / KVL, RMS_EPS, ALU.mult, ALU.add)\
                        .then_inc(s["var"], 1)
                    dve.wait_ge(*at(i, "rstd", done("rstd", "B_rms")))
                    for tb in range(TB):
                        dve.tensor_scalar(nrm[:, tb, 0:QL], small[:, tb, 0:QL], rstd[:, tb:tb + 1], None, ALU.mult)
                        ins = dve.tensor_scalar(nrm[:, tb, QL:P], small[:, tb, QL:KR], rstd[:, 2 + tb:3 + tb], None,
                                                ALU.mult)
                    ins.then_inc(s["nrm"], 1)

                def b_soft(_):
                    dve.wait_ge(*at(i, "z_exp", 1))
                    then(dve.tensor_reduce(zmax[:, :], zexp[:, :], AX_X, ALU.add))
                    then(dve.reciprocal(zmax[:, :], zmax[:, :]))
                    then(dve.tensor_scalar(gate[:, :], zexp[:, :], zmax[:, 0:1], None, ALU.mult))

                def b_krope(_):
                    dve.wait_ge(*at(i, *emptied_before("B_small")))
                    k = small[:, :, KR:GT]
                    dve.tensor_tensor(kr[:, :, :], k, cosx[:, :, 0:ROPE], ALU.mult)
                    then(dve.tensor_tensor(kr_swapped[:, :, :].rearrange("p n (e d) -> p n e d", e=2),
                                           k.rearrange("p n (e d) -> p n e d", e=2)[:, :, ::-1, :],
                                           sinx[:, :, :].rearrange("p n (e d) -> p n e d", e=2), ALU.mult))
                    dve.tensor_tensor(kr[:, :, :], kr[:, :, :], kr_swapped[:, :, :], ALU.add).then_inc(s["krope"], 1)

                def b_rank(_):
                    dve.wait_ge(*at(i, *emptied_before("B_imp")))
                    for tb in range(TB):
                        then(dve.tensor_tensor_reduce(work[:, 0:P], imp[:, tb * P:(tb + 1) * P], ident[:, :], 1.0, 0.0,
                                                      ALU.mult, ALU.add, icol[:, tb:tb + 1]))
                        then(dve.scalar_tensor_tensor(out=work[:, :], in0=imp[:, :], scalar=icol[:, tb:tb + 1],
                                                      in1=before[:, tb, :], op0=ALU.is_equal, op1=ALU.mult))
                        then(dve.scalar_tensor_tensor(out=work[:, :], in0=imp[:, :], scalar=icol[:, tb:tb + 1],
                                                      in1=work[:, :], op0=ALU.is_gt, op1=ALU.add))
                        then(dve.tensor_reduce(rank[:, tb:tb + 1], work[:, :], AX_X, ALU.add))
                    dve.tensor_scalar(keep[:, :], rank[:, :], float(KEEP), None, ALU.is_lt).then_inc(s["picked"], 1)

                def b_pos(_):
                    b = full_bank("B_pos")
                    empties(dve.tensor_copy(pos[:, :], b[:, 0:TB]))
                    written("B_pos")
                    for tb in range(TB):
                        ins = dve.tensor_scalar(onehot[:, tb, :], slots[:, :], pos[:, tb:tb + 1], keep[:, tb:tb + 1],
                                                ALU.is_equal, ALU.mult)
                    ins.then_inc(s["onehot"], 1)

                def b_vs(_):
                    b = full_bank("B_vs")
                    for j in range(G):
                        rows = slice(KEEP * j, KEEP * (j + 1))
                        ins = dve.tensor_copy(vsel[rows, :, j, 0:VD], b[rows, 0:NG * VD].rearrange("p (g d) -> p g d", g=NG))
                    empties(ins)

                def b_s2(tb):
                    n = begun("sq_full", ("B_s2", tb))
                    dve.wait_ge(*at(i, "sq_full", n + 1))
                    b = sq[n % 2][:, :].rearrange("p (h w) -> p h w", w=KEEP)
                    then(dve.tensor_reduce(negm_sel[:, tb, :], b, AX_X, ALU.max, negate=True))
                    dve.tensor_tensor(part[:, 1, tb, :, :], b, negm_sel[:, tb, :].unsqueeze(2).broadcast_to((P, H, KEEP)),
                                      ALU.add).then_inc(s["sq_used"], 1)

                part_of = dict(
                    A_norm=a_norm, A_qkv=a_qkv, A_split=a_split, A_max=lambda g: maxima("A_max", g, negs_a, SA),
                    A_m=a_m,
                    A_pv=lambda g: scale_out("A_pv", g, DA, ya[:, :, G * DA * g:G * DA * (g + 1)]
                                             .rearrange("p n (j d) -> p n j d", j=G), None),
                    A_out=a_out, F0_norm=f0_norm, F0_h=lambda c: hidden(0, c), F0_out=f0_out,
                    B_norm=lambda _: norm("B_norm", x2, xn_b), B_gate=b_gate, B_soft=b_soft, B_rms=b_rms, B_krope=b_krope,
                    B_q=lambda n: rope_ring("B_q", n), B_w=lambda n: rope_ring("B_w", n),
                    B_max1=lambda g: maxima("B_max1", g, negs_b, SB),
                    B_rank=b_rank, B_pos=b_pos, B_ks=lambda g: rope("B_ks", g, ksfull[:, G * g:G * g + G, :], 0, KEEP),
                    B_vs=b_vs, B_s2=b_s2, B_max3=lambda g: maxima("B_max3", g, negs_b, SB + H),
                    B_pv1=lambda g: branch_out("B_pv1", g, 0), B_pv2=lambda g: branch_out("B_pv2", g, 1),
                    B_pv3=lambda g: branch_out("B_pv3", g, 2),
                    B_out=lambda _: add_out("B_out", x2_old, x3),
                    F1_norm=f1_norm, F1_h=lambda c: hidden(1, c), F1_out=f1_out,
                )
                for name, n in walk.order:
                    if name in part_of:
                        part_of[name](n)
                walk.chain["dve_step"] = chain[0]

            for i in walk.first():
                turn(i)
            with dve.Fori(2, NSEQ) as i:
                turn(i)
            assert walk.chain["dve_step"] == PER_TURN["dve_step"], walk.chain
            for i in walk.last():
                turn(i)

        @block.gpsimd
        def _(pool):
            pool.memset(idle_p[:, :], 0.0)
            pool.memset(vsel[:, :, :, :], 0.0).then_inc(s["pool_step"], 1)
            pool.memset(minus_half[:, :], -0.5).then_inc(s["set_pool"], 1)
            pool.wait_ge(s["set_pool"], 1)

            def turn(i):
                chain = [0]

                def then(ins):
                    chain[0] += 1
                    ins.then_inc(s["pool_step"], 1)
                    pool.wait_ge(s["pool_step"], i * PER_TURN["pool_step"] + chain[0] + 1 - walk.short["pool_step"])

                def carry_waits(column=2):
                    pool.tensor_tensor(idle_p[:, column:column + 1], idle_p[:, 0:1], idle_p[:, 1:2], ALU.add)

                def rsqrt(name, n):
                    pool.wait_ge(*at(i, "var", done("var", name)))
                    pool.tensor_tensor(rstd[:, 0:n], var[:, 0:n], minus_half[:, 0:n], ALU.pow).then_inc(s["rstd"], 1)

                def a_split(tb):
                    k = qk[:, tb, C:2 * C].rearrange("p (h d) -> p h d", h=H)
                    r = rest_k[:, :].rearrange("p (h d) -> p h d", h=H)
                    pool.wait_ge(*at(i, *emptied("A_qkv", tb)))
                    carry_waits()
                    pool.tensor_copy(kstack[:, tb, :, 3, :], k)
                    pool.tensor_copy(kstack[:, tb, :, 5, :], k)
                    then(pool.tensor_copy(kstack[:, tb, :, 0, :], k))
                    then(pool.tensor_tensor(r, k, kstack[:, tb, :, 0, :], ALU.subtract))
                    carry_waits()
                    pool.tensor_copy(kstack[:, tb, :, 4, :], r)
                    then(pool.tensor_copy(kstack[:, tb, :, 1, :], r))
                    pool.tensor_tensor(kstack[:, tb, :, 2, :], r, kstack[:, tb, :, 1, :], ALU.subtract)\
                        .then_inc(s["k_split"], 1)
                    pool.wait_ge(*at(i, "k_split", tb + 1))

                def add_swapped(name, n, dst, rows):
                    pool.wait_ge(*at(i, *emptied(name, n)))
                    pool.tensor_tensor(dst, dst, swapped[0:rows, begun("roped", (name, n)) % 2, :, :], ALU.add)\
                        .then_inc(s["roped"], 1)

                def add_branch(name, g, a_part):
                    pool.wait_ge(*at(i, *emptied(name, g)))
                    if begun("summed", (name, g)):
                        pool.wait_ge(*at(i, "summed", begun("summed", (name, g))))
                    first, other = (part[:, k, :, G * g:G * g + G, :] for k in (0, a_part))
                    pool.tensor_tensor(first, first, other, ALU.add).then_inc(s["summed"], 1)

                part_of = dict(
                    A_norm=lambda _: rsqrt("A_norm", TB), F0_norm=lambda _: rsqrt("F0_norm", TB),
                    B_norm=lambda _: rsqrt("B_norm", TB), F1_norm=lambda _: rsqrt("F1_norm", TB),
                    B_rms=lambda _: rsqrt("B_rms", 2 * TB), A_split=a_split,
                    B_q=lambda n: add_swapped("B_q", n, full[:, ring_of("B_q", n), :, 0:ROPE], P),
                    B_w=lambda n: add_swapped("B_w", n, full[:, ring_of("B_w", n), :, 0:ROPE], P),
                    B_ks=lambda g: add_swapped("B_ks", g, ksfull[:, G * g:G * g + G, 0:ROPE], KEEP),
                    B_pv2=lambda g: add_branch("B_pv2", g, 1), B_pv3=lambda g: add_branch("B_pv3", g, 2),
                )
                for name, n in walk.order:
                    if name in part_of:
                        part_of[name](n)
                walk.chain["pool_step"] = chain[0]

            for i in walk.first():
                turn(i)
            with pool.Fori(2, NSEQ) as i:
                turn(i)
            assert walk.chain["pool_step"] == PER_TURN["pool_step"], walk.chain
            for i in walk.last():
                turn(i)


def constants():
    i, j = np.arange(P)[:, None], np.arange(P)[None, :]
    heads_of_rows = np.zeros((P, 2, H), np.float32)
    for h in range(H):
        heads_of_rows[[SA + h, SA + H + h, SB + h], 0, h] = 1
        heads_of_rows[SB + H + h, 1, h] = 1
    token = np.arange(TB)[None, :, None] * P + np.arange(P)[:, None, None]
    freq = (1.0 / np.float32(10000.0) ** (np.arange(0, ROPE, 2, dtype=np.float32) / np.float32(ROPE))).astype(np.float32)
    angle = token.astype(np.float32) * freq
    cos, sin = np.cos(angle).astype(np.float32), np.sin(angle).astype(np.float32)
    return {
        "c_ident": np.eye(P, dtype=np.float32),
        "c_masks": np.concatenate([np.where(j > i, BIG, 0), np.where(i > j, BIG, 0)], axis=1).astype(np.float32),
        "c_heads": heads_of_rows.reshape(P, -1),
        "c_before": (np.arange(T)[None, None, :] < token).astype(np.float32),
        "c_before_k": (i < j).astype(np.float32),
        "c_slots": np.tile(np.arange(KEEP, dtype=np.float32), (P, 1)),
        "c_cos": np.concatenate([cos, cos, np.ones((P, TB, NOPE), np.float32)], axis=2),
        "c_sin": np.concatenate([-sin, sin], axis=2),
    }


INPUTS = ["L0_attn_a_x", "L0_attn_a_W_attn", "L0_attn_a_b_attn", "L0_attn_a_W_proj", "L0_attn_a_b_proj",
          "L0_attn_b_w_cq", "L0_attn_b_g_qnorm", "L0_attn_b_w_dq_nope", "L0_attn_b_w_dq_rope", "L0_attn_b_w_ckv",
          "L0_attn_b_g_kvnorm", "L0_attn_b_w_dk_nope", "L0_attn_b_w_dv", "L0_attn_b_w_krope", "L0_attn_b_w_imp",
          "L0_attn_b_w_selk", "L0_attn_b_w_selv", "L0_attn_b_w_wink", "L0_attn_b_w_winv", "L0_attn_b_w_gate",
          "L0_attn_b_w_proj", "L0_ffn_w_gate", "L0_ffn_w_up", "L0_ffn_w_down"]


def kernel(**inputs):
    import concourse.bacc as bacc
    from concourse.bass_utils import run_bass_kernel_spmd

    nc = bacc.Bacc("TRN2", target_bir_lowering=False, num_devices=1)
    arrays = {name: np.ascontiguousarray(inputs[name]) for name in INPUTS}
    arrays.update(constants())
    args = {name: nc.dram_tensor(name, v.shape, mybir.dt.from_np(v.dtype), kind="ExternalInput").ap()
            for name, v in arrays.items()}
    out = nc.dram_tensor("out", (NSEQ, T, C), F32, kind="ExternalOutput").ap()
    build(nc, args, out)
    r = run_bass_kernel_spmd(nc, [arrays], core_ids=[0])
    return r.results[0]["out"]
```
